# Optimizing a Trainium2 kernel written in Bass

```python
import numpy as np
import jax
import jax.numpy as jnp

def _softmax(x, axis=-1):
    return jax.nn.softmax(x, axis=axis)

def _gelu(x):
    return jax.nn.gelu(x, approximate=True)

def _silu(x):
    return jax.nn.silu(x)

def _sigmoid(x):
    return jax.nn.sigmoid(x)

def _layernorm(x, axis=-1, eps=1e-05):
    m = jnp.mean(x, axis=axis, keepdims=True)
    v = jnp.var(x, axis=axis, keepdims=True)
    return (x - m) / jnp.sqrt(v + eps)

def _scatter_add(tgt, idx, src, axis=0):
    return tgt.at[idx].add(src)

def _segment_sum(src, seg, n):
    return jax.ops.segment_sum(src, seg, n)
kernel_name = 'mk_lm_tower_d1_tok_ids768_r4_fb9ed2'

def setup_inputs(seed: int=0):
    np.random.seed(seed)
    _w = jnp.asarray

    def _rec_inputs():
        import jax
        import jax.numpy as jnp
        _rk = jax.random.key(seed)
        x = jax.random.randint(jax.random.fold_in(_rk, 1), (32, 128), 0, 30521, jnp.int32)
        mask_BS_i1_0 = jnp.where(jnp.ones((32, 128), dtype=bool), 1, 0).astype(jnp.int32)
        fside_BSS_graph = jax.random.uniform(jax.random.fold_in(_rk, 22), (32, 128, 128), jnp.float32, 0.0, 0.00443395)
        return (x, mask_BS_i1_0, fside_BSS_graph)
    x, mask_BS_i1_0, fside_BSS_graph = _rec_inputs()

    def _L0_tok_setup():
        import jax, jax.numpy as jnp
        import numpy as np
        VOCAB = 30522
        N_SEG = 2
        MAX_POS = 128
        D = 192
        LN_EPS = 1e-12
        key = jax.random.key(seed)
        ks = jax.random.split(key, 10)
        B, S = (16, 128)
        input_ids = jax.random.randint(ks[0], (B, S), 0, VOCAB, dtype=jnp.int32)
        segment_ids = jax.random.randint(ks[1], (B, S), 0, N_SEG, dtype=jnp.int32)
        g = jax.random.uniform(ks[2], (B, S, S), dtype=jnp.float32)
        graph = g / jnp.sum(g, axis=-1, keepdims=True)
        tok_emb = jax.random.normal(ks[3], (VOCAB, D), dtype=jnp.float32) * 0.02
        seg_emb = jax.random.normal(ks[4], (N_SEG, D), dtype=jnp.float32) * 0.02
        pos_emb = jax.random.normal(ks[5], (MAX_POS, D), dtype=jnp.float32) * 0.02
        dense_w = jax.random.normal(ks[6], (D, D), dtype=jnp.float32) * 0.02
        dense_b = jnp.zeros((D,), dtype=jnp.float32)
        ln_gamma = jnp.ones((D,), dtype=jnp.float32)
        ln_beta = jnp.zeros((D,), dtype=jnp.float32)
        return {'input_ids': input_ids, 'segment_ids': segment_ids, 'graph': graph, 'tok_emb': tok_emb, 'seg_emb': seg_emb, 'pos_emb': pos_emb, 'dense_w': dense_w, 'dense_b': dense_b, 'ln_gamma': ln_gamma, 'ln_beta': ln_beta}
    _L0_tok_all = _L0_tok_setup()
    _L0_tok_in = {k: v for k, v in _L0_tok_all.items() if k in ('tok_emb', 'seg_emb', 'pos_emb', 'dense_w', 'dense_b', 'ln_gamma', 'ln_beta')}
    del _L0_tok_all

    def _L0_attn_setup():
        import jax, jax.numpy as jnp
        import numpy as np
        from jax import lax
        EMBED_DIM = 192
        N_HEAD = 12
        Q_DIM = 64
        V_DIM = 64
        WINDOW_SIZE = 64

        def _forward(x, Wq, bq, Wk, bk, Wv, bv, Wo, bo):
            B, N, E = x.shape
            half = WINDOW_SIZE // 2
            n_diag = WINDOW_SIZE + 1
            Q = jnp.swapaxes((x @ Wq + bq).reshape(B, N, N_HEAD, Q_DIM), 1, 2)
            K = jnp.swapaxes((x @ Wk + bk).reshape(B, N, N_HEAD, Q_DIM), 1, 2)
            V = jnp.swapaxes((x @ Wv + bv).reshape(B, N, N_HEAD, V_DIM), 1, 2)
            pos = jnp.arange(N)
            offsets = jnp.arange(-half, half + 1)

            def diag_dot(di):
                Ks = jnp.roll(K, -di, axis=2)
                d = jnp.einsum('bhnd,bhnd->bhn', Q, Ks)
                valid = (pos + di >= 0) & (pos + di < N)
                return jnp.where(valid[None, None, :], d, jnp.zeros((), d.dtype))
            band = lax.map(diag_dot, offsets)
            band = jnp.moveaxis(band, 0, -1)
            scores = jnp.pad(band, ((0, 0), (0, 0), (0, 0), (0, N - n_diag)))
            attn = jax.nn.softmax(scores, axis=-1)
            out = attn @ V
            out = jnp.swapaxes(out, 1, 2).reshape(B, N, N_HEAD * V_DIM)
            return out @ Wo + bo
        key = jax.random.key(seed)
        ks = jax.random.split(key, 9)
        B, N, E = (2, 512, EMBED_DIM)
        s = 0.02
        return {'x': jax.random.normal(ks[0], (B, N, E), dtype=jnp.float32), 'Wq': jax.random.normal(ks[1], (E, N_HEAD * Q_DIM), dtype=jnp.float32) * s, 'bq': jax.random.normal(ks[2], (N_HEAD * Q_DIM,), dtype=jnp.float32) * s, 'Wk': jax.random.normal(ks[3], (E, N_HEAD * Q_DIM), dtype=jnp.float32) * s, 'bk': jax.random.normal(ks[4], (N_HEAD * Q_DIM,), dtype=jnp.float32) * s, 'Wv': jax.random.normal(ks[5], (E, N_HEAD * V_DIM), dtype=jnp.float32) * s, 'bv': jax.random.normal(ks[6], (N_HEAD * V_DIM,), dtype=jnp.float32) * s, 'Wo': jax.random.normal(ks[7], (N_HEAD * V_DIM, E), dtype=jnp.float32) * s, 'bo': jax.random.normal(ks[8], (E,), dtype=jnp.float32) * s}
    _L0_attn_all = _L0_attn_setup()
    _L0_attn_in = {k: v for k, v in _L0_attn_all.items() if k in ('Wq', 'bq', 'Wk', 'bk', 'Wv', 'bv', 'Wo', 'bo')}
    del _L0_attn_all

    def _L0_ffn_setup():
        import jax, jax.numpy as jnp
        import numpy as np
        B, S, H, F, E, TOP_K = (4, 512, 192, 768, 8, 2)
        key = jax.random.key(seed)
        ks = jax.random.split(key, 6)
        x = jax.random.normal(ks[0], (B, S, H), dtype=jnp.float32)
        Wr = jax.random.normal(ks[1], (E, H), dtype=jnp.float32) * 0.02
        Wi = jax.random.normal(ks[2], (E, F, H), dtype=jnp.float32) * 0.02
        bi = jnp.zeros((E, F), dtype=jnp.float32)
        Wo = jax.random.normal(ks[3], (E, H, F), dtype=jnp.float32) * 0.02
        bo = jnp.zeros((E, H), dtype=jnp.float32)
        return {'x': x, 'Wr': Wr, 'Wi': Wi, 'bi': bi, 'Wo': Wo, 'bo': bo}
    _L0_ffn_all = _L0_ffn_setup()
    _L0_ffn_in = {k: v for k, v in _L0_ffn_all.items() if k in ('Wr', 'Wi', 'bi', 'Wo', 'bo')}
    del _L0_ffn_all
    return {'x': x, 'mask_BS_i1_0': mask_BS_i1_0, 'fside_BSS_graph': fside_BSS_graph, 'L0_tok_tok_emb': _L0_tok_in['tok_emb'], 'L0_tok_seg_emb': _L0_tok_in['seg_emb'], 'L0_tok_pos_emb': _L0_tok_in['pos_emb'], 'L0_tok_dense_w': _L0_tok_in['dense_w'], 'L0_tok_dense_b': _L0_tok_in['dense_b'], 'L0_tok_ln_gamma': _L0_tok_in['ln_gamma'], 'L0_tok_ln_beta': _L0_tok_in['ln_beta'], 'L0_attn_Wq': _L0_attn_in['Wq'], 'L0_attn_bq': _L0_attn_in['bq'], 'L0_attn_Wk': _L0_attn_in['Wk'], 'L0_attn_bk': _L0_attn_in['bk'], 'L0_attn_Wv': _L0_attn_in['Wv'], 'L0_attn_bv': _L0_attn_in['bv'], 'L0_attn_Wo': _L0_attn_in['Wo'], 'L0_attn_bo': _L0_attn_in['bo'], 'L0_ffn_Wr': _L0_ffn_in['Wr'], 'L0_ffn_Wi': _L0_ffn_in['Wi'], 'L0_ffn_bi': _L0_ffn_in['bi'], 'L0_ffn_Wo': _L0_ffn_in['Wo'], 'L0_ffn_bo': _L0_ffn_in['bo']}

def reference(x, mask_BS_i1_0, fside_BSS_graph, L0_tok_tok_emb, L0_tok_seg_emb, L0_tok_pos_emb, L0_tok_dense_w, L0_tok_dense_b, L0_tok_ln_gamma, L0_tok_ln_beta, L0_attn_Wq, L0_attn_bq, L0_attn_Wk, L0_attn_bk, L0_attn_Wv, L0_attn_bv, L0_attn_Wo, L0_attn_bo, L0_ffn_Wr, L0_ffn_Wi, L0_ffn_bi, L0_ffn_Wo, L0_ffn_bo):
    import jax
    import jax.numpy as jnp

    def _L0_tok_ref(input_ids, segment_ids, graph, tok_emb, seg_emb, pos_emb, dense_w, dense_b, ln_gamma, ln_beta):
        import jax, jax.numpy as jnp
        import numpy as np
        VOCAB = 30522
        N_SEG = 2
        MAX_POS = 128
        D = 192
        LN_EPS = 1e-12
        B, S = input_ids.shape
        emb = tok_emb[input_ids] + seg_emb[segment_ids] + pos_emb[None, :S, :]
        agg = jnp.einsum('bst,btd->bsd', graph, emb)
        proj = jnp.einsum('bsd,de->bse', agg, dense_w) + dense_b
        h = emb + proj
        mu = jnp.mean(h, axis=-1, keepdims=True)
        var = jnp.mean(jnp.square(h - mu), axis=-1, keepdims=True)
        out = (h - mu) * jax.lax.rsqrt(var + LN_EPS) * ln_gamma + ln_beta
        return out

    def _L0_attn_ref(x, Wq, bq, Wk, bk, Wv, bv, Wo, bo):
        import jax, jax.numpy as jnp
        import numpy as np
        from jax import lax
        EMBED_DIM = 192
        N_HEAD = 12
        Q_DIM = 64
        V_DIM = 64
        WINDOW_SIZE = 64

        def _forward(x, Wq, bq, Wk, bk, Wv, bv, Wo, bo):
            B, N, E = x.shape
            half = WINDOW_SIZE // 2
            n_diag = WINDOW_SIZE + 1
            Q = jnp.swapaxes((x @ Wq + bq).reshape(B, N, N_HEAD, Q_DIM), 1, 2)
            K = jnp.swapaxes((x @ Wk + bk).reshape(B, N, N_HEAD, Q_DIM), 1, 2)
            V = jnp.swapaxes((x @ Wv + bv).reshape(B, N, N_HEAD, V_DIM), 1, 2)
            pos = jnp.arange(N)
            offsets = jnp.arange(-half, half + 1)

            def diag_dot(di):
                Ks = jnp.roll(K, -di, axis=2)
                d = jnp.einsum('bhnd,bhnd->bhn', Q, Ks)
                valid = (pos + di >= 0) & (pos + di < N)
                return jnp.where(valid[None, None, :], d, jnp.zeros((), d.dtype))
            band = lax.map(diag_dot, offsets)
            band = jnp.moveaxis(band, 0, -1)
            scores = jnp.pad(band, ((0, 0), (0, 0), (0, 0), (0, N - n_diag)))
            attn = jax.nn.softmax(scores, axis=-1)
            out = attn @ V
            out = jnp.swapaxes(out, 1, 2).reshape(B, N, N_HEAD * V_DIM)
            return out @ Wo + bo
        return _forward(x, Wq, bq, Wk, bk, Wv, bv, Wo, bo)

    def _L0_ffn_ref(x, Wr, Wi, bi, Wo, bo):
        import jax, jax.numpy as jnp
        import numpy as np
        B, S, H, F, E, TOP_K = (4, 512, 192, 768, 8, 2)
        xf = x.reshape(-1, x.shape[-1])
        router_logits = jnp.einsum('th,eh->te', xf, Wr)
        topk_vals, topk_idx = jax.lax.top_k(router_logits, TOP_K)
        routing_weights = jax.nn.softmax(topk_vals, axis=-1)
        h = jnp.einsum('th,efh->etf', xf, Wi) + bi[:, None, :]
        h = jax.nn.gelu(h, approximate=False)
        expert_out = jnp.einsum('etf,ehf->eth', h, Wo) + bo[:, None, :]
        expert_out = jnp.transpose(expert_out, (1, 0, 2))
        gathered = jnp.take_along_axis(expert_out, topk_idx[:, :, None], axis=1)
        out = jnp.einsum('tk,tkh->th', routing_weights, gathered)
        return out.reshape(x.shape)
    h = _L0_tok_ref(x, mask_BS_i1_0, fside_BSS_graph, L0_tok_tok_emb, L0_tok_seg_emb, L0_tok_pos_emb, L0_tok_dense_w, L0_tok_dense_b, L0_tok_ln_gamma, L0_tok_ln_beta)
    h = h + _L0_attn_ref(_layernorm(h, axis=-1), L0_attn_Wq, L0_attn_bq, L0_attn_Wk, L0_attn_bk, L0_attn_Wv, L0_attn_bv, L0_attn_Wo, L0_attn_bo)
    h = h + _L0_ffn_ref(_layernorm(h, axis=-1), L0_ffn_Wr, L0_ffn_Wi, L0_ffn_bi, L0_ffn_Wo, L0_ffn_bo)
    return h

_drawn_inputs = setup_inputs


def setup_inputs(seed=0):
    import zlib

    import numpy as np

    out = dict(_drawn_inputs(seed))
    spreads = {'L0_tok_dense_b': (0.0, 0.1),
     'L0_tok_ln_gamma': (1.0, 0.2),
     'L0_tok_ln_beta': (0.0, 0.1),
     'L0_ffn_bi': (0.0, 0.388),
     'L0_ffn_bo': (0.0, 0.1)}
    factors = {'fside_BSS_graph': 8.0,
     'L0_tok_dense_w': 4.725,
     'L0_attn_Wq': 8.0,
     'L0_attn_bq': 64.0,
     'L0_attn_Wk': 8.0,
     'L0_attn_bk': 64.0,
     'L0_attn_bv': 5.326,
     'L0_attn_bo': 2.995}
    for name, (base, spread) in spreads.items():
        noise = np.random.default_rng([zlib.crc32(name.encode()), seed]).standard_normal(out[name].shape)
        drawn = base * np.exp(spread * noise) if base else spread * noise
        out[name] = jnp.asarray(drawn.astype(out[name].dtype))
    for name, factor in factors.items():
        out[name] = (out[name] * factor).astype(out[name].dtype)
    return out
```

```python
import concourse.bass as bass
from concourse import mybir
from contextlib import ExitStack

f32 = mybir.dt.float32
f32r = mybir.dt.float32r
bf16 = mybir.dt.bfloat16
i32 = mybir.dt.int32
u32 = mybir.dt.uint32
ALU = mybir.AluOpType
ACT = mybir.ActivationFunctionType
AX = mybir.AxisListType

P = 128
B, S, D = 32, 128, 192
DC = D // 2
NH, HD = 12, 64
A = NH * HD
HALF = 32
BAND = 2 * HALF + 1
G = 4
NG = B // G
SLOT = HALF + S
PITCH = NH * SLOT
HEAD_PAIRS = ((0, 4), (4, 6))
NE, F = 8, 768
FC = F // P
T = B * S
REGION = T + P
ROW = D + 2
NOWHERE = NE * REGION
TILES = (2 * T + NE * (P - 1)) // P
NO_TOKEN = 2 * T
CONSTANTS = 23
KC = 5


def wait_apart(eng, passed, sem, value):
    if not isinstance(value, int):
        value = eng.to_reg(value)
        eng.wait_ge(passed, 1)
    eng.wait_ge(sem, value)


def attention_block(nc, dram, route):
    x_ids, mask, graphT = dram["ids"], dram["mask"], dram["graphT"]
    out, shear, rows = dram["out"], dram["shear"], dram["rows"]
    ctx = ExitStack()
    with ctx:
        def sb(name, shape, dt=f32):
            return ctx.enter_context(nc.sbuf_tensor(name, shape, dt))

        def sem(name):
            return ctx.enter_context(nc.semaphore(name))

        w_split = {m: sb(f"w{m}_split", [P, KC, A], f32r) for m in "qkv"}
        w_o = sb("w_o", [P, A // P, D])
        w_dense = sb("w_dense", [DC, 2, D])
        w_router = sb("w_router", [DC, 2, NE])
        bias_row = {m: sb(f"bias_{m}", [P, A]) for m in "qkv"}
        bias_hi = sb("bias_hi", [P, 3, A], f32r)
        seg0_pos = sb("seg0_pos", [P, D])
        seg_diff = sb("seg_diff", [P, D])
        seg0 = sb("seg0", [P, D])
        dense_b = sb("dense_b", [P, D])
        gamma = sb("gamma", [P, D])
        beta = sb("beta", [P, D])
        attn_bo = sb("attn_bo", [P, D])
        ident = sb("ident", [P, P])
        before = sb("before", [P, P], bf16)
        ones_bf = sb("ones_bf", [P, P], bf16)
        expert_i = sb("expert_i", [P, NE], i32)
        token_i = sb("token_i", [P, B], i32)
        expert_no = sb("expert_no", [P, NE])
        token_no = sb("token_no", [P, B])
        minus_half = sb("minus_half", [P, 1])
        ids = sb("ids", [P, B + G], i32)
        seg_i = sb("seg_i", [P, B + G], i32)
        seg_f = sb("seg_f", [P, B + G])
        ids4 = sb("ids4", [P, G], i32)
        seg4 = sb("seg4", [P, G])
        tok = [sb(f"tok{k}", [P, D]) for k in range(G)]
        graph = [sb(f"graph{k}", [P, S]) for k in range(G)]
        seg_part = sb("seg_part", [P, D])
        seg_part2 = sb("seg_part2", [P, D])
        emb = [sb(f"emb{k}", [P, D]) for k in range(2)]
        emb_b = [sb(f"emb_b{k}", [P, D]) for k in range(2)]
        aggT = sb("aggT", [DC, 2, S])
        h0 = sb("h0", [P, D])
        h_stats = sb("h_stats", [P, 6])
        h_mv = sb("h_mv", [P, 2])
        h_ve = sb("h_ve", [P, 1])
        h_rstd = sb("h_rstd", [P, 1])
        hn = sb("hn", [P, D])
        hg = sb("hg", [P, D])
        h1 = [sb(f"h1_{k}", [P, D]) for k in range(2)]
        stats1 = sb("stats1", [P, 6])
        mv1 = sb("mv1", [P, 2])
        ve1 = sb("ve1", [P, 1])
        rstd1 = sb("rstd1", [P, 1])
        x_full = sb("x_full", [P, D])
        x_cat = [sb(f"x_cat{k}", [P, 4, P]) for k in range(2)]
        h_res = sb("h_res", [P, B, D])
        xT = sb("xT", [P, 4, G * S], f32r)
        qT = sb("qT", [P, A // P, G * S])
        kT = sb("kT", [P, A // P, G * S])
        v = sb("v", [P, G, A])
        score = [sb(f"score{k}", [P, NH, S]) for k in range(2)]
        prob = [sb(f"prob{k}", [P, NH, S]) for k in range(2)]
        band_max = sb("band_max", [P, NH])
        band_max0 = sb("band_max0", [P, NH])
        e_zero = sb("e_zero", [P, NH])
        band_sum = sb("band_sum", [P, NH])
        denom = sb("denom", [P, NH])
        r_denom = sb("r_denom", [P, NH])
        p_zero = sb("p_zero", [P, NH])
        probT = sb("probT", [P, NH, S])
        oT = sb("oT", [P, A // P, S])
        h2 = [sb(f"h2_{k}", [P, D]) for k in range(2)]
        stats2 = sb("stats2", [P, 6])
        mv2 = sb("mv2", [P, 2])
        ve2 = sb("ve2", [P, 1])
        rstd2 = sb("rstd2", [P, 1])
        row_a = [sb(f"row_a{k}", [P, ROW]) for k in range(2)]
        row_b = [sb(f"row_b{k}", [P, ROW]) for k in range(2)]
        x2T = sb("x2T", [DC, 2, S])
        logits = sb("logits", [P, NE])
        top = sb("top", [P, 8])
        top_i = sb("top_i", [P, 8], u32)
        top_f = sb("top_f", [P, 2])
        is_1 = sb("is_1", [P, NE])
        is_2 = sb("is_2", [P, NE])
        is_any = sb("is_any", [P, NE], bf16)
        gap = sb("gap", [P, 1])
        e_gap = sb("e_gap", [P, 1])
        one_e = sb("one_e", [P, 1])
        weight2 = [sb(f"weight2_{k}", [P, 1]) for k in range(2)]
        where = sb("where", [P, NE])
        pick1 = sb("pick1", [P, NE])
        pick2 = sb("pick2", [P, NE])
        pos_f = sb("pos_f", [P, 2])
        pos = [sb(f"pos{k}", [P, 2], i32) for k in range(2)]

        ps_s = ctx.enter_context(nc.psum_tensor("ps_s", [P, 1024], f32))
        ps_probT = [ctx.enter_context(nc.psum_tensor(f"ps_probT{i}", [P, 512], f32)) for i in range(2)]
        ps_o = ctx.enter_context(nc.psum_tensor("ps_o", [P, 1024], f32))
        ps_a = ctx.enter_context(nc.psum_tensor("ps_a", [P, 512], f32))
        ps_x = ctx.enter_context(nc.psum_tensor("ps_x", [P, 512], f32))
        ps_score = ps_s[:].rearrange("p (o i s) -> p o i s", o=2, s=S)
        ps_qk = [ps_s[:, 0:512], ps_s[:, 512:1024]]
        ps_oT = ps_o[:, 0:A].rearrange("p (c s) -> p c s", s=S)
        ps_attn = ps_o[:, A:A + D]
        ps_logits = ps_x[:, 0:NE]
        ps_rank = ps_x[:, 16:16 + NE]
        ps_total = ps_x[:, 32:32 + NE]
        ps_agg = ps_a[0:DC, 0:2 * S].rearrange("p (c s) -> p c s", s=S)
        ps_x2T = ps_agg
        ps_proj = ps_a[:, 2 * S:2 * S + D]
        ps_v = [ps_a, ps_x]

        const_in = sem("const_in")
        ids_in = sem("ids_in")
        w_in = {m: sem(f"w{m}_in") for m in "qkv"}
        pad_zero = sem("pad_zero")
        setup_pool = sem("setup_pool")
        setup_dve = sem("setup_dve")
        w_hi = sem("w_hi")
        w_lo = sem("w_lo")
        graph_in = [sem(f"graph_in{k}") for k in range(G)]
        tok_in = [sem(f"tok_in{k}") for k in range(G)]
        staged = sem("staged")
        emb_done = sem("emb_done")
        agg_mm = sem("agg_mm")
        agg_ev = sem("agg_ev")
        proj_mm = sem("proj_mm")
        h0_done = sem("h0_done")
        h0_rstd = sem("h0_rstd")
        hn_done = sem("hn_done")
        h1_done = sem("h1_done")
        h1_stat = sem("h1_stat")
        h1_rstd = sem("h1_rstd")
        x_done = sem("x_done")
        x_lo = sem("x_lo")
        xt_mm = sem("xt_mm")
        xt_ev = sem("xt_ev")
        qk_mm = [sem("qk_mm_even"), sem("qk_mm_odd")]
        qk_ev = [sem("qk_ev_even"), sem("qk_ev_odd")]
        v_mm = [sem("v_mm_low"), sem("v_mm_high")]
        v_ev = [sem("v_ev_low"), sem("v_ev_high")]
        score_mm = sem("score_mm")
        score_ev = sem("score_ev")
        shear_out = sem("shear_out")
        band_in = sem("band_in")
        max_done = sem("max_done")
        sub_done = sem("sub_done")
        exp_done = sem("exp_done")
        norm_done = sem("norm_done")
        fill_done = sem("fill_done")
        probT_mm = sem("probT_mm")
        probT_ev = sem("probT_ev")
        oT_mm = sem("oT_mm")
        oT_ev = sem("oT_ev")
        attn_mm = sem("attn_mm")
        h2_done = sem("h2_done")
        h2_rstd = sem("h2_rstd")
        x2_done = sem("x2_done")
        x2T_mm = sem("x2T_mm")
        x2T_ev = sem("x2T_ev")
        logit_mm = sem("logit_mm")
        choice = sem("choice")
        e_gap_done = sem("e_gap_done")
        rank_mm = sem("rank_mm")
        placed = sem("placed")
        rank_free = sem("rank_free")
        row_done = sem("row_done")
        out_free = [sem(f"out_free{k}") for k in range(2)]
        rowa_free = [sem(f"rowa_free{k}") for k in range(2)]
        rowb_free = [sem(f"rowb_free{k}") for k in range(2)]
        block = ctx.enter_context(nc.Block())

        def bcast(row):
            return bass.AP(row.tensor, row.offset, [[0, P]] + list(row.ap))

        def all_heads(stat, w=BAND):
            return stat[:].unsqueeze(2).broadcast_to([P, NH, w])

        @block.sync
        def _(sp):
            sp.dma_start(ids[:, 0:B], x_ids).then_inc(ids_in, 16)
            sp.dma_start(seg_i[:, 0:B], mask).then_inc(ids_in, 16)
            sp.dma_start(seg0_pos[:], dram["pos_emb"]).then_inc(const_in, 16)
            sp.dma_start(seg0[:], bcast(dram["seg_emb"][0])).then_inc(const_in, 16)
            sp.dma_start(seg_diff[:], bcast(dram["seg_emb"][1])).then_inc(const_in, 16)
            sp.dma_start(dense_b[:], bcast(dram["dense_b"])).then_inc(const_in, 16)

            def load_graph(n, k):
                sp.dma_start(graph[k][:], graphT[n]).then_inc(graph_in[k], 16)

            for k in range(G):
                load_graph(k, k)
            sp.dma_start(w_dense[:], dram["dense_w"].rearrange("(c p) e -> p c e", p=DC)).then_inc(const_in, 16)
            sp.dma_start(gamma[:], bcast(dram["ln_gamma"])).then_inc(const_in, 16)
            sp.dma_start(beta[:], bcast(dram["ln_beta"])).then_inc(const_in, 16)
            sp.dma_start(attn_bo[:], bcast(dram["attn_bo"])).then_inc(const_in, 16)
            sp.dma_start(w_router[:], dram["router"].rearrange("(c p) e -> p c e", p=DC)).then_inc(const_in, 16)
            sp.dma_start(w_o[:], dram["wo"].rearrange("(c p) e -> p c e", p=P)).then_inc(const_in, 16)
            sp.wait_ge(setup_pool, 1)
            sp.dma_start(shear[0:P * PITCH].rearrange("(n h m) -> n h m", h=NH, m=SLOT)[:, :, 0:HALF],
                         prob[0][:, :, 0:HALF]).then_inc(pad_zero, 16)
            sp.dma_start(shear[P * PITCH:P * PITCH + HALF].rearrange("(o m) -> o m", o=1),
                         prob[0][0:1, 0, 0:HALF]).then_inc(pad_zero, 16)
            sp.wait_ge(pad_zero, 32)

            def group(g, more):
                if more:
                    for k in range(G):
                        wait_apart(sp, setup_pool, agg_mm, 4 * g + k + 1)
                        load_graph(4 * g + 4 + k, k)
                for k in range(G):
                    n = 4 * g + k
                    wait_apart(sp, setup_pool, score_ev, 2 * n + 2)
                    sp.dma_start(shear[0:P * PITCH].rearrange("(n h m) -> n h m", h=NH, m=SLOT)[:, :, HALF:SLOT],
                                 score[k % 2][:]).then_inc(shear_out, 16)
                    wait_apart(sp, setup_pool, shear_out, 16 * n + 16)
                    if k >= 2:
                        wait_apart(sp, setup_pool, probT_mm, 3 * n - 3)
                    sp.dma_start(prob[k % 2][:, :, 0:BAND],
                                 bass.AP(shear.tensor, 0, [[PITCH + 1, P], [SLOT, NH], [1, BAND]])).then_inc(band_in, 16)
                    if k >= 2:
                        m = n - 2
                        wait_apart(sp, setup_pool, h2_done, 3 * m + 1)
                        sp.dma_start(out[bass.ds(m * S, S), :], h2[k % 2][:]).then_inc(out_free[k % 2], 16)
                    wait_apart(sp, setup_pool, band_in, 16 * n + 16)
                for k in range(2, G):
                    m = 4 * g + k
                    wait_apart(sp, setup_pool, h2_done, 3 * m + 1)
                    sp.dma_start(out[bass.ds(m * S, S), :], h2[k % 2][:]).then_inc(out_free[k % 2], 16)

            with sp.Fori(0, NG - 1) as g:
                group(g, True)
            group(NG - 1, False)
            for k in range(2):
                sp.wait_ge(out_free[k], 16 * (B // 2 + 1))

        @block.gpsimd
        def _(pool):
            setup = [0]

            def made(ins):
                setup[0] += 1
                ins.then_inc(setup_pool, 1)
                pool.wait_ge(setup_pool, setup[0])

            made(pool.memset(prob[0][:], 0.0))
            made(pool.memset(ids[:, B:B + G], 0))
            pool.wait_ge(ids_in, 32)
            pool.tensor_copy(ids4[:], ids[:, 0:G]).then_inc(staged, 1)
            pool.wait_ge(staged, 1)

            def gather(k):
                pool.indirect_dma_start(tok[k][:], None, dram["tok_emb"],
                                        bass.IndirectOffsetOnAxis(ap=ids4[:, k:k + 1], axis=0)).then_inc(tok_in[k], 16)

            for k in range(G):
                gather(k)
            made(pool.memset(seg_i[:, B:B + G], 0))
            made(pool.tensor_copy(seg_f[:], seg_i[:]))
            pool.tensor_copy(seg4[:], seg_f[:, 0:G]).then_inc(staged, 1)
            made(pool.memset(minus_half[:], -0.5))
            made(pool.memset(ident[:], 0.0))
            made(pool.affine_select(out=ident[:], in_=ident[:], compare_op=ALU.not_equal, fill=1.0, base=0,
                                    pattern=[[-1, P]], channel_multiplier=1))
            for k in range(2):
                made(pool.memset(x_cat[k][:, 3, :], 0.0))
                made(pool.memset(x_cat[k][:, 3, 64:65], 1.0))
                made(pool.memset(x_cat[k][:, 3, 96:97], 1.0))
            made(pool.iota(expert_i[:], pattern=[[1, NE]], base=0, channel_multiplier=0))
            made(pool.tensor_copy(expert_no[:], expert_i[:]))
            made(pool.iota(token_i[:], pattern=[[S, B]], base=0, channel_multiplier=1))
            made(pool.tensor_copy(token_no[:], token_i[:]))
            made(pool.tensor_scalar(route[:], expert_no[:], float(REGION), None, ALU.mult))
            made(pool.memset(ones_bf[:], 1.0))
            made(pool.memset(before[:], 1.0))
            made(pool.affine_select(out=before[:], in_=before[:], compare_op=ALU.is_ge, fill=0.0, base=-1,
                                    pattern=[[1, P]], channel_multiplier=-1))
            pool.wait_ge(const_in, 16 * 10)
            made(pool.tensor_tensor(seg0_pos[:], seg0_pos[:], seg0[:], ALU.add))
            made(pool.tensor_tensor(seg_diff[:], seg_diff[:], seg0[:], ALU.subtract))
            assert setup[0] == CONSTANTS
            for i, free in enumerate(rowa_free + rowb_free):
                pool.dma_start(rows[NOWHERE + i:NOWHERE + i + 1, 0:P], ident[0:1, :]).then_inc(free, 16)

            def embed(a, k, first):
                if k >= 2 or not first:
                    wait_apart(pool, setup_pool, agg_mm, a - 1)
                    wait_apart(pool, setup_pool, h0_done, 3 * a - 5)
                pool.tensor_scalar(seg_part[:], seg_diff[:], seg4[:, k:k + 1], None, ALU.mult).then_inc(emb_done, 1)
                wait_apart(pool, setup_pool, emb_done, 4 * a + 1)
                pool.tensor_tensor(seg_part2[:], seg_part[:], seg0_pos[:], ALU.add).then_inc(emb_done, 1)
                wait_apart(pool, setup_pool, emb_done, 4 * a + 2)
                wait_apart(pool, setup_pool, tok_in[k], 4 * (a - k) + 16)
                pool.tensor_tensor(emb[k % 2][:], tok[k][:], seg_part2[:], ALU.add).then_inc(emb_done, 1)
                wait_apart(pool, setup_pool, emb_done, 4 * a + 3)
                pool.tensor_tensor(emb_b[k % 2][:], emb[k % 2][:], dense_b[:], ALU.add).then_inc(emb_done, 1)

            def rstd(var_sem, value, mv, ve, out_, eps, done, n):
                wait_apart(pool, setup_pool, var_sem, value)
                pool.tensor_scalar(ve[:], mv[:, 1:2], eps, None, ALU.add).then_inc(done, 1)
                wait_apart(pool, setup_pool, done, 2 * n + 1)
                pool.tensor_tensor(out_[:], ve[:], minus_half[:], ALU.pow).then_inc(done, 1)

            def rstd0(a):
                rstd(h0_done, 3 * a + 3, h_mv, h_ve, h_rstd, 1e-12, h0_rstd, a)

            def affine(a, k):
                wait_apart(pool, setup_pool, hn_done, a + 1)
                pool.tensor_tensor(hg[:], hn[:], gamma[:], ALU.mult).then_inc(h1_done, 1)
                wait_apart(pool, setup_pool, h1_done, 3 * a + 1)
                pool.tensor_tensor(h1[k % 2][:], hg[:], beta[:], ALU.add).then_inc(h1_done, 1)
                wait_apart(pool, setup_pool, h1_done, 3 * a + 2)
                pool.tensor_tensor(h_res[:, bass.ds(a, 1), :].rearrange("p o d -> p (o d)"), h1[k % 2][:],
                                   attn_bo[:], ALU.add).then_inc(h1_done, 1)

            def rstd1_(a):
                rstd(h1_stat, 2 * a + 2, mv1, ve1, rstd1, 1e-5, h1_rstd, a)

            def low_part(a, k):
                wait_apart(pool, setup_pool, x_done, 3 * a + 3)
                flat = x_cat[k % 2][:].rearrange("p c s -> p (c s)")
                pool.tensor_tensor(flat[:, D:2 * D], x_full[:], flat[:, 0:D], ALU.subtract).then_inc(x_lo, 1)

            def stage_seg(g):
                pool.tensor_copy(seg4[:], seg_f[:, bass.ds(4 * g + 4, G)]).then_inc(staged, 1)
                wait_apart(pool, setup_pool, staged, 2 * g + 4)

            def stage_ids(g):
                pool.tensor_copy(ids4[:], ids[:, bass.ds(4 * g + 8, G)]).then_inc(staged, 1)
                wait_apart(pool, setup_pool, staged, 2 * g + 5)

            def subtract_max(n, k):
                wait_apart(pool, setup_pool, max_done, 2 * n + 2)
                band = prob[k % 2][:, :, 0:BAND]
                pool.tensor_tensor(band, band, all_heads(band_max0), ALU.subtract).then_inc(sub_done, 1)

            def fill(n, k):
                wait_apart(pool, setup_pool, norm_done, 5 * n + 4)
                pool.tensor_copy(prob[k % 2][:, :, BAND:S], all_heads(p_zero, S - BAND)).then_inc(fill_done, 1)

            def rstd2_(n):
                rstd(h2_done, 3 * n + 3, mv2, ve2, rstd2, 1e-5, h2_rstd, n)

            def scatter(n, k):
                wait_apart(pool, setup_pool, placed, 9 * n + 9)
                pool.tensor_copy(row_a[k % 2][:, D + 1:D + 2], token_no[:, bass.ds(n, 1)]).then_inc(row_done, 1)
                wait_apart(pool, setup_pool, rowb_free[k % 2], 8 * (n - k) + 16 * (k // 2) + 16)
                pool.tensor_copy(row_b[k % 2][:, 0:D], row_a[k % 2][:, 0:D]).then_inc(row_done, 1)
                pool.tensor_copy(row_b[k % 2][:, D + 1:D + 2], token_no[:, bass.ds(n, 1)]).then_inc(row_done, 1)
                pool.tensor_copy(row_b[k % 2][:, D:D + 1], weight2[k % 2][:]).then_inc(row_done, 1)
                wait_apart(pool, setup_pool, row_done, 4 * n + 4)
                for row, free, c in ((row_a, rowa_free, 0), (row_b, rowb_free, 1)):
                    pool.indirect_dma_start(rows, bass.IndirectOffsetOnAxis(ap=pos[k % 2][:, c:c + 1], axis=0),
                                            row[k % 2][:], None).then_inc(free[k % 2], 16)

            pool.wait_ge(staged, 2)
            for k in range(G):
                embed(k, k, True)
                rstd0(k)
                affine(k, k)
                rstd1_(k)
                low_part(k, k)
            pool.wait_ge(emb_done, 4 * G)
            pool.tensor_copy(ids4[:], ids[:, G:2 * G]).then_inc(staged, 1)
            pool.wait_ge(staged, 3)
            for k in range(G):
                gather(k)

            def group(g, more):
                n = 4 * g
                a = n + 4
                if more:
                    stage_seg(g)
                    embed(a, 0, False)
                    embed(a + 1, 1, False)
                    rstd0(a)
                    affine(a, 0)
                subtract_max(n, 0)
                if more:
                    rstd1_(a)
                    low_part(a, 0)
                fill(n, 0)
                if more:
                    rstd0(a + 1)
                    affine(a + 1, 1)
                    rstd1_(a + 1)
                    low_part(a + 1, 1)
                subtract_max(n + 1, 1)
                if more:
                    embed(a + 2, 2, False)
                fill(n + 1, 1)
                if more:
                    embed(a + 3, 3, False)
                    rstd0(a + 2)
                    affine(a + 2, 2)
                    rstd1_(a + 2)
                    low_part(a + 2, 2)
                subtract_max(n + 2, 2)
                if more:
                    rstd0(a + 3)
                    affine(a + 3, 3)
                    rstd1_(a + 3)
                fill(n + 2, 2)
                if more:
                    low_part(a + 3, 3)
                rstd2_(n)
                subtract_max(n + 3, 3)
                rstd2_(n + 1)
                rstd2_(n + 2)
                fill(n + 3, 3)
                scatter(n, 0)
                scatter(n + 1, 1)
                rstd2_(n + 3)
                if more:
                    stage_ids(g)
                    for k in range(G):
                        gather(k)
                scatter(n + 2, 2)
                scatter(n + 3, 3)

            with pool.Fori(0, NG - 1) as g:
                group(g, True)
            group(NG - 1, False)
            for k in range(G):
                pool.wait_ge(tok_in[k], 16 * (NG + 1))
            for k in range(2):
                pool.wait_ge(rowa_free[k], 16 * (B // 2 + 1))
                pool.wait_ge(rowb_free[k], 16 * (B // 2 + 1))

        @block.scalar
        def _(act):
            for m, raw in (("q", qT), ("k", kT), ("v", v)):
                w, flat = dram["w" + m], raw[:].rearrange("p a b -> p (a b)")
                act.dma_start(flat[:, 0:A], w[0:P]).then_inc(w_in[m], 16)
                act.dma_start(flat[0:64, A:2 * A], w[P:D]).then_inc(w_in[m], 16)
                act.dma_start(flat[64:P, A:2 * A], w[0:64]).then_inc(w_in[m], 16)
                act.dma_start(flat[:, 2 * A:3 * A], w[64:D]).then_inc(w_in[m], 16)
                for p in (64, 96):
                    act.dma_start(bias_row[m][p:p + 1, :], dram["b" + m].rearrange("(o n) -> o n", o=1)).then_inc(w_in[m], 16)

            def agg(a):
                act.wait_ge(agg_mm, a + 1)
                if not isinstance(a, int) or a:
                    act.wait_ge(proj_mm, a)
                act.activation(aggT[:], ps_agg, ACT.Copy).then_inc(agg_ev, 1)

            def x_t(a, k):
                act.wait_ge(xt_mm, a + 1)
                act.activation(xT[:, :, k * S:(k + 1) * S], ps_x[:].rearrange("p (c s) -> p c s", s=S),
                               ACT.Copy).then_inc(xt_ev, 1)

            def high(m, raw):
                act.wait_ge(w_in[m], 16 * 6)
                act.activation(w_split[m][:, 0:3, :].rearrange("p c n -> p (c n)"),
                               raw[:].rearrange("p a b -> p (a b)")[:, 0:3 * A], ACT.Copy).then_inc(w_hi, 1)
                i = "qkv".index(m)
                for p in (64, 96):
                    act.activation(bias_hi[p:p + 1, i, :], bias_row[m][p:p + 1, :], ACT.Copy).then_inc(w_hi, 1)

            def qk(g, t):
                act.wait_ge(qk_mm[0], 6 * g + t + 1)
                j = 2 * t
                dst = (qT if j < 6 else kT)[:, j % 6, :]
                act.activation(dst, ps_qk[0], ACT.Copy).then_inc(qk_ev[0], 1)

            def v_low(n, k):
                act.wait_ge(v_mm[0], n + 1)
                act.activation(v[:, k, 0:A // 2], ps_v[0][:, 0:A // 2], ACT.Copy).then_inc(v_ev[0], 1)

            def scores(n, k, units=(0, 1)):
                if k >= 2 and 0 in units:
                    act.wait_ge(shear_out, 16 * n - 16)
                by_bank = score[k % 2][:].rearrange("p (i o) s -> p o i s", o=2)
                for u in units:
                    i0, i1 = HEAD_PAIRS[u]
                    act.wait_ge(score_mm, 2 * n + u + 1)
                    act.activation(by_bank[:, :, i0:i1, :], ps_score[:, :, 0:i1 - i0, :], ACT.Copy).then_inc(score_ev, 1)

            def exps(n, k):
                act.wait_ge(sub_done, n + 1)
                band = prob[k % 2][:, :, 0:BAND]
                act.activation(band, band, ACT.Exp).then_inc(exp_done, 1)
                act.activation(e_zero[:], band_max0[:], ACT.Exp, scale=-1.0).then_inc(exp_done, 1)

            def o_t(n):
                act.wait_ge(oT_mm, n + 1)
                act.activation(oT[:], ps_oT, ACT.Copy).then_inc(oT_ev, 1)

            def x2_t(n):
                act.wait_ge(x2T_mm, n + 1)
                act.activation(x2T[:], ps_x2T, ACT.Copy).then_inc(x2T_ev, 1)

            def exp_gap(n):
                act.wait_ge(choice, 8 * n + 8)
                act.activation(e_gap[:], gap[:], ACT.Exp).then_inc(e_gap_done, 1)

            agg(0)
            high("q", qT)
            agg(1)
            x_t(0, 0)
            high("k", kT)
            agg(2)
            x_t(1, 1)
            agg(3)
            high("v", v)
            x_t(2, 2)
            x_t(3, 3)
            for t in range(6):
                qk(0, t)

            def group(g, more):
                n = 4 * g
                a = n + 4
                scores(n, 0)
                v_low(n, 0)
                v_low(n + 1, 1)
                scores(n + 1, 1)
                v_low(n + 2, 2)
                v_low(n + 3, 3)
                if more:
                    agg(a)
                scores(n + 2, 2)
                exps(n, 0)
                if more:
                    agg(a + 1)
                    x_t(a, 0)
                scores(n + 3, 3, (0,))
                if more:
                    agg(a + 2)
                scores(n + 3, 3, (1,))
                exps(n + 1, 1)
                if more:
                    x_t(a + 1, 1)
                    agg(a + 3)
                    x_t(a + 2, 2)
                o_t(n)
                exps(n + 2, 2)
                o_t(n + 1)
                if more:
                    x_t(a + 3, 3)
                x2_t(n)
                o_t(n + 2)
                exps(n + 3, 3)
                x2_t(n + 1)
                exp_gap(n)
                o_t(n + 3)
                x2_t(n + 2)
                exp_gap(n + 1)
                if more:
                    qk(g + 1, 0)
                    qk(g + 1, 1)
                exp_gap(n + 2)
                if more:
                    qk(g + 1, 2)
                x2_t(n + 3)
                if more:
                    qk(g + 1, 3)
                    qk(g + 1, 4)
                exp_gap(n + 3)
                if more:
                    qk(g + 1, 5)

            with act.Fori(0, NG - 1) as g:
                group(g, True)
            group(NG - 1, False)

        @block.vector
        def _(dve):
            def residual(a, k):
                dve.wait_ge(proj_mm, a + 1)
                dve.wait_ge(emb_done, 4 * a + 4)
                dve.tensor_tensor(h0[:], ps_proj, emb_b[k % 2][:], ALU.add).then_inc(h0_done, 1)
                dve.wait_ge(h0_done, 3 * a + 1)
                dve.bn_stats(h_stats[:], h0[:]).then_inc(h0_done, 1)
                wait_apart(dve, setup_pool, h0_done, 3 * a + 2)
                dve.bn_aggr(h_mv[:], h_stats[:]).then_inc(h0_done, 1)

            def norm0(a):
                dve.wait_ge(h0_rstd, 2 * a + 2)
                dve.tensor_scalar(hn[:], h0[:], h_mv[:, 0:1], h_rstd[:, 0:1], ALU.subtract, ALU.mult).then_inc(hn_done, 1)

            def stat1(a, k):
                dve.wait_ge(h1_done, 3 * a + 2)
                dve.bn_stats(stats1[:], h1[k % 2][:]).then_inc(h1_stat, 1)
                wait_apart(dve, setup_pool, h1_stat, 2 * a + 1)
                dve.bn_aggr(mv1[:], stats1[:]).then_inc(h1_stat, 1)

            def x_parts(a, k):
                dve.wait_ge(h1_rstd, 2 * a + 2)
                if k >= 2 or not isinstance(a, int):
                    dve.wait_ge(xt_mm, a - 1)
                cat = x_cat[k % 2][:].rearrange("p c s -> p (c s)")
                dve.tensor_scalar(cat[:, 0:D].bitcast(f32r), h1[k % 2][:], mv1[:, 0:1], rstd1[:, 0:1],
                                  ALU.subtract, ALU.mult).then_inc(x_done, 1)
                dve.tensor_scalar(cat[:, 2 * D:2 * D + 64].bitcast(f32r), h1[k % 2][:, P:D], mv1[:, 0:1], rstd1[:, 0:1],
                                  ALU.subtract, ALU.mult).then_inc(x_done, 1)
                dve.tensor_scalar(x_full[:], h1[k % 2][:], mv1[:, 0:1], rstd1[:, 0:1],
                                  ALU.subtract, ALU.mult).then_inc(x_done, 1)

            def low(m, raw):
                i = "qkv".index(m)
                flat = raw[:].rearrange("p a b -> p (a b)")
                dve.wait_ge(w_hi, 3 * i + 3)
                dve.tensor_tensor(w_split[m][:, 3, :], flat[:, 0:A], w_split[m][:, 0, :].bitcast(f32),
                                  ALU.subtract).then_inc(w_lo, 1)
                dve.tensor_tensor(w_split[m][0:64, 4, :], flat[0:64, A:2 * A], w_split[m][0:64, 1, :].bitcast(f32),
                                  ALU.subtract).then_inc(w_lo, 1)
                dve.memset(w_split[m][64:P, 4, :].bitcast(f32), 0.0).then_inc(w_lo, 1)
                dve.wait_ge(w_lo, 5 * i + 3)
                dve.tensor_copy(w_split[m][64:65, 4, :], bias_hi[64:65, i, :].bitcast(f32)).then_inc(w_lo, 1)
                dve.tensor_tensor(w_split[m][96:97, 4, :], bias_row[m][96:97, :], bias_hi[96:97, i, :].bitcast(f32),
                                  ALU.subtract).then_inc(w_lo, 1)

            def qk(g, t):
                dve.wait_ge(qk_mm[1], 6 * g + t + 1)
                j = 2 * t + 1
                dst = (qT if j < 6 else kT)[:, j % 6, :]
                dve.tensor_copy(dst, ps_qk[1]).then_inc(qk_ev[1], 1)

            def v_high(n, k):
                dve.wait_ge(v_mm[1], n + 1)
                dve.tensor_copy(v[:, k, A // 2:A], ps_v[1][:, 0:A // 2]).then_inc(v_ev[1], 1)

            def maximum(n, k):
                dve.wait_ge(band_in, 16 * n + 16)
                dve.tensor_reduce(band_max[:], prob[k % 2][:, :, 0:BAND], AX.X, ALU.max).then_inc(max_done, 1)
                dve.wait_ge(max_done, 2 * n + 1)
                dve.tensor_scalar(band_max0[:], band_max[:], 0.0, None, ALU.max).then_inc(max_done, 1)

            def normalise(n, k):
                dve.wait_ge(exp_done, 2 * n + 2)
                band = prob[k % 2][:, :, 0:BAND]
                dve.tensor_reduce(band_sum[:], band, AX.X, ALU.add).then_inc(norm_done, 1)
                dve.wait_ge(norm_done, 5 * n + 1)
                dve.scalar_tensor_tensor(denom[:], e_zero[:], float(S - BAND), band_sum[:],
                                         ALU.mult, ALU.add).then_inc(norm_done, 1)
                dve.wait_ge(norm_done, 5 * n + 2)
                dve.reciprocal(r_denom[:], denom[:]).then_inc(norm_done, 1)
                dve.wait_ge(norm_done, 5 * n + 3)
                dve.tensor_tensor(p_zero[:], e_zero[:], r_denom[:], ALU.mult).then_inc(norm_done, 1)
                dve.tensor_tensor(band, band, all_heads(r_denom), ALU.mult).then_inc(norm_done, 1)

            def prob_t(n, k, u):
                dve.wait_ge(probT_mm, 3 * n + u + 1)
                dve.tensor_copy(probT[:, 4 * u:4 * u + 4, :],
                                ps_probT[(3 * k + u) % 2][:].rearrange("p (h s) -> p h s", s=S)).then_inc(probT_ev, 1)

            def residual2(n, k):
                dve.wait_ge(attn_mm, n + 1)
                dve.wait_ge(out_free[k % 2], 8 * (n - k) + 16 * (k // 2) + 16)
                dve.tensor_tensor(h2[k % 2][:], ps_attn, h_res[:, bass.ds(n, 1), :].rearrange("p o d -> p (o d)"),
                                  ALU.add).then_inc(h2_done, 1)
                dve.wait_ge(h2_done, 3 * n + 1)
                dve.bn_stats(stats2[:], h2[k % 2][:]).then_inc(h2_done, 1)
                wait_apart(dve, setup_pool, h2_done, 3 * n + 2)
                dve.bn_aggr(mv2[:], stats2[:]).then_inc(h2_done, 1)

            def norm2(n, k):
                dve.wait_ge(h2_rstd, 2 * n + 2)
                dve.wait_ge(rowa_free[k % 2], 8 * (n - k) + 16 * (k // 2) + 16)
                dve.tensor_scalar(row_a[k % 2][:, 0:D], h2[k % 2][:], mv2[:, 0:1], rstd2[:, 0:1],
                                  ALU.subtract, ALU.mult).then_inc(x2_done, 1)

            def choose(n):
                dve.wait_ge(logit_mm, n + 1)
                dve.tensor_copy(logits[:], ps_logits).then_inc(choice, 1)
                wait_apart(dve, setup_pool, choice, 8 * n + 1)
                dve.max(top[:], logits[:]).then_inc(choice, 1)
                wait_apart(dve, setup_pool, choice, 8 * n + 2)
                dve.max_index(top_i[:], top[:], logits[:]).then_inc(choice, 1)
                dve.wait_ge(choice, 8 * n + 3)
                dve.tensor_copy(top_f[:], top_i[:, 0:2]).then_inc(choice, 1)
                dve.wait_ge(choice, 8 * n + 4)
                dve.tensor_scalar(is_1[:], expert_no[:], top_f[:, 0:1], None, ALU.is_equal).then_inc(choice, 1)
                dve.tensor_scalar(is_2[:], expert_no[:], top_f[:, 1:2], None, ALU.is_equal).then_inc(choice, 1)
                dve.wait_ge(choice, 8 * n + 6)
                dve.tensor_tensor(is_any[:], is_1[:], is_2[:], ALU.add).then_inc(choice, 1)
                dve.tensor_tensor(gap[:], top[:, 1:2], top[:, 0:1], ALU.subtract).then_inc(choice, 1)

            def place(n, k):
                dve.wait_ge(rank_mm, n + 1)
                dve.wait_ge(rank_free, n + 1)
                dve.tensor_tensor(where[:], ps_rank, route[:], ALU.add).then_inc(placed, 1)
                dve.tensor_tensor(route[:], ps_total, route[:], ALU.add).then_inc(rank_free, 1)
                dve.wait_ge(placed, 9 * n + 1)
                dve.tensor_tensor(pick1[:], where[:], is_1[:], ALU.mult).then_inc(placed, 1)
                dve.tensor_tensor(pick2[:], where[:], is_2[:], ALU.mult).then_inc(placed, 1)
                dve.wait_ge(placed, 9 * n + 3)
                dve.tensor_reduce(pos_f[:, 0:1], pick1[:], AX.X, ALU.add).then_inc(placed, 1)
                dve.tensor_reduce(pos_f[:, 1:2], pick2[:], AX.X, ALU.add).then_inc(placed, 1)
                dve.wait_ge(placed, 9 * n + 5)
                dve.wait_ge(rowb_free[k % 2], 8 * (n - k) + 16 * (k // 2) + 16)
                dve.tensor_copy(pos[k % 2][:], pos_f[:]).then_inc(placed, 1)
                dve.wait_ge(e_gap_done, n + 1)
                dve.tensor_scalar(one_e[:], e_gap[:], 1.0, None, ALU.add).then_inc(placed, 1)
                dve.wait_ge(placed, 9 * n + 7)
                dve.reciprocal(row_a[k % 2][:, D:D + 1], one_e[:]).then_inc(placed, 1)
                dve.wait_ge(placed, 9 * n + 8)
                dve.tensor_tensor(weight2[k % 2][:], row_a[k % 2][:, D:D + 1], e_gap[:], ALU.mult).then_inc(placed, 1)

            dve.sem_inc(rank_free, 1)
            for s_ in out_free:
                dve.sem_inc(s_, 16)
            dve.wait_ge(setup_pool, CONSTANTS)
            for k in range(G):
                residual(k, k)
                norm0(k)
                stat1(k, k)
                x_parts(k, k)
                if k < 3:
                    low("qkv"[k], (qT, kT, v)[k])
            for t in range(6):
                qk(0, t)

            def group(g, more):
                n = 4 * g
                a = n + 4
                for k in range(G):
                    v_high(n + k, k)
                if more:
                    residual(a, 0)
                    norm0(a)
                maximum(n, 0)
                if more:
                    stat1(a, 0)
                    x_parts(a, 0)
                    residual(a + 1, 1)
                normalise(n, 0)
                if more:
                    norm0(a + 1)
                    stat1(a + 1, 1)
                maximum(n + 1, 1)
                if more:
                    x_parts(a + 1, 1)
                    residual(a + 2, 2)
                normalise(n + 1, 1)
                if more:
                    norm0(a + 2)
                    stat1(a + 2, 2)
                prob_t(n, 0, 0)
                prob_t(n, 0, 1)
                if more:
                    x_parts(a + 2, 2)
                prob_t(n, 0, 2)
                if more:
                    residual(a + 3, 3)
                maximum(n + 2, 2)
                if more:
                    norm0(a + 3)
                    stat1(a + 3, 3)
                residual2(n, 0)
                for u in range(3):
                    prob_t(n + 1, 1, u)
                normalise(n + 2, 2)
                if more:
                    x_parts(a + 3, 3)
                norm2(n, 0)
                residual2(n + 1, 1)
                maximum(n + 3, 3)
                for u in range(3):
                    prob_t(n + 2, 2, u)
                choose(n)
                norm2(n + 1, 1)
                residual2(n + 2, 2)
                normalise(n + 3, 3)
                place(n, 0)
                norm2(n + 2, 2)
                for u in range(3):
                    prob_t(n + 3, 3, u)
                choose(n + 1)
                if more:
                    qk(g + 1, 0)
                residual2(n + 3, 3)
                place(n + 1, 1)
                choose(n + 2)
                if more:
                    qk(g + 1, 1)
                place(n + 2, 2)
                if more:
                    qk(g + 1, 2)
                norm2(n + 3, 3)
                if more:
                    qk(g + 1, 3)
                choose(n + 3)
                if more:
                    qk(g + 1, 4)
                place(n + 3, 3)
                if more:
                    qk(g + 1, 5)

            with dve.Fori(0, NG - 1) as g:
                group(g, True)
            group(NG - 1, False)

        @block.tensor
        def _(pe):
            def mix(a, k):
                pe.wait_ge(emb_done, 4 * a + 3)
                pe.wait_ge(graph_in[k], 4 * (a - k) + 16)
                if not isinstance(a, int) or a:
                    pe.wait_ge(h0_done, 3 * a - 2)
                for c in range(2):
                    mm = pe.matmul(ps_agg[:, c, :], emb[k % 2][:, c * DC:(c + 1) * DC], graph[k][:], start=True, stop=True)
                mm.then_inc(agg_mm, 1)

            def project(a):
                pe.wait_ge(agg_ev, a + 1)
                for c in range(2):
                    mm = pe.matmul(ps_proj, aggT[:, c, :], w_dense[:, c, :], start=c == 0, stop=c == 1)
                mm.then_inc(proj_mm, 1)

            def turn_x(a, k):
                pe.wait_ge(x_lo, a + 1)
                if not isinstance(a, int) or a:
                    pe.wait_ge(xt_ev, a)
                for c in range(4):
                    mm = pe.transpose(ps_x[:, c * S:(c + 1) * S], x_cat[k % 2][:, c, :], ident[:])
                mm.then_inc(xt_mm, 1)

            TERMS = ((0, 0), (1, 1), (2, 2), (0, 3), (3, 4))

            def qk(g, j):
                bank, t = j % 2, j // 2
                if t == 0:
                    pe.wait_ge(xt_ev, 4 * g + 4)
                if t:
                    pe.wait_ge(qk_ev[bank], 6 * g + t)
                elif not isinstance(g, int) or g:
                    pe.wait_ge(score_ev, 8 * g)
                m = "q" if j < 6 else "k"
                for i, (cx, cw) in enumerate(TERMS):
                    mm = pe.matmul(ps_qk[bank], w_split[m][:, cw, (j % 6) * P:(j % 6 + 1) * P], xT[:, cx, :],
                                   start=i == 0, stop=i == KC - 1)
                mm.then_inc(qk_mm[bank], 1)

            def values(n, k):
                for half in range(2):
                    if k:
                        pe.wait_ge(v_ev[half], n)
                    elif half:
                        pe.wait_ge(rank_free, n + 1)
                    for i, (cx, cw) in enumerate(TERMS):
                        mm = pe.matmul(ps_v[half][:, 0:A // 2], xT[:, cx, k * S:(k + 1) * S],
                                       w_split["v"][:, cw, half * (A // 2):(half + 1) * (A // 2)],
                                       start=i == 0, stop=i == KC - 1)
                    mm.then_inc(v_mm[half], 1)

            def scores(g, k, u):
                n = 4 * g + k
                if k == 0 and u == 0:
                    pe.wait_ge(qk_ev[0], 6 * g + 6)
                    pe.wait_ge(qk_ev[1], 6 * g + 6)
                else:
                    pe.wait_ge(score_ev, 2 * n + u)
                i0, i1 = HEAD_PAIRS[u]
                for i in range(i0, i1):
                    for o in range(2):
                        mm = pe.matmul(ps_score[:, o, i - i0, :], qT[64 * o:64 * o + 64, i, k * S:(k + 1) * S],
                                       kT[64 * o:64 * o + 64, i, k * S:(k + 1) * S], start=True, stop=True)
                mm.then_inc(score_mm, 1)

            def turn_prob(n, k, u):
                i = 3 * k + u
                if i >= 2:
                    pe.wait_ge(probT_ev, 3 * (n - k) + i - 1)
                if u == 0:
                    pe.wait_ge(norm_done, 5 * n + 5)
                    pe.wait_ge(fill_done, n + 1)
                for h in range(4 * u, 4 * u + 4):
                    mm = pe.transpose(ps_probT[i % 2][:, (h % 4) * S:(h % 4 + 1) * S], prob[k % 2][:, h, :], ident[:])
                mm.then_inc(probT_mm, 1)

            def weigh(n, k, u):
                pe.wait_ge(probT_ev, 3 * n + u + 1)
                if k == 0 and u == 0:
                    pe.wait_ge(v_ev[0], n + 4)
                    pe.wait_ge(v_ev[1], n + 4)
                if k and u == 2:
                    pe.wait_ge(h2_done, 3 * n - 2)
                for h in range(4 * u, 4 * u + 4):
                    r = 64 * (h % 2)
                    mm = pe.matmul(ps_oT[r:r + 64, h // 2, :], v[:, k, h * HD:(h + 1) * HD], probT[:, h, :],
                                   start=True, stop=True)
                if u == 2:
                    mm.then_inc(oT_mm, 1)

            def attend_a(n, k):
                turn_prob(n, k, 0)
                turn_prob(n, k, 1)

            def attend_b(n, k):
                weigh(n, k, 0)
                turn_prob(n, k, 2)
                weigh(n, k, 1)
                weigh(n, k, 2)

            def output(n):
                pe.wait_ge(oT_ev, n + 1)
                for c in range(A // P):
                    mm = pe.matmul(ps_attn, oT[:, c, :], w_o[:, c, :], start=c == 0, stop=c == A // P - 1)
                mm.then_inc(attn_mm, 1)

            def turn_x2(n, k):
                pe.wait_ge(x2_done, n + 1)
                for c in range(2):
                    mm = pe.transpose(ps_x2T[:, c, :], row_a[k % 2][:, c * DC:(c + 1) * DC], ident[:])
                mm.then_inc(x2T_mm, 1)

            def router(n):
                pe.wait_ge(x2T_ev, n + 1)
                pe.wait_ge(rank_free, n + 1)
                for c in range(2):
                    mm = pe.matmul(ps_logits, x2T[:, c, :], w_router[:, c, :], start=c == 0, stop=c == 1)
                mm.then_inc(logit_mm, 1)

            def rank(n):
                pe.wait_ge(choice, 8 * n + 7)
                pe.matmul(ps_rank, before[:], is_any[:], start=True, stop=True)
                pe.matmul(ps_total, ones_bf[:], is_any[:], start=True, stop=True).then_inc(rank_mm, 1)

            pe.wait_ge(const_in, 16 * 10)
            pe.wait_ge(setup_pool, CONSTANTS)
            for k in range(G):
                mix(k, k)
                project(k)
                if k:
                    turn_x(k - 1, k - 1)
            turn_x(3, 3)
            pe.wait_ge(w_lo, 10)
            for j in range(12):
                qk(0, j)
            pe.wait_ge(w_lo, 15)

            def group(g, more):
                n = 4 * g
                a = n + 4
                for k in range(G):
                    scores(g, k // 2, k % 2)
                    values(n + k, k)
                scores(g, 2, 0)
                if more:
                    pe.wait_ge(v_ev[0], n + 4)
                    mix(a, 0)
                    project(a)
                scores(g, 2, 1)
                if more:
                    mix(a + 1, 1)
                    pe.wait_ge(v_ev[1], n + 4)
                    turn_x(a, 0)
                    project(a + 1)
                scores(g, 3, 0)
                if more:
                    mix(a + 2, 2)
                    turn_x(a + 1, 1)
                    project(a + 2)
                scores(g, 3, 1)
                attend_a(n, 0)
                if more:
                    mix(a + 3, 3)
                attend_b(n, 0)
                if more:
                    project(a + 3)
                    turn_x(a + 2, 2)
                output(n)
                attend_a(n + 1, 1)
                attend_b(n + 1, 1)
                if more:
                    turn_x(a + 3, 3)
                output(n + 1)
                turn_x2(n, 0)
                attend_a(n + 2, 2)
                attend_b(n + 2, 2)
                if more:
                    pe.wait_ge(xt_ev, a + 4)
                router(n)
                turn_x2(n + 1, 1)
                output(n + 2)
                rank(n)
                attend_a(n + 3, 3)
                attend_b(n + 3, 3)
                router(n + 1)
                turn_x2(n + 2, 2)
                if more:
                    qk(g + 1, 0)
                    qk(g + 1, 1)
                output(n + 3)
                rank(n + 1)
                router(n + 2)
                if more:
                    qk(g + 1, 2)
                    qk(g + 1, 3)
                rank(n + 2)
                if more:
                    qk(g + 1, 4)
                    qk(g + 1, 5)
                turn_x2(n + 3, 3)
                if more:
                    qk(g + 1, 6)
                    qk(g + 1, 7)
                    qk(g + 1, 8)
                router(n + 3)
                if more:
                    qk(g + 1, 9)
                rank(n + 3)
                if more:
                    qk(g + 1, 10)
                    qk(g + 1, 11)

            with pe.Fori(0, NG - 1) as g:
                group(g, True)
            group(NG - 1, False)


def expert_block(nc, dram, route):
    out, rows = dram["out"], dram["rows"]
    ctx = ExitStack()
    with ctx:
        def sb(name, shape, dt=f32):
            return ctx.enter_context(nc.sbuf_tensor("ffn_" + name, shape, dt))

        def sem(name):
            return ctx.enter_context(nc.semaphore("ffn_" + name))

        w_in = sb("w_in", [DC + 1, NE, 2, F])
        w_out = sb("w_out", [P, NE, FC, D])
        out_b = sb("out_b", [P, NE, D])
        ident = sb("ident2", [P, P])
        filler = sb("filler", [P, ROW])
        step_i = sb("step_i", [P, 32], i32)
        step = sb("step", [P, 32])
        tile_i = sb("tile_i", [P, TILES], i32)
        tile_no = sb("tile_no", [P, TILES])
        expert_i = sb("expert_i2", [P, NE], i32)
        expert_no = sb("expert_no2", [P, NE])
        base = sb("base", [P, NE])
        count = sb("count", [P, NE])
        over = sb("over", [P, NE, 32])
        tiles = sb("tiles", [P, NE])
        upto = sb("upto", [P, NE])
        begin = sb("begin", [P, NE])
        passed = sb("passed", [P, TILES, NE])
        owner = sb("owner", [P, TILES])
        owned = sb("owned", [P, TILES, NE])
        used = sb("used", [P, TILES])
        offset = sb("offset", [P, TILES])
        row_f = sb("row_f", [P, TILES])
        owner7 = sb("owner7", [P, TILES])
        row_of = sb("row_of", [P, TILES], i32)
        expert_of = sb("expert_of", [P, TILES], i32)
        end_of = sb("end_of", [P, NE], i32)
        RING = 4
        x = [sb(f"x{k}", [P, ROW]) for k in range(RING)]
        xT = [sb(f"xT{k}", [DC + 1, 2, P]) for k in range(2)]
        h = [sb(f"h{k}", [P, F]) for k in range(2)]
        hT = sb("hT", [P, FC, P])
        y = [sb(f"y{k}", [P, D]) for k in range(2)]
        yw = [sb(f"yw{k}", [P, D]) for k in range(2)]
        token = [sb(f"token{k}", [P, 1], i32) for k in range(2)]
        ps_xT = ctx.enter_context(nc.psum_tensor("ps_xT", [P, 512], f32))
        ps_h = [ctx.enter_context(nc.psum_tensor(f"ps_h{k}", [P, 1024], f32)) for k in range(2)]
        ps_hT = ctx.enter_context(nc.psum_tensor("ps_hT", [P, 1024], f32))
        ps_y = ctx.enter_context(nc.psum_tensor("ps_y", [P, 512], f32))

        w_ready = sem("w_ready")
        b_ready = sem("b_ready")
        made_p = sem("made_p")
        made_d = sem("made_d")
        filled = sem("filled")
        x_in = [sem(f"x_in{k}") for k in range(RING)]
        xT_mm = sem("xT_mm")
        xT_ev = sem("xT_ev")
        h_mm = sem("h_mm")
        gelu_done = sem("gelu_done")
        hT_mm = sem("hT_mm")
        hT_ev = sem("hT_ev")
        y_mm = sem("y_mm")
        y_done = sem("y_done")
        added = sem("added")
        block = ctx.enter_context(nc.Block())
        POOL_MADE, DVE_MADE = 10, 27

        @block.sync
        def _(sp):
            for e in range(NE):
                sp.dma_start(w_in[0:DC, e], dram["wi"][e].rearrange("(c p) f -> p c f", p=DC)).then_inc(w_ready, 16)
                sp.dma_start(w_in[DC:DC + 1, e, 1, :], dram["bi"][e:e + 1, :]).then_inc(w_ready, 16)
            sp.wait_ge(made_d, DVE_MADE)
            for e in range(NE):
                at = sp.value_load(end_of[0:1, e:e + 1], min_val=0, max_val=NE * REGION - P)
                sp.dma_start(rows[bass.ds(at, P), :], filler[:]).then_inc(filled, 16)
            sp.dma_start(rows[NOWHERE:NOWHERE + P, :], filler[:]).then_inc(filled, 16)
            sp.wait_ge(filled, 16 * (NE + 1))

            def load(t, k):
                at = sp.value_load(row_of[0:1, bass.ds(t, 1)], min_val=0, max_val=NOWHERE)
                sp.dma_start(x[k][:], rows[bass.ds(at, P), :]).then_inc(x_in[k], 16)

            for k in range(RING):
                load(k, k)
            with sp.Fori(0, TILES // RING - 1) as r:
                for k in range(RING):
                    t = RING * r + k
                    wait_apart(sp, made_p, y_done, 3 * t + 3)
                    load(t + RING, k)
            for t in range(TILES // RING * RING, TILES):
                sp.wait_ge(y_done, 3 * (t - RING) + 3)
                load(t, t % RING)

        @block.gpsimd
        def _(pool):
            made = [0]

            def link(ins):
                made[0] += 1
                ins.then_inc(made_p, 1)
                pool.wait_ge(made_p, made[0])

            link(pool.iota(step_i[:], pattern=[[P, 32]], base=0, channel_multiplier=0))
            link(pool.tensor_copy(step[:], step_i[:]))
            link(pool.iota(tile_i[:], pattern=[[1, TILES]], base=0, channel_multiplier=0))
            link(pool.tensor_copy(tile_no[:], tile_i[:]))
            link(pool.iota(expert_i[:], pattern=[[1, NE]], base=0, channel_multiplier=0))
            link(pool.tensor_copy(expert_no[:], expert_i[:]))
            link(pool.memset(filler[:], 0.0))
            link(pool.memset(filler[:, D + 1:D + 2], float(NO_TOKEN)))
            link(pool.memset(ident[:], 0.0))
            link(pool.affine_select(out=ident[:], in_=ident[:], compare_op=ALU.not_equal, fill=1.0, base=0,
                                    pattern=[[-1, P]], channel_multiplier=1))
            assert made[0] == POOL_MADE

            def add(t, k):
                wait_apart(pool, made_p, y_done, 3 * t + 3)
                pool.indirect_dma_start(out, bass.IndirectOffsetOnAxis(ap=token[k][:], axis=0), yw[k][:], None,
                                        bounds_check=T - 1, oob_is_err=False, compute_op=ALU.add).then_inc(added, 16)
                wait_apart(pool, made_p, added, 16 * t + 16)

            with pool.Fori(0, TILES // 2) as r:
                for k in range(2):
                    add(2 * r + k, k)
            add(TILES - 1, (TILES - 1) % 2)

        @block.scalar
        def _(act):
            for e in range(NE):
                act.dma_start(w_out[:, e], dram["wout"][e].rearrange("(c p) n -> p c n", p=P)).then_inc(w_ready, 16)
            act.dma_start(out_b[:], bass.AP(dram["bo"].tensor, 0, [[0, P], [D, NE], [1, D]])).then_inc(b_ready, 16)
            act.wait_ge(made_d, DVE_MADE)

            def x_t(t, k):
                act.wait_ge(xT_mm, t + 1)
                act.activation(xT[k][0:DC], ps_xT[0:DC, k * 2 * P:(k + 1) * 2 * P].rearrange("p (c s) -> p c s", s=P),
                               ACT.Copy).then_inc(xT_ev, 1)

            def gelu(t, k):
                act.wait_ge(h_mm, t + 1)
                act.activation(h[k][:], ps_h[k][:, 0:F], ACT.Gelu).then_inc(gelu_done, 1)

            x_t(0, 0)
            x_t(1, 1)
            gelu(0, 0)
            with act.Fori(0, (TILES - 3) // 2) as r:
                for k in range(2):
                    t = 2 * r + 1 + k
                    gelu(t, (k + 1) % 2)
                    x_t(t + 1, k)
            gelu(TILES - 2, (TILES - 2) % 2)
            x_t(TILES - 1, (TILES - 1) % 2)
            gelu(TILES - 1, (TILES - 1) % 2)

        @block.vector
        def _(dve):
            made = [0]

            def link(ins):
                made[0] += 1
                ins.then_inc(made_d, 1)
                dve.wait_ge(made_d, made[0])

            def per_expert(t_):
                return t_[:].unsqueeze(1).broadcast_to([P, TILES, NE])

            def per_tile(t_):
                return t_[:].unsqueeze(2).broadcast_to([P, TILES, NE])

            dve.wait_ge(made_p, POOL_MADE)
            link(dve.memset(xT[0][DC:DC + 1], 1.0))
            link(dve.memset(xT[1][DC:DC + 1], 1.0))
            link(dve.tensor_copy(end_of[:], route[:]))
            link(dve.tensor_scalar(base[:], expert_no[:], float(REGION), None, ALU.mult))
            link(dve.tensor_tensor(count[:], route[:], base[:], ALU.subtract))
            link(dve.tensor_tensor(over[:], count[:].unsqueeze(2).broadcast_to([P, NE, 32]),
                                   step[:].unsqueeze(1).broadcast_to([P, NE, 32]), ALU.is_gt))
            link(dve.tensor_reduce(tiles[:], over[:], AX.X, ALU.add))
            link(dve.tensor_copy(upto[:], tiles[:]))
            for e in range(1, NE):
                link(dve.tensor_tensor(upto[:, e:e + 1], upto[:, e - 1:e], tiles[:, e:e + 1], ALU.add))
            link(dve.tensor_tensor(begin[:], upto[:], tiles[:], ALU.subtract))
            link(dve.tensor_tensor(passed[:], per_tile(tile_no), per_expert(upto), ALU.is_ge))
            link(dve.tensor_reduce(owner[:], passed[:], AX.X, ALU.add))
            link(dve.tensor_tensor(owned[:], per_tile(owner), per_expert(expert_no), ALU.is_equal))
            link(dve.scalar_tensor_tensor(base[:], begin[:], -float(P), base[:], ALU.mult, ALU.add))
            link(dve.tensor_tensor(owned[:], owned[:], per_expert(base), ALU.mult))
            link(dve.tensor_reduce(offset[:], owned[:], AX.X, ALU.add))
            link(dve.tensor_scalar(used[:], owner[:], float(NE), None, ALU.is_lt))
            link(dve.tensor_scalar(row_f[:], tile_no[:], float(P), float(-NOWHERE), ALU.mult, ALU.add))
            link(dve.tensor_tensor(row_f[:], row_f[:], used[:], ALU.mult))
            link(dve.scalar_tensor_tensor(row_of[:], row_f[:], float(NOWHERE), offset[:], ALU.add, ALU.add))
            dve.tensor_scalar(expert_of[:], owner[:], float(NE - 1), None, ALU.min).then_inc(made_d, 1)
            made[0] += 1
            assert made[0] == DVE_MADE, made[0]
            dve.wait_ge(made_d, DVE_MADE)
            dve.wait_ge(b_ready, 16)

            def h_t(t):
                for half in range(2):
                    dve.wait_ge(hT_mm, 2 * t + half + 1)
                    c0, c1 = ((0, 4), (4, 6))[half]
                    dve.tensor_copy(hT[:, c0:c1, :], ps_hT[:, c0 * P:c1 * P].rearrange("p (c s) -> p c s", s=P)).then_inc(hT_ev, 1)

            def finish(t, k, kx):
                e = dve.value_load(expert_of[0:1, bass.ds(t, 1)], min_val=0, max_val=NE - 1)
                dve.wait_ge(y_mm, t + 1)
                dve.tensor_tensor(y[k][:], ps_y[:, k * 256:k * 256 + D],
                                  out_b[:, bass.ds(e, 1), :].rearrange("p o n -> p (o n)"), ALU.add).then_inc(y_done, 1)
                dve.wait_ge(y_done, 3 * t + 1)
                if not isinstance(t, int) or t >= 2:
                    dve.wait_ge(added, 16 * t - 16)
                dve.tensor_scalar(yw[k][:], y[k][:], x[kx][:, D:D + 1], None, ALU.mult).then_inc(y_done, 1)
                dve.tensor_copy(token[k][:], x[kx][:, D + 1:D + 2]).then_inc(y_done, 1)

            for t in range(4):
                h_t(t)
                finish(t, t % 2, t % 4)
            with dve.Fori(1, TILES // 4) as r:
                for k in range(4):
                    t = 4 * r + k
                    h_t(t)
                    finish(t, k % 2, k)
            for t in range(TILES // 4 * 4, TILES):
                h_t(t)
                finish(t, t % 2, t % 4)

        @block.tensor
        def _(pe):
            pe.wait_ge(made_d, DVE_MADE)

            def turn_x(t, k, kx):
                pe.wait_ge(x_in[kx], 16 * (t // RING) + 16 if isinstance(t, int) else 4 * (t - kx) + 16)
                for c in range(2):
                    mm = pe.transpose(ps_xT[0:DC, (2 * k + c) * P:(2 * k + c + 1) * P], x[kx][:, c * DC:(c + 1) * DC], ident[:])
                mm.then_inc(xT_mm, 1)

            def up(t, k):
                e = pe.value_load(expert_of[0:1, bass.ds(t, 1)], min_val=0, max_val=NE - 1)
                pe.wait_ge(xT_ev, t + 1)
                for c0, c1 in ((0, 512), (512, F)):
                    for c in range(2):
                        rows_ = DC + c
                        mm = pe.matmul(ps_h[k][:, c0:c1], xT[k][0:rows_, c, :],
                                       w_in[0:rows_, bass.ds(e, 1), c, c0:c1].rearrange("p o f -> p (o f)"),
                                       start=c == 0, stop=c == 1)
                mm.then_inc(h_mm, 1)

            def turn_h(t, k):
                for half, (c0, c1) in enumerate(((0, 4), (4, 6))):
                    if half == 0:
                        pe.wait_ge(gelu_done, t + 1)
                    for c in range(c0, c1):
                        mm = pe.transpose(ps_hT[:, c * P:(c + 1) * P], h[k][:, c * P:(c + 1) * P], ident[:])
                    mm.then_inc(hT_mm, 1)

            def down(t, k):
                e = pe.value_load(expert_of[0:1, bass.ds(t, 1)], min_val=0, max_val=NE - 1)
                for c in range(FC):
                    if c in (0, 4):
                        pe.wait_ge(hT_ev, 2 * t + (1 if c == 0 else 2))
                    mm = pe.matmul(ps_y[:, k * 256:k * 256 + D], hT[:, c, :],
                                   w_out[:, bass.ds(e, 1), c, :].rearrange("p o n -> p (o n)"),
                                   start=c == 0, stop=c == FC - 1)
                mm.then_inc(y_mm, 1)

            turn_x(0, 0, 0)
            pe.wait_ge(xT_ev, 1)
            turn_x(1, 1, 1)
            pe.wait_ge(w_ready, 16 * 3 * NE)
            up(0, 0)

            def turn(t, k, kx):
                up(t, (k + 1) % 2)
                turn_h(t - 1, k)
                turn_x(t + 1, k, kx)
                down(t - 1, k)

            for t in (1, 2, 3, 4):
                turn(t, (t - 1) % 2, (t + 1) % 4)
            with pe.Fori(0, (TILES - 3 - 4) // 4) as r:
                for k in range(4):
                    turn(4 * r + 5 + k, k % 2, (6 + k) % 4)
            for t in range(5 + (TILES - 3 - 4) // 4 * 4, TILES - 1):
                turn(t, (t - 1) % 2, (t + 1) % 4)
            up(TILES - 1, (TILES - 1) % 2)
            turn_h(TILES - 2, (TILES - 2) % 2)
            down(TILES - 2, (TILES - 2) % 2)
            turn_h(TILES - 1, (TILES - 1) % 2)
            down(TILES - 1, (TILES - 1) % 2)


def tower(nc, dram):
    with nc.sbuf_tensor("route", [P, NE], f32) as route:
        attention_block(nc, dram, route)
        expert_block(nc, dram, route)


def kernel(x, mask_BS_i1_0, fside_BSS_graph, L0_tok_tok_emb, L0_tok_seg_emb, L0_tok_pos_emb, L0_tok_dense_w,
           L0_tok_dense_b, L0_tok_ln_gamma, L0_tok_ln_beta, L0_attn_Wq, L0_attn_bq, L0_attn_Wk, L0_attn_bk,
           L0_attn_Wv, L0_attn_bv, L0_attn_Wo, L0_attn_bo, L0_ffn_Wr, L0_ffn_Wi, L0_ffn_bi, L0_ffn_Wo, L0_ffn_bo):
    import numpy as np
    import concourse.bacc as bacc
    from concourse import mybir as mb
    from concourse.bass_utils import run_bass_kernel_spmd

    def turned(a, *axes):
        return np.ascontiguousarray(np.transpose(np.asarray(a), axes))

    def as_is(a):
        return np.ascontiguousarray(np.asarray(a))

    arrays = {
        "ids": turned(x, 1, 0), "mask": turned(mask_BS_i1_0, 1, 0), "graphT": turned(fside_BSS_graph, 0, 2, 1),
        "tok_emb": as_is(L0_tok_tok_emb), "seg_emb": as_is(L0_tok_seg_emb), "pos_emb": as_is(L0_tok_pos_emb),
        "dense_w": as_is(L0_tok_dense_w), "dense_b": as_is(L0_tok_dense_b), "ln_gamma": as_is(L0_tok_ln_gamma),
        "ln_beta": as_is(L0_tok_ln_beta), "wq": as_is(L0_attn_Wq), "bq": as_is(L0_attn_bq), "wk": as_is(L0_attn_Wk),
        "bk": as_is(L0_attn_bk), "wv": as_is(L0_attn_Wv), "bv": as_is(L0_attn_bv), "wo": as_is(L0_attn_Wo),
        "attn_bo": as_is(L0_attn_bo), "router": turned(L0_ffn_Wr, 1, 0), "wi": turned(L0_ffn_Wi, 0, 2, 1),
        "bi": as_is(L0_ffn_bi), "wout": turned(L0_ffn_Wo, 0, 2, 1), "bo": as_is(L0_ffn_bo),
    }
    nc = bacc.Bacc("TRN2", target_bir_lowering=False, num_devices=1)
    dram = {n: nc.dram_tensor(f"in_{n}", a.shape, mb.dt.from_np(a.dtype), kind="ExternalInput").ap()
            for n, a in arrays.items()}
    dram["out"] = nc.dram_tensor("out_rows", (T, D), f32, kind="ExternalOutput").ap()
    dram["shear"] = nc.dram_tensor("shear", (P * PITCH + HALF,), f32, kind="Internal").ap()
    dram["rows"] = nc.dram_tensor("rows", (NOWHERE + P, ROW), f32, kind="Internal").ap()
    tower(nc, dram)
    r = run_bass_kernel_spmd(nc, [{f"in_{n}": a for n, a in arrays.items()}], core_ids=[0])
    return r.results[0]["out_rows"].reshape(B, S, D)
```

```python
import concourse.bass as bass
from concourse import mybir
from contextlib import ExitStack

f32 = mybir.dt.float32
f32r = mybir.dt.float32r
bf16 = mybir.dt.bfloat16
i32 = mybir.dt.int32
u32 = mybir.dt.uint32
ALU = mybir.AluOpType
ACT = mybir.ActivationFunctionType
AX = mybir.AxisListType

P = 128
B, S, D = 32, 128, 192
DC = D // 2
NH, HD = 12, 64
A = NH * HD
HALF = 32
BAND = 2 * HALF + 1
G = 4
NG = B // G
SLOT = HALF + S
PITCH = NH * SLOT
HEAD_PAIRS = ((0, 4), (4, 6))
NE, F = 8, 768
FC = F // P
T = B * S
REGION = T + P
ROW = D + 2
NOWHERE = NE * REGION
TILES = (2 * T + NE * (P - 1)) // P
NO_TOKEN = 2 * T
CONSTANTS = 23
KC = 5


def wait_apart(eng, passed, sem, value):
    if not isinstance(value, int):
        value = eng.to_reg(value)
        eng.wait_ge(passed, 1)
    if not isinstance(value, int) or value > 0:
        eng.wait_ge(sem, value)


def exists(m):
    return not isinstance(m, int) or 0 <= m < B


def wait_count(eng, sem, value):
    if not isinstance(value, int) or value > 0:
        eng.wait_ge(sem, value)


def attention_block(nc, dram, route):
    x_ids, mask, graphT = dram["ids"], dram["mask"], dram["graphT"]
    out, shear, rows = dram["out"], dram["shear"], dram["rows"]
    ctx = ExitStack()
    with ctx:
        def sb(name, shape, dt=f32):
            return ctx.enter_context(nc.sbuf_tensor(name, shape, dt))

        def sem(name):
            return ctx.enter_context(nc.semaphore(name))

        w_split = {m: sb(f"w{m}_split", [P, KC, A], f32r) for m in "qkv"}
        w_o = sb("w_o", [P, A // P, D])
        w_dense = sb("w_dense", [DC, 2, D])
        w_router = sb("w_router", [DC, 2, NE])
        bias_row = {m: sb(f"bias_{m}", [P, A]) for m in "qkv"}
        bias_hi = sb("bias_hi", [P, 3, A], f32r)
        seg0_pos = sb("seg0_pos", [P, D])
        seg_diff = sb("seg_diff", [P, D])
        seg0 = sb("seg0", [P, D])
        dense_b = sb("dense_b", [P, D])
        gamma = sb("gamma", [P, D])
        beta = sb("beta", [P, D])
        attn_bo = sb("attn_bo", [P, D])
        ident = sb("ident", [P, P])
        before = sb("before", [P, P], bf16)
        ones_bf = sb("ones_bf", [P, P], bf16)
        expert_i = sb("expert_i", [P, NE], i32)
        token_i = sb("token_i", [P, B], i32)
        expert_no = sb("expert_no", [P, NE])
        token_no = sb("token_no", [P, B])
        minus_half = sb("minus_half", [P, 1])
        ids = sb("ids", [P, B + G], i32)
        seg_i = sb("seg_i", [P, B + G], i32)
        seg_f = sb("seg_f", [P, B + G])
        ids4 = sb("ids4", [P, G], i32)
        seg4 = sb("seg4", [P, G])
        tok = [sb(f"tok{k}", [P, D]) for k in range(G)]
        graph = [sb(f"graph{k}", [P, S]) for k in range(G)]
        seg_part = sb("seg_part", [P, D])
        seg_part2 = sb("seg_part2", [P, D])
        emb = [sb(f"emb{k}", [P, D]) for k in range(2)]
        emb_b = [sb(f"emb_b{k}", [P, D]) for k in range(2)]
        aggT = sb("aggT", [DC, 2, S])
        h0 = sb("h0", [P, D])
        h_stats = sb("h_stats", [P, 6])
        h_mv = sb("h_mv", [P, 2])
        h_ve = sb("h_ve", [P, 1])
        h_rstd = sb("h_rstd", [P, 1])
        hn = sb("hn", [P, D])
        hg = sb("hg", [P, D])
        h1 = [sb(f"h1_{k}", [P, D]) for k in range(2)]
        stats1 = sb("stats1", [P, 6])
        mv1 = sb("mv1", [P, 2])
        ve1 = sb("ve1", [P, 1])
        rstd1 = sb("rstd1", [P, 1])
        x_full = sb("x_full", [P, D])
        x_cat = [sb(f"x_cat{k}", [P, 4, P]) for k in range(2)]
        h_res = sb("h_res", [P, B, D])
        xT = sb("xT", [P, 4, G * S], f32r)
        qT = sb("qT", [P, A // P, G * S])
        kT = sb("kT", [P, A // P, G * S])
        v = sb("v", [P, G, A])
        score = [sb(f"score{k}", [P, NH, S]) for k in range(2)]
        prob = [sb(f"prob{k}", [P, NH, S]) for k in range(2)]
        band_max = sb("band_max", [P, NH])
        band_max0 = sb("band_max0", [P, NH])
        e_zero = sb("e_zero", [P, NH])
        band_sum = sb("band_sum", [P, NH])
        denom = sb("denom", [P, NH])
        r_denom = sb("r_denom", [P, NH])
        p_zero = sb("p_zero", [P, NH])
        probT = sb("probT", [P, NH, S])
        oT = sb("oT", [P, A // P, S])
        h2 = [sb(f"h2_{k}", [P, D]) for k in range(2)]
        stats2 = sb("stats2", [P, 6])
        mv2 = sb("mv2", [P, 2])
        ve2 = sb("ve2", [P, 1])
        rstd2 = sb("rstd2", [P, 1])
        row_a = [sb(f"row_a{k}", [P, ROW]) for k in range(2)]
        row_b = [sb(f"row_b{k}", [P, ROW]) for k in range(2)]
        x2T = sb("x2T", [DC, 2, S])
        logits = sb("logits", [P, NE])
        top = sb("top", [P, 8])
        top_i = sb("top_i", [P, 8], u32)
        top_f = sb("top_f", [P, 2])
        is_1 = sb("is_1", [P, NE])
        is_2 = sb("is_2", [P, NE])
        is_any = sb("is_any", [P, NE], bf16)
        gap = sb("gap", [P, 1])
        e_gap = sb("e_gap", [P, 1])
        one_e = sb("one_e", [P, 1])
        where = sb("where", [P, NE])
        pick1 = sb("pick1", [P, NE])
        pick2 = sb("pick2", [P, NE])
        pos_f = sb("pos_f", [P, 2])
        pos = [sb(f"pos{k}", [P, 2], i32) for k in range(2)]

        ps_s = ctx.enter_context(nc.psum_tensor("ps_s", [P, 1024], f32))
        ps_probT = [ctx.enter_context(nc.psum_tensor(f"ps_probT{i}", [P, 512], f32)) for i in range(2)]
        ps_o = ctx.enter_context(nc.psum_tensor("ps_o", [P, 1024], f32))
        ps_a = ctx.enter_context(nc.psum_tensor("ps_a", [P, 512], f32))
        ps_x = ctx.enter_context(nc.psum_tensor("ps_x", [P, 512], f32))
        ps_score = ps_s[:].rearrange("p (o i s) -> p o i s", o=2, s=S)
        ps_qk = [ps_s[:, 0:512], ps_s[:, 512:1024]]
        ps_oT = ps_o[:, 0:A].rearrange("p (c s) -> p c s", s=S)
        ps_attn = ps_o[:, A:A + D]
        ps_logits = ps_x[:, 0:NE]
        ps_rank = ps_x[:, 16:16 + NE]
        ps_total = ps_x[:, 32:32 + NE]
        ps_agg = ps_a[0:DC, 0:2 * S].rearrange("p (c s) -> p c s", s=S)
        ps_x2T = ps_agg
        ps_proj = ps_a[:, 2 * S:2 * S + D]
        ps_v = [ps_a, ps_x]

        const_in = sem("const_in")
        ids_in = sem("ids_in")
        w_in = {m: sem(f"w{m}_in") for m in "qkv"}
        pad_zero = sem("pad_zero")
        setup_pool = sem("setup_pool")
        setup_dve = sem("setup_dve")
        w_hi = sem("w_hi")
        w_lo = sem("w_lo")
        graph_in = [sem(f"graph_in{k}") for k in range(G)]
        tok_in = [sem(f"tok_in{k}") for k in range(G)]
        staged = sem("staged")
        emb_done = sem("emb_done")
        agg_mm = sem("agg_mm")
        agg_ev = sem("agg_ev")
        proj_mm = sem("proj_mm")
        h0_done = sem("h0_done")
        h0_rstd = sem("h0_rstd")
        hn_done = sem("hn_done")
        h1_done = sem("h1_done")
        h1_stat = sem("h1_stat")
        h1_rstd = sem("h1_rstd")
        x_done = sem("x_done")
        x_lo = sem("x_lo")
        xt_mm = sem("xt_mm")
        xt_ev = sem("xt_ev")
        qk_mm = [sem("qk_mm_even"), sem("qk_mm_odd")]
        qk_ev = [sem("qk_ev_even"), sem("qk_ev_odd")]
        v_mm = [sem("v_mm_low"), sem("v_mm_high")]
        v_ev = [sem("v_ev_low"), sem("v_ev_high")]
        score_mm = sem("score_mm")
        score_ev = sem("score_ev")
        shear_out = sem("shear_out")
        band_in = sem("band_in")
        max_done = sem("max_done")
        sub_done = sem("sub_done")
        exp_done = sem("exp_done")
        norm_done = sem("norm_done")
        fill_done = sem("fill_done")
        probT_mm = sem("probT_mm")
        probT_ev = sem("probT_ev")
        probT2_ev = sem("probT2_ev")
        oT_mm = sem("oT_mm")
        oT_ev = sem("oT_ev")
        rowb_x = sem("rowb_x")
        attn_mm = sem("attn_mm")
        h2_done = sem("h2_done")
        h2_rstd = sem("h2_rstd")
        x2_done = sem("x2_done")
        x2T_mm = sem("x2T_mm")
        x2T_ev = sem("x2T_ev")
        logit_mm = sem("logit_mm")
        choice = sem("choice")
        e_gap_done = sem("e_gap_done")
        rank_mm = sem("rank_mm")
        placed = sem("placed")
        rank_free = sem("rank_free")
        row_done = sem("row_done")
        out_free = [sem(f"out_free{k}") for k in range(2)]
        rowa_free = [sem(f"rowa_free{k}") for k in range(2)]
        rowb_free = [sem(f"rowb_free{k}") for k in range(2)]
        block = ctx.enter_context(nc.Block())

        def bcast(row):
            return bass.AP(row.tensor, row.offset, [[0, P]] + list(row.ap))

        def all_heads(stat, w=BAND):
            return stat[:].unsqueeze(2).broadcast_to([P, NH, w])

        @block.sync
        def _(sp):
            sp.dma_start(ids[:, 0:B], x_ids).then_inc(ids_in, 16)
            sp.dma_start(seg_i[:, 0:B], mask).then_inc(ids_in, 16)
            sp.dma_start(seg0_pos[:], dram["pos_emb"]).then_inc(const_in, 16)
            sp.dma_start(seg0[:], bcast(dram["seg_emb"][0])).then_inc(const_in, 16)
            sp.dma_start(seg_diff[:], bcast(dram["seg_emb"][1])).then_inc(const_in, 16)
            sp.dma_start(dense_b[:], bcast(dram["dense_b"])).then_inc(const_in, 16)

            def load_graph(n, k):
                sp.dma_start(graph[k][:], graphT[n]).then_inc(graph_in[k], 16)

            for k in range(G):
                load_graph(k, k)
            sp.dma_start(w_dense[:], dram["dense_w"].rearrange("(c p) e -> p c e", p=DC)).then_inc(const_in, 16)
            sp.dma_start(gamma[:], bcast(dram["ln_gamma"])).then_inc(const_in, 16)
            sp.dma_start(beta[:], bcast(dram["ln_beta"])).then_inc(const_in, 16)
            sp.dma_start(attn_bo[:], bcast(dram["attn_bo"])).then_inc(const_in, 16)
            sp.dma_start(w_router[:], dram["router"].rearrange("(c p) e -> p c e", p=DC)).then_inc(const_in, 16)
            sp.dma_start(w_o[:], dram["wo"].rearrange("(c p) e -> p c e", p=P)).then_inc(const_in, 16)
            sp.wait_ge(setup_pool, 1)
            sp.dma_start(shear[0:P * PITCH].rearrange("(n h m) -> n h m", h=NH, m=SLOT)[:, :, 0:HALF],
                         prob[0][:, :, 0:HALF]).then_inc(pad_zero, 16)
            sp.dma_start(shear[P * PITCH:P * PITCH + HALF].rearrange("(o m) -> o m", o=1),
                         prob[0][0:1, 0, 0:HALF]).then_inc(pad_zero, 16)
            sp.wait_ge(pad_zero, 32)

            def store_h2(m, k):
                wait_apart(sp, setup_pool, h2_done, 3 * m + 1)
                sp.dma_start(out[bass.ds(m * S, S), :], h2[k % 2][:]).then_inc(out_free[k % 2], 16)

            def shift(c, k):
                wait_apart(sp, setup_pool, score_ev, 2 * c + 2)
                sp.dma_start(shear[0:P * PITCH].rearrange("(n h m) -> n h m", h=NH, m=SLOT)[:, :, HALF:SLOT],
                             score[k % 2][:]).then_inc(shear_out, 16)
                wait_apart(sp, setup_pool, shear_out, 16 * c + 16)
                wait_apart(sp, setup_pool, probT_mm, 3 * c - 3)
                sp.dma_start(prob[k % 2][:, :, 0:BAND],
                             bass.AP(shear.tensor, 0, [[PITCH + 1, P], [SLOT, NH], [1, BAND]])).then_inc(band_in, 16)

            def group(g):
                n = 4 * g
                if exists(n + 4):
                    for k in range(G):
                        wait_apart(sp, setup_pool, agg_mm, n + k + 1)
                        load_graph(n + 4 + k, k)
                for k in range(G):
                    c = n + k
                    if exists(c - 3):
                        store_h2(c - 3, (k + 1) % G)
                    if exists(c - 1):
                        wait_apart(sp, setup_pool, band_in, 16 * c)
                    if exists(c):
                        shift(c, k)

            group(0)
            with sp.Fori(1, NG - 1) as g:
                group(g)
            group(NG - 1)
            group(NG)
            for k in range(2):
                sp.wait_ge(out_free[k], 16 * (B // 2 + 1))

        @block.gpsimd
        def _(pool):
            setup = [0]

            def made(ins):
                setup[0] += 1
                ins.then_inc(setup_pool, 1)
                pool.wait_ge(setup_pool, setup[0])

            made(pool.memset(prob[0][:], 0.0))
            made(pool.memset(ids[:, B:B + G], 0))
            pool.wait_ge(ids_in, 32)
            pool.tensor_copy(ids4[:], ids[:, 0:G]).then_inc(staged, 1)
            pool.wait_ge(staged, 1)

            def gather(k):
                pool.indirect_dma_start(tok[k][:], None, dram["tok_emb"],
                                        bass.IndirectOffsetOnAxis(ap=ids4[:, k:k + 1], axis=0)).then_inc(tok_in[k], 16)

            for k in range(G):
                gather(k)
            made(pool.memset(seg_i[:, B:B + G], 0))
            made(pool.tensor_copy(seg_f[:], seg_i[:]))
            pool.tensor_copy(seg4[:], seg_f[:, 0:G]).then_inc(staged, 1)
            made(pool.memset(minus_half[:], -0.5))
            made(pool.memset(ident[:], 0.0))
            made(pool.affine_select(out=ident[:], in_=ident[:], compare_op=ALU.not_equal, fill=1.0, base=0,
                                    pattern=[[-1, P]], channel_multiplier=1))
            for k in range(2):
                made(pool.memset(x_cat[k][:, 3, :], 0.0))
                made(pool.memset(x_cat[k][:, 3, 64:65], 1.0))
                made(pool.memset(x_cat[k][:, 3, 96:97], 1.0))
            made(pool.iota(expert_i[:], pattern=[[1, NE]], base=0, channel_multiplier=0))
            made(pool.tensor_copy(expert_no[:], expert_i[:]))
            made(pool.iota(token_i[:], pattern=[[S, B]], base=0, channel_multiplier=1))
            made(pool.tensor_copy(token_no[:], token_i[:]))
            made(pool.tensor_scalar(route[:], expert_no[:], float(REGION), None, ALU.mult))
            made(pool.memset(ones_bf[:], 1.0))
            made(pool.memset(before[:], 1.0))
            made(pool.affine_select(out=before[:], in_=before[:], compare_op=ALU.is_ge, fill=0.0, base=-1,
                                    pattern=[[1, P]], channel_multiplier=-1))
            pool.wait_ge(const_in, 16 * 10)
            made(pool.tensor_tensor(seg0_pos[:], seg0_pos[:], seg0[:], ALU.add))
            made(pool.tensor_tensor(seg_diff[:], seg_diff[:], seg0[:], ALU.subtract))
            assert setup[0] == CONSTANTS
            for i, free in enumerate(rowa_free + rowb_free):
                pool.dma_start(rows[NOWHERE + i:NOWHERE + i + 1, 0:P], ident[0:1, :]).then_inc(free, 16)

            def embed(a, k):
                wait_apart(pool, setup_pool, agg_mm, a - 1)
                wait_apart(pool, setup_pool, h0_done, 3 * a - 5)
                pool.tensor_scalar(seg_part[:], seg_diff[:], seg4[:, k:k + 1], None, ALU.mult).then_inc(emb_done, 1)
                wait_apart(pool, setup_pool, emb_done, 4 * a + 1)
                pool.tensor_tensor(seg_part2[:], seg_part[:], seg0_pos[:], ALU.add).then_inc(emb_done, 1)
                wait_apart(pool, setup_pool, emb_done, 4 * a + 2)
                wait_apart(pool, setup_pool, tok_in[k], 4 * (a - k) + 16)
                pool.tensor_tensor(emb[k % 2][:], tok[k][:], seg_part2[:], ALU.add).then_inc(emb_done, 1)
                wait_apart(pool, setup_pool, emb_done, 4 * a + 3)
                pool.tensor_tensor(emb_b[k % 2][:], emb[k % 2][:], dense_b[:], ALU.add).then_inc(emb_done, 1)

            def rstd(var_sem, value, mv, ve, out_, eps, done, n):
                wait_apart(pool, setup_pool, var_sem, value)
                pool.tensor_scalar(ve[:], mv[:, 1:2], eps, None, ALU.add).then_inc(done, 1)
                wait_apart(pool, setup_pool, done, 2 * n + 1)
                pool.tensor_tensor(out_[:], ve[:], minus_half[:], ALU.pow).then_inc(done, 1)

            def rstd0(a):
                rstd(h0_done, 3 * a + 3, h_mv, h_ve, h_rstd, 1e-12, h0_rstd, a)

            def affine(a, k):
                wait_apart(pool, setup_pool, hn_done, a + 1)
                pool.tensor_tensor(hg[:], hn[:], gamma[:], ALU.mult).then_inc(h1_done, 1)
                wait_apart(pool, setup_pool, h1_done, 3 * a + 1)
                pool.tensor_tensor(h1[k % 2][:], hg[:], beta[:], ALU.add).then_inc(h1_done, 1)

            def keep(a, k):
                wait_apart(pool, setup_pool, h1_done, 3 * a + 2)
                pool.tensor_tensor(h_res[:, bass.ds(a, 1), :].rearrange("p o d -> p (o d)"), h1[k % 2][:],
                                   attn_bo[:], ALU.add).then_inc(h1_done, 1)

            def rstd1_(a):
                rstd(h1_stat, 2 * a + 2, mv1, ve1, rstd1, 1e-5, h1_rstd, a)

            def low_part(a, k):
                wait_apart(pool, setup_pool, x_done, 3 * a + 3)
                flat = x_cat[k % 2][:].rearrange("p c s -> p (c s)")
                pool.tensor_tensor(flat[:, D:2 * D], x_full[:], flat[:, 0:D], ALU.subtract).then_inc(x_lo, 1)

            def stage_seg(g):
                pool.tensor_copy(seg4[:], seg_f[:, bass.ds(4 * g + 4, G)]).then_inc(staged, 1)
                wait_apart(pool, setup_pool, staged, 2 * g + 4)

            def stage_ids(g):
                pool.tensor_copy(ids4[:], ids[:, bass.ds(4 * g + 8, G)]).then_inc(staged, 1)
                wait_apart(pool, setup_pool, staged, 2 * g + 5)

            def subtract_max(n, k):
                wait_apart(pool, setup_pool, max_done, 2 * n + 2)
                band = prob[k % 2][:, :, 0:BAND]
                pool.tensor_tensor(band, band, all_heads(band_max0), ALU.subtract).then_inc(sub_done, 1)

            def rstd2_(n):
                rstd(h2_done, 3 * n + 3, mv2, ve2, rstd2, 1e-5, h2_rstd, n)

            def scatter(n, k):
                wait_apart(pool, setup_pool, placed, 9 * n + 9)
                pool.tensor_copy(row_a[k % 2][:, D + 1:D + 2], token_no[:, bass.ds(n, 1)]).then_inc(row_done, 1)
                wait_apart(pool, setup_pool, rowb_x, n + 1)
                pool.tensor_copy(row_b[k % 2][:, D + 1:D + 2], token_no[:, bass.ds(n, 1)]).then_inc(row_done, 1)
                wait_apart(pool, setup_pool, row_done, 2 * n + 2)
                for row, free, c in ((row_a, rowa_free, 0), (row_b, rowb_free, 1)):
                    pool.indirect_dma_start(rows, bass.IndirectOffsetOnAxis(ap=pos[k % 2][:, c:c + 1], axis=0),
                                            row[k % 2][:], None).then_inc(free[k % 2], 16)

            pool.wait_ge(staged, 2)
            for k in range(G):
                embed(k, k)
                rstd0(k)
                affine(k, k)
                rstd1_(k)
                low_part(k, k)
                keep(k, k)
            pool.wait_ge(emb_done, 4 * G)
            pool.tensor_copy(ids4[:], ids[:, G:2 * G]).then_inc(staged, 1)
            pool.wait_ge(staged, 3)
            for k in range(G):
                gather(k)

            def group(g):
                n = 4 * g
                a = n + 4
                more = exists(a)
                if more:
                    stage_seg(g)
                for k in range(G):
                    c = n + k
                    if exists(c - 1):
                        subtract_max(c - 1, (k + 3) % G)
                    if more and k == 0:
                        embed(a, 0)
                    if exists(c - 4):
                        scatter(c - 4, k)
                    if more and k < 2:
                        embed(a + k + 1, k + 1)
                    if more and k < 3:
                        first = (0, 1, 3)[k]
                        rstd0(a + first)
                        affine(a + first, first)
                    if exists(c - 2):
                        rstd2_(c - 2)
                    if more and k < 3:
                        rstd1_(a + first)
                        keep(a + first, first)
                        low_part(a + first, first)
                    if more and k == 1:
                        rstd0(a + 2)
                        affine(a + 2, 2)
                        rstd1_(a + 2)
                        embed(a + 3, 3)
                        keep(a + 2, 2)
                        low_part(a + 2, 2)
                    if more and k == 2:
                        stage_ids(g)
                        for j in range(G):
                            gather(j)

            group(0)
            with pool.Fori(1, NG - 1) as g:
                group(g)
            group(NG - 1)
            group(NG)
            for k in range(G):
                pool.wait_ge(tok_in[k], 16 * (NG + 1))
            for k in range(2):
                pool.wait_ge(rowa_free[k], 16 * (B // 2 + 1))
                pool.wait_ge(rowb_free[k], 16 * (B // 2 + 1))

        @block.scalar
        def _(act):
            for m, raw in (("q", qT), ("k", kT), ("v", v)):
                w, flat = dram["w" + m], raw[:].rearrange("p a b -> p (a b)")
                act.dma_start(flat[:, 0:A], w[0:P]).then_inc(w_in[m], 16)
                act.dma_start(flat[0:64, A:2 * A], w[P:D]).then_inc(w_in[m], 16)
                act.dma_start(flat[64:P, A:2 * A], w[0:64]).then_inc(w_in[m], 16)
                act.dma_start(flat[:, 2 * A:3 * A], w[64:D]).then_inc(w_in[m], 16)
                for p in (64, 96):
                    act.dma_start(bias_row[m][p:p + 1, :], dram["b" + m].rearrange("(o n) -> o n", o=1)).then_inc(w_in[m], 16)

            def agg(a):
                act.wait_ge(agg_mm, a + 1)
                if not isinstance(a, int) or a:
                    act.wait_ge(proj_mm, a)
                act.activation(aggT[:], ps_agg, ACT.Copy).then_inc(agg_ev, 1)

            def x_t(a, k):
                act.wait_ge(xt_mm, a + 1)
                act.activation(xT[:, :, k * S:(k + 1) * S], ps_x[:].rearrange("p (c s) -> p c s", s=S),
                               ACT.Copy).then_inc(xt_ev, 1)

            def high(m, raw):
                act.wait_ge(w_in[m], 16 * 6)
                act.activation(w_split[m][:, 0:3, :].rearrange("p c n -> p (c n)"),
                               raw[:].rearrange("p a b -> p (a b)")[:, 0:3 * A], ACT.Copy).then_inc(w_hi, 1)
                i = "qkv".index(m)
                for p in (64, 96):
                    act.activation(bias_hi[p:p + 1, i, :], bias_row[m][p:p + 1, :], ACT.Copy).then_inc(w_hi, 1)

            def qk(g, t):
                act.wait_ge(qk_mm[0], 6 * g + t + 1)
                j = 2 * t
                dst = (qT if j < 6 else kT)[:, j % 6, :]
                act.activation(dst, ps_qk[0], ACT.Copy).then_inc(qk_ev[0], 1)

            def v_low(n, k):
                act.wait_ge(v_mm[0], n + 1)
                act.activation(v[:, k, 0:A // 2], ps_v[0][:, 0:A // 2], ACT.Copy).then_inc(v_ev[0], 1)

            def scores(n, k, units=(0, 1)):
                if 0 in units:
                    wait_count(act, shear_out, 16 * n - 16)
                by_bank = score[k % 2][:].rearrange("p (i o) s -> p o i s", o=2)
                for u in units:
                    i0, i1 = HEAD_PAIRS[u]
                    act.wait_ge(score_mm, 2 * n + u + 1)
                    act.activation(by_bank[:, :, i0:i1, :], ps_score[:, :, 0:i1 - i0, :], ACT.Copy).then_inc(score_ev, 1)

            def exps(n, k):
                act.wait_ge(sub_done, n + 1)
                band = prob[k % 2][:, :, 0:BAND]
                act.activation(band, band, ACT.Exp).then_inc(exp_done, 1)
                act.activation(e_zero[:], band_max0[:], ACT.Exp, scale=-1.0).then_inc(exp_done, 1)

            def prob_t2(n, k):
                act.wait_ge(probT_mm, 3 * n + 3)
                act.activation(probT[:, 8:12, :], ps_probT[(3 * k + 2) % 2][:].rearrange("p (h s) -> p h s", s=S),
                               ACT.Copy).then_inc(probT2_ev, 1)

            def fill(n, k):
                act.wait_ge(norm_done, 5 * n + 4)
                act.activation(prob[k % 2][:, :, BAND:S], all_heads(p_zero, S - BAND), ACT.Copy).then_inc(fill_done, 1)

            def copy_row(n, k):
                act.wait_ge(x2_done, n + 1)
                act.wait_ge(rowb_free[k % 2], 8 * (n - k) + 16 * (k // 2) + 16)
                act.activation(row_b[k % 2][:, 0:D], row_a[k % 2][:, 0:D], ACT.Copy).then_inc(rowb_x, 1)

            def o_t(n, half):
                act.wait_ge(oT_mm, 2 * n + half + 1)
                c0, c1 = ((0, 4), (4, 6))[half]
                act.activation(oT[:, c0:c1, :], ps_oT[:, c0:c1, :], ACT.Copy).then_inc(oT_ev, 1)

            def x2_t(n):
                act.wait_ge(x2T_mm, n + 1)
                act.activation(x2T[:], ps_x2T, ACT.Copy).then_inc(x2T_ev, 1)

            def exp_gap(n):
                act.wait_ge(choice, 8 * n + 8)
                act.activation(e_gap[:], gap[:], ACT.Exp).then_inc(e_gap_done, 1)

            agg(0)
            high("q", qT)
            agg(1)
            x_t(0, 0)
            high("k", kT)
            agg(2)
            x_t(1, 1)
            agg(3)
            high("v", v)
            x_t(2, 2)
            x_t(3, 3)
            for t in range(6):
                qk(0, t)

            def group(g):
                n = 4 * g
                a = n + 4
                more = exists(a)
                for k in range(G):
                    c = n + k
                    k1, k2, k3 = (k + 3) % G, (k + 2) % G, (k + 1) % G
                    if exists(c):
                        scores(c, k, (0,))
                        v_low(c, k)
                    if exists(c - 1):
                        exps(c - 1, k1)
                    if exists(c):
                        scores(c, k, (1,))
                    if more and k < 3:
                        agg(a + (0, 1, 3)[k])
                    if exists(c - 2):
                        prob_t2(c - 2, k2)
                        o_t(c - 2, 0)
                    if more and k >= 2:
                        x_t(a + 2 * k - 3, 2 * k - 3)
                    if exists(c - 2):
                        o_t(c - 2, 1)
                    if more and k in (1, 2):
                        x_t(a + 2 * k - 2, 2 * k - 2)
                    if exists(c - 3):
                        x2_t(c - 3)
                    if more and k == 1:
                        agg(a + 2)
                    if more and k == 3:
                        qk(g + 1, 0)
                    if exists(c - 1):
                        fill(c - 1, k1)
                    if exists(c - 3):
                        copy_row(c - 3, k3)
                    if more and k == 3:
                        for t in range(1, 5):
                            qk(g + 1, t)
                    if exists(c - 3):
                        exp_gap(c - 3)
                    if more and k == 3:
                        qk(g + 1, 5)

            group(0)
            with act.Fori(1, NG - 1) as g:
                group(g)
            group(NG - 1)
            group(NG)

        @block.vector
        def _(dve):
            def residual(a, k):
                dve.wait_ge(proj_mm, a + 1)
                dve.wait_ge(emb_done, 4 * a + 4)
                dve.tensor_tensor(h0[:], ps_proj, emb_b[k % 2][:], ALU.add).then_inc(h0_done, 1)
                dve.wait_ge(h0_done, 3 * a + 1)
                dve.bn_stats(h_stats[:], h0[:]).then_inc(h0_done, 1)
                wait_apart(dve, setup_pool, h0_done, 3 * a + 2)
                dve.bn_aggr(h_mv[:], h_stats[:]).then_inc(h0_done, 1)

            def norm0(a):
                dve.wait_ge(h0_rstd, 2 * a + 2)
                dve.tensor_scalar(hn[:], h0[:], h_mv[:, 0:1], h_rstd[:, 0:1], ALU.subtract, ALU.mult).then_inc(hn_done, 1)

            def stat1(a, k):
                dve.wait_ge(h1_done, 3 * a + 2)
                dve.bn_stats(stats1[:], h1[k % 2][:]).then_inc(h1_stat, 1)
                wait_apart(dve, setup_pool, h1_stat, 2 * a + 1)
                dve.bn_aggr(mv1[:], stats1[:]).then_inc(h1_stat, 1)

            def x_parts(a, k):
                dve.wait_ge(h1_rstd, 2 * a + 2)
                if k >= 2 or not isinstance(a, int):
                    dve.wait_ge(xt_mm, a - 1)
                cat = x_cat[k % 2][:].rearrange("p c s -> p (c s)")
                dve.tensor_scalar(cat[:, 0:D].bitcast(f32r), h1[k % 2][:], mv1[:, 0:1], rstd1[:, 0:1],
                                  ALU.subtract, ALU.mult).then_inc(x_done, 1)
                dve.tensor_scalar(cat[:, 2 * D:2 * D + 64].bitcast(f32r), h1[k % 2][:, P:D], mv1[:, 0:1], rstd1[:, 0:1],
                                  ALU.subtract, ALU.mult).then_inc(x_done, 1)
                dve.tensor_scalar(x_full[:], h1[k % 2][:], mv1[:, 0:1], rstd1[:, 0:1],
                                  ALU.subtract, ALU.mult).then_inc(x_done, 1)

            def low(m, raw):
                i = "qkv".index(m)
                flat = raw[:].rearrange("p a b -> p (a b)")
                dve.wait_ge(w_hi, 3 * i + 3)
                dve.tensor_tensor(w_split[m][:, 3, :], flat[:, 0:A], w_split[m][:, 0, :].bitcast(f32),
                                  ALU.subtract).then_inc(w_lo, 1)
                dve.tensor_tensor(w_split[m][0:64, 4, :], flat[0:64, A:2 * A], w_split[m][0:64, 1, :].bitcast(f32),
                                  ALU.subtract).then_inc(w_lo, 1)
                dve.memset(w_split[m][64:P, 4, :].bitcast(f32), 0.0).then_inc(w_lo, 1)
                dve.wait_ge(w_lo, 5 * i + 3)
                dve.tensor_copy(w_split[m][64:65, 4, :], bias_hi[64:65, i, :].bitcast(f32)).then_inc(w_lo, 1)
                dve.tensor_tensor(w_split[m][96:97, 4, :], bias_row[m][96:97, :], bias_hi[96:97, i, :].bitcast(f32),
                                  ALU.subtract).then_inc(w_lo, 1)

            def qk(g, t):
                dve.wait_ge(qk_mm[1], 6 * g + t + 1)
                j = 2 * t + 1
                dst = (qT if j < 6 else kT)[:, j % 6, :]
                dve.tensor_copy(dst, ps_qk[1]).then_inc(qk_ev[1], 1)

            def v_high(n, k):
                dve.wait_ge(v_mm[1], n + 1)
                dve.tensor_copy(v[:, k, A // 2:A], ps_v[1][:, 0:A // 2]).then_inc(v_ev[1], 1)

            def maximum(n, k):
                dve.wait_ge(band_in, 16 * n + 16)
                dve.tensor_reduce(band_max[:], prob[k % 2][:, :, 0:BAND], AX.X, ALU.max).then_inc(max_done, 1)
                dve.wait_ge(max_done, 2 * n + 1)
                dve.tensor_scalar(band_max0[:], band_max[:], 0.0, None, ALU.max).then_inc(max_done, 1)

            def normalise(n, k):
                dve.wait_ge(exp_done, 2 * n + 2)
                band = prob[k % 2][:, :, 0:BAND]
                dve.tensor_reduce(band_sum[:], band, AX.X, ALU.add).then_inc(norm_done, 1)
                dve.wait_ge(norm_done, 5 * n + 1)
                dve.scalar_tensor_tensor(denom[:], e_zero[:], float(S - BAND), band_sum[:],
                                         ALU.mult, ALU.add).then_inc(norm_done, 1)
                dve.wait_ge(norm_done, 5 * n + 2)
                dve.reciprocal(r_denom[:], denom[:]).then_inc(norm_done, 1)
                dve.wait_ge(norm_done, 5 * n + 3)
                dve.tensor_tensor(p_zero[:], e_zero[:], r_denom[:], ALU.mult).then_inc(norm_done, 1)
                dve.tensor_tensor(band, band, all_heads(r_denom), ALU.mult).then_inc(norm_done, 1)

            def prob_t(n, k, u):
                dve.wait_ge(probT_mm, 3 * n + u + 1)
                dve.tensor_copy(probT[:, 4 * u:4 * u + 4, :],
                                ps_probT[(3 * k + u) % 2][:].rearrange("p (h s) -> p h s", s=S)).then_inc(probT_ev, 1)

            def residual2(n, k):
                dve.wait_ge(attn_mm, n + 1)
                dve.wait_ge(out_free[k % 2], 8 * (n - k) + 16 * (k // 2) + 16)
                dve.tensor_tensor(h2[k % 2][:], ps_attn, h_res[:, bass.ds(n, 1), :].rearrange("p o d -> p (o d)"),
                                  ALU.add).then_inc(h2_done, 1)
                dve.wait_ge(h2_done, 3 * n + 1)
                dve.bn_stats(stats2[:], h2[k % 2][:]).then_inc(h2_done, 1)
                wait_apart(dve, setup_pool, h2_done, 3 * n + 2)
                dve.bn_aggr(mv2[:], stats2[:]).then_inc(h2_done, 1)

            def norm2(n, k):
                dve.wait_ge(h2_rstd, 2 * n + 2)
                dve.wait_ge(rowa_free[k % 2], 8 * (n - k) + 16 * (k // 2) + 16)
                dve.tensor_scalar(row_a[k % 2][:, 0:D], h2[k % 2][:], mv2[:, 0:1], rstd2[:, 0:1],
                                  ALU.subtract, ALU.mult).then_inc(x2_done, 1)

            def choose(n):
                dve.wait_ge(logit_mm, n + 1)
                dve.tensor_copy(logits[:], ps_logits).then_inc(choice, 1)
                wait_apart(dve, setup_pool, choice, 8 * n + 1)
                dve.max(top[:], logits[:]).then_inc(choice, 1)
                wait_apart(dve, setup_pool, choice, 8 * n + 2)
                dve.max_index(top_i[:], top[:], logits[:]).then_inc(choice, 1)
                dve.wait_ge(choice, 8 * n + 3)
                dve.tensor_copy(top_f[:], top_i[:, 0:2]).then_inc(choice, 1)
                dve.wait_ge(choice, 8 * n + 4)
                dve.tensor_scalar(is_1[:], expert_no[:], top_f[:, 0:1], None, ALU.is_equal).then_inc(choice, 1)
                dve.tensor_scalar(is_2[:], expert_no[:], top_f[:, 1:2], None, ALU.is_equal).then_inc(choice, 1)
                dve.wait_ge(choice, 8 * n + 6)
                dve.tensor_tensor(is_any[:], is_1[:], is_2[:], ALU.add).then_inc(choice, 1)
                dve.tensor_tensor(gap[:], top[:, 1:2], top[:, 0:1], ALU.subtract).then_inc(choice, 1)

            def place(n, k):
                dve.wait_ge(rank_mm, n + 1)
                dve.wait_ge(rank_free, n + 1)
                dve.tensor_tensor(where[:], ps_rank, route[:], ALU.add).then_inc(placed, 1)
                dve.tensor_tensor(route[:], ps_total, route[:], ALU.add).then_inc(rank_free, 1)
                dve.wait_ge(placed, 9 * n + 1)
                dve.tensor_tensor(pick1[:], where[:], is_1[:], ALU.mult).then_inc(placed, 1)
                dve.tensor_tensor(pick2[:], where[:], is_2[:], ALU.mult).then_inc(placed, 1)
                dve.wait_ge(placed, 9 * n + 3)
                dve.tensor_reduce(pos_f[:, 0:1], pick1[:], AX.X, ALU.add).then_inc(placed, 1)
                dve.tensor_reduce(pos_f[:, 1:2], pick2[:], AX.X, ALU.add).then_inc(placed, 1)
                dve.wait_ge(placed, 9 * n + 5)
                dve.wait_ge(rowb_free[k % 2], 8 * (n - k) + 16 * (k // 2) + 16)
                dve.tensor_copy(pos[k % 2][:], pos_f[:]).then_inc(placed, 1)
                dve.wait_ge(e_gap_done, n + 1)
                dve.tensor_scalar(one_e[:], e_gap[:], 1.0, None, ALU.add).then_inc(placed, 1)
                dve.wait_ge(placed, 9 * n + 7)
                dve.reciprocal(row_a[k % 2][:, D:D + 1], one_e[:]).then_inc(placed, 1)
                dve.wait_ge(placed, 9 * n + 8)
                dve.tensor_tensor(row_b[k % 2][:, D:D + 1], row_a[k % 2][:, D:D + 1], e_gap[:], ALU.mult).then_inc(placed, 1)

            dve.sem_inc(rank_free, 1)
            for s_ in out_free:
                dve.sem_inc(s_, 16)
            dve.wait_ge(setup_pool, CONSTANTS)
            for k in range(G):
                residual(k, k)
                norm0(k)
                stat1(k, k)
                x_parts(k, k)
                if k < 3:
                    low("qkv"[k], (qT, kT, v)[k])
            for t in range(6):
                qk(0, t)

            def group(g):
                n = 4 * g
                a = n + 4
                more = exists(a)
                for k in range(G):
                    c = n + k
                    k1, k2, k3 = (k + 3) % G, (k + 2) % G, (k + 1) % G
                    if exists(c - 1):
                        maximum(c - 1, k1)
                    if exists(c - 2):
                        prob_t(c - 2, k2, 0)
                        prob_t(c - 2, k2, 1)
                    if exists(c - 4):
                        place(c - 4, k)
                    if exists(c - 3):
                        norm2(c - 3, k3)
                    if exists(c):
                        v_high(c, k)
                    if exists(c - 1):
                        normalise(c - 1, k1)
                    if more and k < 3:
                        first = (0, 1, 3)[k]
                        residual(a + first, first)
                        norm0(a + first)
                    if more and k == 3:
                        qk(g + 1, 0)
                    if exists(c - 2):
                        residual2(c - 2, k2)
                    if more and k < 3:
                        stat1(a + first, first)
                    if more and k == 3:
                        qk(g + 1, 1)
                    if exists(c - 3):
                        choose(c - 3)
                    if more and k < 3:
                        x_parts(a + first, first)
                    if more and k == 1:
                        residual(a + 2, 2)
                        norm0(a + 2)
                        stat1(a + 2, 2)
                        x_parts(a + 2, 2)
                    if more and k == 3:
                        for t in range(2, 6):
                            qk(g + 1, t)

            group(0)
            with dve.Fori(1, NG - 1) as g:
                group(g)
            group(NG - 1)
            group(NG)

        @block.tensor
        def _(pe):
            def mix(a, k, c):
                pe.wait_ge(emb_done, 4 * a + 3)
                pe.wait_ge(graph_in[k], 4 * (a - k) + 16)
                wait_count(pe, h0_done, 3 * a - 2)
                if c is not None:
                    pe.wait_ge(v_ev[0], c + 1)
                    if exists(c - 3):
                        pe.wait_ge(x2T_ev, c - 3 + (k == 2))
                for c in range(2):
                    mm = pe.matmul(ps_agg[:, c, :], emb[k % 2][:, c * DC:(c + 1) * DC], graph[k][:], start=True, stop=True)
                mm.then_inc(agg_mm, 1)

            def project(a):
                pe.wait_ge(agg_ev, a + 1)
                for c in range(2):
                    mm = pe.matmul(ps_proj, aggT[:, c, :], w_dense[:, c, :], start=c == 0, stop=c == 1)
                mm.then_inc(proj_mm, 1)

            def turn_x(a, k, c=None):
                pe.wait_ge(x_lo, a + 1)
                wait_count(pe, xt_ev, a)
                if c is not None:
                    pe.wait_ge(v_ev[1], c + 1)
                for c in range(4):
                    mm = pe.transpose(ps_x[:, c * S:(c + 1) * S], x_cat[k % 2][:, c, :], ident[:])
                mm.then_inc(xt_mm, 1)

            TERMS = ((0, 0), (1, 1), (2, 2), (0, 3), (3, 4))

            def qk(g, j):
                bank, t = j % 2, j // 2
                if t == 0:
                    pe.wait_ge(xt_ev, 4 * g + 4)
                if t:
                    pe.wait_ge(qk_ev[bank], 6 * g + t)
                elif not isinstance(g, int) or g:
                    pe.wait_ge(score_ev, 8 * g)
                m = "q" if j < 6 else "k"
                for i, (cx, cw) in enumerate(TERMS):
                    mm = pe.matmul(ps_qk[bank], w_split[m][:, cw, (j % 6) * P:(j % 6 + 1) * P], xT[:, cx, :],
                                   start=i == 0, stop=i == KC - 1)
                mm.then_inc(qk_mm[bank], 1)

            def values(n, k, half):
                for i, (cx, cw) in enumerate(TERMS):
                    mm = pe.matmul(ps_v[half][:, 0:A // 2], xT[:, cx, k * S:(k + 1) * S],
                                   w_split["v"][:, cw, half * (A // 2):(half + 1) * (A // 2)],
                                   start=i == 0, stop=i == KC - 1)
                mm.then_inc(v_mm[half], 1)

            def values_low(n, k, mixed):
                pe.wait_ge(h0_done, 3 * mixed - 2)
                if exists(n - 4):
                    pe.wait_ge(x2T_ev, n - 3)
                values(n, k, 0)

            def values_high(n, k, turned):
                pe.wait_ge(xt_ev, turned)
                if exists(n - 4):
                    pe.wait_ge(rank_free, n - 2)
                values(n, k, 1)

            def scores(g, k, u):
                n = 4 * g + k
                if k == 0 and u == 0:
                    pe.wait_ge(qk_ev[0], 6 * g + 6)
                    pe.wait_ge(qk_ev[1], 6 * g + 6)
                else:
                    pe.wait_ge(score_ev, 2 * n + u)
                i0, i1 = HEAD_PAIRS[u]
                for i in range(i0, i1):
                    for o in range(2):
                        mm = pe.matmul(ps_score[:, o, i - i0, :], qT[64 * o:64 * o + 64, i, k * S:(k + 1) * S],
                                       kT[64 * o:64 * o + 64, i, k * S:(k + 1) * S], start=True, stop=True)
                mm.then_inc(score_mm, 1)

            def turn_prob(n, k, u):
                i = 3 * k + u
                if u == 1:
                    wait_count(pe, probT2_ev, n)
                else:
                    wait_count(pe, probT_ev, 2 * n + u // 2)
                if u == 0:
                    pe.wait_ge(norm_done, 5 * n + 5)
                    pe.wait_ge(fill_done, n + 1)
                for h in range(4 * u, 4 * u + 4):
                    mm = pe.transpose(ps_probT[i % 2][:, (h % 4) * S:(h % 4 + 1) * S], prob[k % 2][:, h, :], ident[:])
                mm.then_inc(probT_mm, 1)

            def weigh(n, k, u):
                if u < 2:
                    pe.wait_ge(probT_ev, 2 * n + u + 1)
                else:
                    pe.wait_ge(probT2_ev, n + 1)
                if u == 0:
                    pe.wait_ge(v_ev[0], n + 1)
                    pe.wait_ge(v_ev[1], n + 1)
                if u == 2:
                    wait_count(pe, h2_done, 3 * n - 2)
                for h in range(4 * u, 4 * u + 4):
                    r = 64 * (h % 2)
                    mm = pe.matmul(ps_oT[r:r + 64, h // 2, :], v[:, k, h * HD:(h + 1) * HD], probT[:, h, :],
                                   start=True, stop=True)
                if u:
                    mm.then_inc(oT_mm, 1)

            def output(n):
                pe.wait_ge(oT_ev, 2 * n + 2)
                for c in range(A // P):
                    mm = pe.matmul(ps_attn, oT[:, c, :], w_o[:, c, :], start=c == 0, stop=c == A // P - 1)
                mm.then_inc(attn_mm, 1)

            def turn_x2(n, k, mixed):
                pe.wait_ge(x2_done, n + 1)
                pe.wait_ge(h0_done, 3 * mixed - 2)
                if exists(n + 3):
                    pe.wait_ge(v_ev[0], n + 4)
                for c in range(2):
                    mm = pe.transpose(ps_x2T[:, c, :], row_a[k % 2][:, c * DC:(c + 1) * DC], ident[:])
                mm.then_inc(x2T_mm, 1)

            def router(n, turned):
                pe.wait_ge(x2T_ev, n + 1)
                pe.wait_ge(xt_ev, turned)
                if exists(n + 3):
                    pe.wait_ge(v_ev[1], n + 4)
                pe.wait_ge(rank_free, n + 1)
                for c in range(2):
                    mm = pe.matmul(ps_logits, x2T[:, c, :], w_router[:, c, :], start=c == 0, stop=c == 1)
                mm.then_inc(logit_mm, 1)

            def rank(n):
                pe.wait_ge(choice, 8 * n + 7)
                pe.matmul(ps_rank, before[:], is_any[:], start=True, stop=True)
                pe.matmul(ps_total, ones_bf[:], is_any[:], start=True, stop=True).then_inc(rank_mm, 1)

            pe.wait_ge(const_in, 16 * 10)
            pe.wait_ge(setup_pool, CONSTANTS)
            for k in range(G):
                mix(k, k, None)
                project(k)
                if k:
                    turn_x(k - 1, k - 1)
            turn_x(3, 3)
            pe.wait_ge(w_lo, 10)
            for j in range(12):
                qk(0, j)
            pe.wait_ge(w_lo, 15)

            def group(g):
                n = 4 * g
                a = n + 4
                more = exists(a)
                for k in range(G):
                    c = n + k
                    k2, k3 = (k + 2) % G, (k + 1) % G
                    mixed = [a + j for j in (0, 1, 3, 4)] if more else [B] * 4
                    mixed_after = [a + j for j in (1, 2, 4, 4)] if more else [B] * 4
                    turned = [a + j for j in (0, 0, 1, 3)] if more else [B] * 4
                    turned_after = [a + j for j in (0, 1, 3, 4)] if more else [B] * 4
                    if exists(c - 2):
                        turn_prob(c - 2, k2, 0)
                        turn_prob(c - 2, k2, 1)
                    if exists(c):
                        scores(g, k, 0)
                    if exists(c - 4):
                        rank(c - 4)
                    if exists(c):
                        values_low(c, k, mixed[k])
                    if exists(c - 2):
                        weigh(c - 2, k2, 0)
                    if exists(c):
                        values_high(c, k, turned[k])
                        scores(g, k, 1)
                    if more and k < 3:
                        mix(a + (0, 1, 3)[k], (0, 1, 3)[k], c)
                    if more and k >= 2:
                        turn_x(a + 2 * k - 3, 2 * k - 3, c)
                    if exists(c - 2):
                        turn_prob(c - 2, k2, 2)
                        weigh(c - 2, k2, 1)
                    if more and k < 3:
                        project(a + (0, 1, 3)[k])
                    if exists(c - 2):
                        weigh(c - 2, k2, 2)
                    if more and k in (1, 2):
                        turn_x(a + 2 * k - 2, 2 * k - 2, c)
                    if exists(c - 3):
                        turn_x2(c - 3, k3, mixed_after[k])
                    if more and k == 3:
                        qk(g + 1, 0)
                        qk(g + 1, 1)
                    if exists(c - 2):
                        output(c - 2)
                    if more and k == 3:
                        qk(g + 1, 2)
                    if more and k == 1:
                        mix(a + 2, 2, c)
                    if exists(c - 3):
                        router(c - 3, turned_after[k])
                    if more and k == 1:
                        project(a + 2)
                    if more and k == 3:
                        for j in range(3, 12):
                            qk(g + 1, j)

            group(0)
            with pe.Fori(1, NG - 1) as g:
                group(g)
            group(NG - 1)
            group(NG)


def expert_block(nc, dram, route):
    out, rows = dram["out"], dram["rows"]
    ctx = ExitStack()
    with ctx:
        def sb(name, shape, dt=f32):
            return ctx.enter_context(nc.sbuf_tensor("ffn_" + name, shape, dt))

        def sem(name):
            return ctx.enter_context(nc.semaphore("ffn_" + name))

        w_in = sb("w_in", [DC + 1, NE, 2, F])
        w_out = sb("w_out", [P, NE, FC, D])
        out_b = sb("out_b", [P, NE, D])
        ident = sb("ident2", [P, P])
        filler = sb("filler", [P, ROW])
        step_i = sb("step_i", [P, 32], i32)
        step = sb("step", [P, 32])
        tile_i = sb("tile_i", [P, TILES], i32)
        tile_no = sb("tile_no", [P, TILES])
        expert_i = sb("expert_i2", [P, NE], i32)
        expert_no = sb("expert_no2", [P, NE])
        base = sb("base", [P, NE])
        count = sb("count", [P, NE])
        over = sb("over", [P, NE, 32])
        tiles = sb("tiles", [P, NE])
        upto = sb("upto", [P, NE])
        begin = sb("begin", [P, NE])
        passed = sb("passed", [P, TILES, NE])
        owner = sb("owner", [P, TILES])
        owned = sb("owned", [P, TILES, NE])
        used = sb("used", [P, TILES])
        offset = sb("offset", [P, TILES])
        row_f = sb("row_f", [P, TILES])
        owner7 = sb("owner7", [P, TILES])
        row_of = sb("row_of", [P, TILES], i32)
        expert_of = sb("expert_of", [P, TILES], i32)
        end_of = sb("end_of", [P, NE], i32)
        RING = 4
        x = [sb(f"x{k}", [P, ROW]) for k in range(RING)]
        xT = [sb(f"xT{k}", [DC + 1, 2, P]) for k in range(2)]
        h = [sb(f"h{k}", [P, F]) for k in range(2)]
        hT = sb("hT", [P, FC, P])
        y = [sb(f"y{k}", [P, D]) for k in range(2)]
        yw = [sb(f"yw{k}", [P, D]) for k in range(2)]
        token = [sb(f"token{k}", [P, 1], i32) for k in range(2)]
        ps_xT = ctx.enter_context(nc.psum_tensor("ps_xT", [P, 512], f32))
        ps_h = [ctx.enter_context(nc.psum_tensor(f"ps_h{k}", [P, 1024], f32)) for k in range(2)]
        ps_hT = ctx.enter_context(nc.psum_tensor("ps_hT", [P, 1024], f32))
        ps_y = ctx.enter_context(nc.psum_tensor("ps_y", [P, 512], f32))

        w_ready = sem("w_ready")
        b_ready = sem("b_ready")
        made_p = sem("made_p")
        made_d = sem("made_d")
        filled = sem("filled")
        x_in = [sem(f"x_in{k}") for k in range(RING)]
        xT_mm = sem("xT_mm")
        xT_ev = sem("xT_ev")
        h_mm = sem("h_mm")
        gelu_done = sem("gelu_done")
        hT_mm = sem("hT_mm")
        hT_ev = sem("hT_ev")
        y_mm = sem("y_mm")
        y_done = sem("y_done")
        added = sem("added")
        block = ctx.enter_context(nc.Block())
        POOL_MADE, DVE_MADE = 10, 27

        @block.sync
        def _(sp):
            for e in range(NE):
                sp.dma_start(w_in[0:DC, e], dram["wi"][e].rearrange("(c p) f -> p c f", p=DC)).then_inc(w_ready, 16)
                sp.dma_start(w_in[DC:DC + 1, e, 1, :], dram["bi"][e:e + 1, :]).then_inc(w_ready, 16)
            sp.wait_ge(made_d, DVE_MADE)
            for e in range(NE):
                at = sp.value_load(end_of[0:1, e:e + 1], min_val=0, max_val=NE * REGION - P)
                sp.dma_start(rows[bass.ds(at, P), :], filler[:]).then_inc(filled, 16)
            sp.dma_start(rows[NOWHERE:NOWHERE + P, :], filler[:]).then_inc(filled, 16)
            sp.wait_ge(filled, 16 * (NE + 1))

            def load(t, k):
                at = sp.value_load(row_of[0:1, bass.ds(t, 1)], min_val=0, max_val=NOWHERE)
                sp.dma_start(x[k][:], rows[bass.ds(at, P), :]).then_inc(x_in[k], 16)

            for k in range(RING):
                load(k, k)
            with sp.Fori(0, TILES // RING - 1) as r:
                for k in range(RING):
                    t = RING * r + k
                    wait_apart(sp, made_p, y_done, 3 * t + 3)
                    load(t + RING, k)
            for t in range(TILES // RING * RING, TILES):
                sp.wait_ge(y_done, 3 * (t - RING) + 3)
                load(t, t % RING)

        @block.gpsimd
        def _(pool):
            made = [0]

            def link(ins):
                made[0] += 1
                ins.then_inc(made_p, 1)
                pool.wait_ge(made_p, made[0])

            link(pool.iota(step_i[:], pattern=[[P, 32]], base=0, channel_multiplier=0))
            link(pool.tensor_copy(step[:], step_i[:]))
            link(pool.iota(tile_i[:], pattern=[[1, TILES]], base=0, channel_multiplier=0))
            link(pool.tensor_copy(tile_no[:], tile_i[:]))
            link(pool.iota(expert_i[:], pattern=[[1, NE]], base=0, channel_multiplier=0))
            link(pool.tensor_copy(expert_no[:], expert_i[:]))
            link(pool.memset(filler[:], 0.0))
            link(pool.memset(filler[:, D + 1:D + 2], float(NO_TOKEN)))
            link(pool.memset(ident[:], 0.0))
            link(pool.affine_select(out=ident[:], in_=ident[:], compare_op=ALU.not_equal, fill=1.0, base=0,
                                    pattern=[[-1, P]], channel_multiplier=1))
            assert made[0] == POOL_MADE

            def add(t, k):
                wait_apart(pool, made_p, y_done, 3 * t + 3)
                pool.indirect_dma_start(out, bass.IndirectOffsetOnAxis(ap=token[k][:], axis=0), yw[k][:], None,
                                        bounds_check=T - 1, oob_is_err=False, compute_op=ALU.add).then_inc(added, 16)
                wait_apart(pool, made_p, added, 16 * t + 16)

            with pool.Fori(0, TILES // 2) as r:
                for k in range(2):
                    add(2 * r + k, k)
            add(TILES - 1, (TILES - 1) % 2)

        @block.scalar
        def _(act):
            for e in range(NE):
                act.dma_start(w_out[:, e], dram["wout"][e].rearrange("(c p) n -> p c n", p=P)).then_inc(w_ready, 16)
            act.dma_start(out_b[:], bass.AP(dram["bo"].tensor, 0, [[0, P], [D, NE], [1, D]])).then_inc(b_ready, 16)
            act.wait_ge(made_d, DVE_MADE)

            def x_t(t, k):
                act.wait_ge(xT_mm, t + 1)
                act.activation(xT[k][0:DC], ps_xT[0:DC, k * 2 * P:(k + 1) * 2 * P].rearrange("p (c s) -> p c s", s=P),
                               ACT.Copy).then_inc(xT_ev, 1)

            def gelu(t, k):
                act.wait_ge(h_mm, t + 1)
                act.activation(h[k][:], ps_h[k][:, 0:F], ACT.Gelu).then_inc(gelu_done, 1)

            x_t(0, 0)
            x_t(1, 1)
            gelu(0, 0)
            with act.Fori(0, (TILES - 3) // 2) as r:
                for k in range(2):
                    t = 2 * r + 1 + k
                    gelu(t, (k + 1) % 2)
                    x_t(t + 1, k)
            gelu(TILES - 2, (TILES - 2) % 2)
            x_t(TILES - 1, (TILES - 1) % 2)
            gelu(TILES - 1, (TILES - 1) % 2)

        @block.vector
        def _(dve):
            made = [0]

            def link(ins):
                made[0] += 1
                ins.then_inc(made_d, 1)
                dve.wait_ge(made_d, made[0])

            def per_expert(t_):
                return t_[:].unsqueeze(1).broadcast_to([P, TILES, NE])

            def per_tile(t_):
                return t_[:].unsqueeze(2).broadcast_to([P, TILES, NE])

            dve.wait_ge(made_p, POOL_MADE)
            link(dve.memset(xT[0][DC:DC + 1], 1.0))
            link(dve.memset(xT[1][DC:DC + 1], 1.0))
            link(dve.tensor_copy(end_of[:], route[:]))
            link(dve.tensor_scalar(base[:], expert_no[:], float(REGION), None, ALU.mult))
            link(dve.tensor_tensor(count[:], route[:], base[:], ALU.subtract))
            link(dve.tensor_tensor(over[:], count[:].unsqueeze(2).broadcast_to([P, NE, 32]),
                                   step[:].unsqueeze(1).broadcast_to([P, NE, 32]), ALU.is_gt))
            link(dve.tensor_reduce(tiles[:], over[:], AX.X, ALU.add))
            link(dve.tensor_copy(upto[:], tiles[:]))
            for e in range(1, NE):
                link(dve.tensor_tensor(upto[:, e:e + 1], upto[:, e - 1:e], tiles[:, e:e + 1], ALU.add))
            link(dve.tensor_tensor(begin[:], upto[:], tiles[:], ALU.subtract))
            link(dve.tensor_tensor(passed[:], per_tile(tile_no), per_expert(upto), ALU.is_ge))
            link(dve.tensor_reduce(owner[:], passed[:], AX.X, ALU.add))
            link(dve.tensor_tensor(owned[:], per_tile(owner), per_expert(expert_no), ALU.is_equal))
            link(dve.scalar_tensor_tensor(base[:], begin[:], -float(P), base[:], ALU.mult, ALU.add))
            link(dve.tensor_tensor(owned[:], owned[:], per_expert(base), ALU.mult))
            link(dve.tensor_reduce(offset[:], owned[:], AX.X, ALU.add))
            link(dve.tensor_scalar(used[:], owner[:], float(NE), None, ALU.is_lt))
            link(dve.tensor_scalar(row_f[:], tile_no[:], float(P), float(-NOWHERE), ALU.mult, ALU.add))
            link(dve.tensor_tensor(row_f[:], row_f[:], used[:], ALU.mult))
            link(dve.scalar_tensor_tensor(row_of[:], row_f[:], float(NOWHERE), offset[:], ALU.add, ALU.add))
            dve.tensor_scalar(expert_of[:], owner[:], float(NE - 1), None, ALU.min).then_inc(made_d, 1)
            made[0] += 1
            assert made[0] == DVE_MADE, made[0]
            dve.wait_ge(made_d, DVE_MADE)
            dve.wait_ge(b_ready, 16)

            def h_t(t):
                for half in range(2):
                    dve.wait_ge(hT_mm, 2 * t + half + 1)
                    c0, c1 = ((0, 4), (4, 6))[half]
                    dve.tensor_copy(hT[:, c0:c1, :], ps_hT[:, c0 * P:c1 * P].rearrange("p (c s) -> p c s", s=P)).then_inc(hT_ev, 1)

            def finish(t, k, kx):
                e = dve.value_load(expert_of[0:1, bass.ds(t, 1)], min_val=0, max_val=NE - 1)
                dve.wait_ge(y_mm, t + 1)
                dve.tensor_tensor(y[k][:], ps_y[:, k * 256:k * 256 + D],
                                  out_b[:, bass.ds(e, 1), :].rearrange("p o n -> p (o n)"), ALU.add).then_inc(y_done, 1)
                dve.wait_ge(y_done, 3 * t + 1)
                if not isinstance(t, int) or t >= 2:
                    dve.wait_ge(added, 16 * t - 16)
                dve.tensor_scalar(yw[k][:], y[k][:], x[kx][:, D:D + 1], None, ALU.mult).then_inc(y_done, 1)
                dve.tensor_copy(token[k][:], x[kx][:, D + 1:D + 2]).then_inc(y_done, 1)

            for t in range(4):
                h_t(t)
                finish(t, t % 2, t % 4)
            with dve.Fori(1, TILES // 4) as r:
                for k in range(4):
                    t = 4 * r + k
                    h_t(t)
                    finish(t, k % 2, k)
            for t in range(TILES // 4 * 4, TILES):
                h_t(t)
                finish(t, t % 2, t % 4)

        @block.tensor
        def _(pe):
            pe.wait_ge(made_d, DVE_MADE)

            def turn_x(t, k, kx):
                pe.wait_ge(x_in[kx], 16 * (t // RING) + 16 if isinstance(t, int) else 4 * (t - kx) + 16)
                for c in range(2):
                    mm = pe.transpose(ps_xT[0:DC, (2 * k + c) * P:(2 * k + c + 1) * P], x[kx][:, c * DC:(c + 1) * DC], ident[:])
                mm.then_inc(xT_mm, 1)

            def up(t, k):
                e = pe.value_load(expert_of[0:1, bass.ds(t, 1)], min_val=0, max_val=NE - 1)
                pe.wait_ge(xT_ev, t + 1)
                for c0, c1 in ((0, 512), (512, F)):
                    for c in range(2):
                        rows_ = DC + c
                        mm = pe.matmul(ps_h[k][:, c0:c1], xT[k][0:rows_, c, :],
                                       w_in[0:rows_, bass.ds(e, 1), c, c0:c1].rearrange("p o f -> p (o f)"),
                                       start=c == 0, stop=c == 1)
                mm.then_inc(h_mm, 1)

            def turn_h(t, k):
                for half, (c0, c1) in enumerate(((0, 4), (4, 6))):
                    if half == 0:
                        pe.wait_ge(gelu_done, t + 1)
                    for c in range(c0, c1):
                        mm = pe.transpose(ps_hT[:, c * P:(c + 1) * P], h[k][:, c * P:(c + 1) * P], ident[:])
                    mm.then_inc(hT_mm, 1)

            def down(t, k):
                e = pe.value_load(expert_of[0:1, bass.ds(t, 1)], min_val=0, max_val=NE - 1)
                for c in range(FC):
                    if c in (0, 4):
                        pe.wait_ge(hT_ev, 2 * t + (1 if c == 0 else 2))
                    mm = pe.matmul(ps_y[:, k * 256:k * 256 + D], hT[:, c, :],
                                   w_out[:, bass.ds(e, 1), c, :].rearrange("p o n -> p (o n)"),
                                   start=c == 0, stop=c == FC - 1)
                mm.then_inc(y_mm, 1)

            turn_x(0, 0, 0)
            pe.wait_ge(xT_ev, 1)
            turn_x(1, 1, 1)
            pe.wait_ge(w_ready, 16 * 3 * NE)
            up(0, 0)

            def turn(t, k, kx):
                up(t, (k + 1) % 2)
                turn_h(t - 1, k)
                turn_x(t + 1, k, kx)
                down(t - 1, k)

            for t in (1, 2, 3, 4):
                turn(t, (t - 1) % 2, (t + 1) % 4)
            with pe.Fori(0, (TILES - 3 - 4) // 4) as r:
                for k in range(4):
                    turn(4 * r + 5 + k, k % 2, (6 + k) % 4)
            for t in range(5 + (TILES - 3 - 4) // 4 * 4, TILES - 1):
                turn(t, (t - 1) % 2, (t + 1) % 4)
            up(TILES - 1, (TILES - 1) % 2)
            turn_h(TILES - 2, (TILES - 2) % 2)
            down(TILES - 2, (TILES - 2) % 2)
            turn_h(TILES - 1, (TILES - 1) % 2)
            down(TILES - 1, (TILES - 1) % 2)


def tower(nc, dram):
    with nc.sbuf_tensor("route", [P, NE], f32) as route:
        attention_block(nc, dram, route)
        expert_block(nc, dram, route)


def kernel(x, mask_BS_i1_0, fside_BSS_graph, L0_tok_tok_emb, L0_tok_seg_emb, L0_tok_pos_emb, L0_tok_dense_w,
           L0_tok_dense_b, L0_tok_ln_gamma, L0_tok_ln_beta, L0_attn_Wq, L0_attn_bq, L0_attn_Wk, L0_attn_bk,
           L0_attn_Wv, L0_attn_bv, L0_attn_Wo, L0_attn_bo, L0_ffn_Wr, L0_ffn_Wi, L0_ffn_bi, L0_ffn_Wo, L0_ffn_bo):
    import numpy as np
    import concourse.bacc as bacc
    from concourse import mybir as mb
    from concourse.bass_utils import run_bass_kernel_spmd

    def turned(a, *axes):
        return np.ascontiguousarray(np.transpose(np.asarray(a), axes))

    def as_is(a):
        return np.ascontiguousarray(np.asarray(a))

    arrays = {
        "ids": turned(x, 1, 0), "mask": turned(mask_BS_i1_0, 1, 0), "graphT": turned(fside_BSS_graph, 0, 2, 1),
        "tok_emb": as_is(L0_tok_tok_emb), "seg_emb": as_is(L0_tok_seg_emb), "pos_emb": as_is(L0_tok_pos_emb),
        "dense_w": as_is(L0_tok_dense_w), "dense_b": as_is(L0_tok_dense_b), "ln_gamma": as_is(L0_tok_ln_gamma),
        "ln_beta": as_is(L0_tok_ln_beta), "wq": as_is(L0_attn_Wq), "bq": as_is(L0_attn_bq), "wk": as_is(L0_attn_Wk),
        "bk": as_is(L0_attn_bk), "wv": as_is(L0_attn_Wv), "bv": as_is(L0_attn_bv), "wo": as_is(L0_attn_Wo),
        "attn_bo": as_is(L0_attn_bo), "router": turned(L0_ffn_Wr, 1, 0), "wi": turned(L0_ffn_Wi, 0, 2, 1),
        "bi": as_is(L0_ffn_bi), "wout": turned(L0_ffn_Wo, 0, 2, 1), "bo": as_is(L0_ffn_bo),
    }
    nc = bacc.Bacc("TRN2", target_bir_lowering=False, num_devices=1)
    dram = {n: nc.dram_tensor(f"in_{n}", a.shape, mb.dt.from_np(a.dtype), kind="ExternalInput").ap()
            for n, a in arrays.items()}
    dram["out"] = nc.dram_tensor("out_rows", (T, D), f32, kind="ExternalOutput").ap()
    dram["shear"] = nc.dram_tensor("shear", (P * PITCH + HALF,), f32, kind="Internal").ap()
    dram["rows"] = nc.dram_tensor("rows", (NOWHERE + P, ROW), f32, kind="Internal").ap()
    tower(nc, dram)
    r = run_bass_kernel_spmd(nc, [{f"in_{n}": a for n, a in arrays.items()}], core_ids=[0])
    return r.results[0]["out_rows"].reshape(B, S, D)
```

```python
import concourse.bass as bass
from concourse import mybir
from contextlib import ExitStack

f32 = mybir.dt.float32
f32r = mybir.dt.float32r
bf16 = mybir.dt.bfloat16
i32 = mybir.dt.int32
u32 = mybir.dt.uint32
ALU = mybir.AluOpType
ACT = mybir.ActivationFunctionType
AX = mybir.AxisListType

P = 128
B, S, D = 32, 128, 192
DC = D // 2
NH, HD = 12, 64
A = NH * HD
HALF = 32
BAND = 2 * HALF + 1
G = 4
NG = B // G
SLOT = HALF + S
PITCH = NH * SLOT
HEAD_PAIRS = ((0, 4), (4, 6))
NE, F = 8, 768
FC = F // P
T = B * S
REGION = T + P
LOAD_AT = (30, 31, 32, 33, 34, 35)
EARLY_EXPERTS = len(LOAD_AT)
ROW = D + 2
NOWHERE = NE * REGION
TILES = (2 * T + NE * (P - 1)) // P
NO_TOKEN = 2 * T
STEPS = T // P
EARLY, CONSTANTS = 6, 24
KC = 5
ROOM = (NE - 3) * KC * F
TERMS = ((0, 0), (1, 1), (2, 2), (0, 3), (3, 4))


def wait_apart(eng, passed, sem, value):
    if not isinstance(value, int):
        value = eng.to_reg(value)
        eng.wait_ge(passed, 1)
    if not isinstance(value, int) or value > 0:
        eng.wait_ge(sem, value)


def exists(m):
    return not isinstance(m, int) or 0 <= m < B


def wait_count(eng, sem, value):
    if not isinstance(value, int) or value > 0:
        eng.wait_ge(sem, value)


def attention_block(nc, dram, shared):
    route, ident, tile_row, step, filler, row_of, expert_of, end_of, w_in_all, qkv_split, room = shared
    x_ids, mask, graphT = dram["ids"], dram["mask"], dram["graphT"]
    out, shear, rows = dram["out"], dram["shear"], dram["rows"]
    ctx = ExitStack()
    with ctx:
        def sb(name, shape, dt=f32):
            return ctx.enter_context(nc.sbuf_tensor(name, shape, dt))

        def sem(name):
            return ctx.enter_context(nc.semaphore(name))

        w_split = {m: qkv_split[:, i] for i, m in enumerate("qkv")}
        taken = [0]

        def part(a, b):
            at = taken[0]
            taken[0] += a * b
            return room[:, at:at + a * b].rearrange("p (a b) -> p a b", b=b)

        w_o = sb("w_o", [P, A // P, D])
        w_dense = sb("w_dense", [DC + 1, 2, D])
        w_router = sb("w_router", [DC, 2, NE])
        seg0_pos = sb("seg0_pos", [P, D])
        seg_diff = sb("seg_diff", [P, D])
        seg0 = sb("seg0", [P, D])
        gamma = sb("gamma", [P, D])
        beta = sb("beta", [P, D])
        attn_bo = sb("attn_bo", [P, D])
        before = sb("before", [P, P], bf16)
        ones_bf = sb("ones_bf", [P, P], bf16)
        expert_i = sb("expert_i", [P, NE], i32)
        tile_i = sb("tile_i", [P, TILES], i32)
        step_i = sb("step_i", [P, STEPS], i32)
        token_i = sb("token_i", [P, B], i32)
        token_no = sb("token_no", [P, B])
        minus_half = sb("minus_half", [P, 1])
        ids = sb("ids", [P, B + G], i32)
        seg_i = sb("seg_i", [P, B + G], i32)
        seg_f = sb("seg_f", [P, B + G])
        up_hi = sb("up_hi", [DC + 1, F], f32r)
        ids4 = sb("ids4", [P, G], i32)
        seg4 = sb("seg4", [P, G])
        tok = [sb(f"tok{k}", [P, D]) for k in range(G)]
        graph = [sb(f"graph{k}", [P, S]) for k in range(G)]
        seg_part = [sb(f"seg_part{k}", [P, D]) for k in range(2)]
        seg_pos = [sb(f"seg_pos{k}", [P, D]) for k in range(2)]
        emb = [sb(f"emb{k}", [P, D]) for k in range(2)]
        aggT = sb("aggT", [DC + 1, 2, S])
        h0 = sb("h0", [P, D])
        h_stats = sb("h_stats", [P, 6])
        h_mv = sb("h_mv", [P, 2])
        h_ve = sb("h_ve", [P, 1])
        h_rstd = sb("h_rstd", [P, 1])
        hn = sb("hn", [P, D])
        hg = sb("hg", [P, D])
        h1 = [sb(f"h1_{k}", [P, D]) for k in range(2)]
        stats1 = sb("stats1", [P, 6])
        mv1 = sb("mv1", [P, 2])
        ve1 = sb("ve1", [P, 1])
        rstd1 = sb("rstd1", [P, 1])
        x_full = sb("x_full", [P, D])
        x_cat = [sb(f"x_cat{k}", [P, 4, P]) for k in range(2)]
        h_res = sb("h_res", [P, B, D])
        xT = sb("xT", [P, 4, G * S], f32r)
        qT, kT = part(A // P, G * S), part(A // P, G * S)
        score = [part(NH, S) for k in range(2)]
        up_raw = part(1, F)[:, 0, :]
        prob = [part(NH, S) for k in range(3)]
        v = part(G, A)
        prob.append(part(NH, S))
        assert taken[0] == ROOM
        zeros = prob[3][:].rearrange("p (o h) s -> p o (h s)", o=2)[:, 0, :]
        bias_row = {m: s_[:].rearrange("p (o h) s -> p o (h s)", o=2)[:, o, :]
                    for m, s_, o in (("q", score[0], 0), ("k", score[0], 1), ("v", score[1], 0))}
        band_max = sb("band_max", [P, NH])
        band_max0 = [sb(f"band_max0_{k}", [P, NH]) for k in range(2)]
        e_zero = [sb(f"e_zero{k}", [P, NH]) for k in range(2)]
        band_sum = sb("band_sum", [P, NH])
        denom = sb("denom", [P, NH])
        r_denom = sb("r_denom", [P, NH])
        p_zero = sb("p_zero", [P, NH])
        probT = sb("probT", [P, NH, S])
        oT = sb("oT", [P, A // P, S])
        h2 = [sb(f"h2_{k}", [P, D]) for k in range(2)]
        stats2 = sb("stats2", [P, 6])
        mv2 = sb("mv2", [P, 2])
        ve2 = sb("ve2", [P, 1])
        rstd2 = sb("rstd2", [P, 1])
        row_a = [sb(f"row_a{k}", [P, ROW]) for k in range(2)]
        row_b = [sb(f"row_b{k}", [P, ROW]) for k in range(2)]
        x2T = sb("x2T", [DC, 2, S])
        logits = sb("logits", [P, NE])
        top = sb("top", [P, 8])
        top_i = sb("top_i", [P, 8], u32)
        top_f = sb("top_f", [P, 2])
        is_1 = sb("is_1", [P, NE])
        is_2 = sb("is_2", [P, NE])
        is_any = sb("is_any", [P, NE], bf16)
        gap = sb("gap", [P, 1])
        e_gap = sb("e_gap", [P, 1])
        one_e = sb("one_e", [P, 1])
        where = sb("where", [P, NE])
        pick1 = sb("pick1", [P, NE])
        pick2 = sb("pick2", [P, NE])
        pos_f = sb("pos_f", [P, 2])
        pos = [sb(f"pos{k}", [P, 2], i32) for k in range(2)]
        expert_no = sb("expert_no", [P, NE])
        tile_no = sb("tile_no", [P, TILES])
        base = sb("base", [P, NE])
        count = sb("count", [P, NE])
        over = sb("over", [P, NE, STEPS])
        tiles = sb("tiles", [P, NE])
        upto = [sb(f"upto{k}", [P, NE]) for k in range(4)]
        jump = sb("jump", [P, NE])
        owner = sb("owner", [P, TILES])
        passed, jumps = (probT[:, h:h + NH // 2, :].rearrange("p h s -> p (h s)")[:, 0:TILES * NE].rearrange(
            "p (t e) -> p t e", e=NE) for h in (0, NH // 2))
        offset = sb("offset", [P, TILES])
        row_f = sb("row_f", [P, TILES])

        ps_s = ctx.enter_context(nc.psum_tensor("ps_s", [P, 1024], f32))
        ps_probT = [ctx.enter_context(nc.psum_tensor(f"ps_probT{i}", [P, 512], f32)) for i in range(2)]
        ps_o = ctx.enter_context(nc.psum_tensor("ps_o", [P, 1024], f32))
        ps_a = ctx.enter_context(nc.psum_tensor("ps_a", [P, 512], f32))
        ps_x = ctx.enter_context(nc.psum_tensor("ps_x", [P, 512], f32))
        ps_score = ps_s[:].rearrange("p (o i s) -> p o i s", o=2, s=S)
        ps_qk = [ps_s[:, 0:512], ps_s[:, 512:1024]]
        ps_oT = ps_o[:, 0:A].rearrange("p (c s) -> p c s", s=S)
        ps_attn = ps_o[:, A:A + D]
        ps_logits = ps_x[:, 0:NE]
        ps_rank = ps_x[:, 16:16 + NE]
        ps_total = ps_x[:, 32:32 + NE]
        ps_agg = ps_a[0:DC, 0:2 * S].rearrange("p (c s) -> p c s", s=S)
        ps_x2T = ps_agg
        ps_proj = ps_a[:, 2 * S:2 * S + D]
        ps_v = [ps_a, ps_x]

        emb_in = sem("emb_in")
        dense_in = sem("dense_in")
        const_in = sem("const_in")
        ids_in = sem("ids_in")
        w_in = {m: sem(f"w{m}_in") for m in "qkv"}
        pad_zero = sem("pad_zero")
        setup_pool = sem("setup_pool")
        setup_dve = sem("setup_dve")
        later = sem("later")
        plan = sem("plan")
        zeros_out = sem("zeros_out")
        raw_in = sem("raw_in")
        raw_hi_done = sem("raw_hi_done")
        raw_lo_done = sem("raw_lo_done")
        w_in_done = sem("w_in_done")
        split_out = sem("split_out")
        w_hi = sem("w_hi")
        w_lo = sem("w_lo")
        wv_lo = sem("wv_lo")
        graph_in = [sem(f"graph_in{k}") for k in range(G)]
        tok_in = [sem(f"tok_in{k}") for k in range(G)]
        staged = sem("staged")
        seg_done = sem("seg_done")
        emb_done = sem("emb_done")
        agg_mm = sem("agg_mm")
        agg_ev = sem("agg_ev")
        proj_mm = sem("proj_mm")
        h0_done = sem("h0_done")
        h0_rstd = sem("h0_rstd")
        hn_done = sem("hn_done")
        h1_done = sem("h1_done")
        kept = sem("kept")
        h1_stat = sem("h1_stat")
        h1_rstd = sem("h1_rstd")
        x_done = sem("x_done")
        x_lo = sem("x_lo")
        xt_mm = sem("xt_mm")
        xt_ev = sem("xt_ev")
        qk_mm = [sem("qk_mm_even"), sem("qk_mm_odd")]
        qk_ev = [sem("qk_ev_even"), sem("qk_ev_odd")]
        v_mm = [sem("v_mm_low"), sem("v_mm_high")]
        v_ev = [sem("v_ev_low"), sem("v_ev_high")]
        score_mm = sem("score_mm")
        score_ev = sem("score_ev")
        shear_out = sem("shear_out")
        band_in = sem("band_in")
        max_done = sem("max_done")
        sub_done = sem("sub_done")
        exp_done = sem("exp_done")
        norm_done = sem("norm_done")
        fill_done = sem("fill_done")
        probT_mm = sem("probT_mm")
        probT_ev = sem("probT_ev")
        probT2_ev = sem("probT2_ev")
        oT_mm = sem("oT_mm")
        oT_ev = sem("oT_ev")
        rowb_x = sem("rowb_x")
        attn_mm = sem("attn_mm")
        h2_done = sem("h2_done")
        h2_rstd = sem("h2_rstd")
        x2_done = sem("x2_done")
        x2T_mm = sem("x2T_mm")
        x2T_ev = sem("x2T_ev")
        logit_mm = sem("logit_mm")
        choice = sem("choice")
        e_gap_done = sem("e_gap_done")
        rank_mm = sem("rank_mm")
        placed = sem("placed")
        rank_free = sem("rank_free")
        row_done = sem("row_done")
        out_free = [sem(f"out_free{k}") for k in range(2)]
        rowa_free = [sem(f"rowa_free{k}") for k in range(2)]
        rowb_free = [sem(f"rowb_free{k}") for k in range(2)]
        block = ctx.enter_context(nc.Block())

        def bcast(row):
            return bass.AP(row.tensor, row.offset, [[0, P]] + list(row.ap))

        def all_heads(stat, w=BAND):
            return stat[:].unsqueeze(2).broadcast_to([P, NH, w])

        def low_part_of(m, raw, eng, done):
            i = "qkv".index(m)
            flat = raw[:].rearrange("p a b -> p (a b)")
            before_this = 3 if m == "k" else 0
            eng.wait_ge(w_hi, 3 * i + 3)
            eng.tensor_tensor(w_split[m][:, 3, :], flat[:, 0:A], w_split[m][:, 0, :].bitcast(f32),
                              ALU.subtract).then_inc(done, 1)
            eng.tensor_tensor(w_split[m][0:64, 4, :], flat[0:64, A:2 * A], w_split[m][0:64, 1, :].bitcast(f32),
                              ALU.subtract).then_inc(done, 1)
            eng.wait_ge(done, before_this + 2)
            eng.tensor_tensor(w_split[m][96:97, 4, :], bias_row[m][96:97, :], w_split[m][96:97, 4, :].bitcast(f32),
                              ALU.subtract).then_inc(done, 1)

        @block.sync
        def _(sp):
            sp.dma_start(ids[:, 0:B], x_ids).then_inc(ids_in, 16)
            sp.dma_start(seg_i[:, 0:B], mask).then_inc(ids_in, 16)
            sp.dma_start(seg0_pos[:], dram["pos_emb"]).then_inc(emb_in, 16)
            sp.dma_start(seg0[:], bcast(dram["seg_emb"][0])).then_inc(emb_in, 16)
            sp.dma_start(seg_diff[:], bcast(dram["seg_emb"][1])).then_inc(emb_in, 16)

            def load_graph(n, k):
                sp.dma_start(graph[k][:], graphT[n]).then_inc(graph_in[k], 16)

            load_graph(0, 0)
            sp.dma_start(w_dense[0:DC], dram["dense_w"].rearrange("(c p) e -> p c e", p=DC)).then_inc(dense_in, 16)
            sp.dma_start(w_dense[DC:DC + 1, 1, :], dram["dense_b"].rearrange("(o n) -> o n", o=1)).then_inc(dense_in, 16)
            load_graph(1, 1)
            sp.dma_start(gamma[:], bcast(dram["ln_gamma"])).then_inc(const_in, 16)
            sp.dma_start(beta[:], bcast(dram["ln_beta"])).then_inc(const_in, 16)
            sp.dma_start(attn_bo[:], bcast(dram["attn_bo"])).then_inc(const_in, 16)
            load_graph(2, 2)
            load_graph(3, 3)
            for m, raw in (("q", qT), ("k", kT), ("v", v)):
                w, flat = dram["w" + m], raw[:].rearrange("p a b -> p (a b)")
                sp.dma_start(flat[:, 0:A], w[0:P]).then_inc(w_in[m], 16)
                sp.dma_start(flat[0:64, A:2 * A], w[P:D]).then_inc(w_in[m], 16)
                sp.dma_start(flat[64:P, A:2 * A], w[0:64]).then_inc(w_in[m], 16)
                sp.dma_start(flat[:, 2 * A:3 * A], w[64:D]).then_inc(w_in[m], 16)
                for p in (64, 96):
                    sp.dma_start(bias_row[m][p:p + 1, :], dram["b" + m].rearrange("(o n) -> o n", o=1)).then_inc(w_in[m], 16)
            sp.dma_start(w_router[:], dram["router"].rearrange("(c p) e -> p c e", p=DC)).then_inc(const_in, 16)
            sp.dma_start(w_o[:], dram["wo"].rearrange("(c p) e -> p c e", p=P)).then_inc(const_in, 16)
            sp.wait_ge(setup_pool, CONSTANTS)
            sp.dma_start(shear[0:P * PITCH].rearrange("(n h m) -> n h m", h=NH, m=SLOT)[:, :, 0:HALF],
                         prob[0][:, :, 0:HALF]).then_inc(pad_zero, 16)
            sp.dma_start(shear[P * PITCH:P * PITCH + HALF].rearrange("(o m) -> o m", o=1),
                         prob[0][0:1, 0, 0:HALF]).then_inc(pad_zero, 16)
            sp.dma_start(dram["w_up"][:, 4, 64:P, :].rearrange("e p f -> p e f"),
                         zeros[0:64].unsqueeze(1).broadcast_to([64, NE, F])).then_inc(zeros_out, 16)
            sp.wait_ge(pad_zero, 32)

            def store_h2(m, k):
                wait_apart(sp, setup_pool, h2_done, 3 * m + 1)
                sp.dma_start(out[bass.ds(m * S, S), :], h2[k % 2][:]).then_inc(out_free[k % 2], 16)

            def shift(c, k):
                wait_apart(sp, setup_pool, score_ev, 2 * c + 2)
                sp.dma_start(shear[0:P * PITCH].rearrange("(n h m) -> n h m", h=NH, m=SLOT)[:, :, HALF:SLOT],
                             score[k % 2][:]).then_inc(shear_out, 16)
                wait_apart(sp, setup_pool, shear_out, 16 * c + 16)
                wait_apart(sp, setup_pool, probT_mm, 3 * c - 9)
                if isinstance(c, int) and c == 3:
                    sp.wait_ge(zeros_out, 16)
                sp.dma_start(prob[k][:, :, 0:BAND],
                             bass.AP(shear.tensor, 0, [[PITCH + 1, P], [SLOT, NH], [1, BAND]])).then_inc(band_in, 16)

            def load_raw(e, c):
                value = 176 * e + 64 * c
                if not isinstance(value, int) or value > 0:
                    wait_apart(sp, setup_pool, split_out, value)
                sp.dma_start(up_raw[0:DC], dram["wi"][bass.ds(e, 1), c * DC:(c + 1) * DC, :].rearrange("o p f -> (o p) f")
                             ).then_inc(raw_in, 16)
                if c:
                    sp.dma_start(up_raw[DC:DC + 1], dram["bi"][bass.ds(e, 1), :]).then_inc(raw_in, 16)

            def store_split(e, c):
                wait_apart(sp, setup_pool, raw_lo_done, 2 * e + c + 1)
                hi, lo = up_hi, up_raw
                if c == 0:
                    parts = ((hi, 0, 96, 0, 0), (hi, 0, 64, 1, 64), (hi, 64, 96, 2, 0), (lo, 0, 96, 3, 0))
                else:
                    parts = ((hi, 0, 32, 0, 96), (hi, 32, 96, 1, 0), (hi, 0, 96, 2, 32), (lo, 0, 32, 3, 96),
                             (lo, 32, 96, 4, 0), (hi, 96, 97, 4, 64), (lo, 96, 97, 4, 96))
                for src, r0, r1, chunk, at in parts:
                    sp.dma_start(dram["w_up"][bass.ds(e, 1), chunk, at:at + r1 - r0, :].rearrange("o p f -> (o p) f"),
                                 src[r0:r1].bitcast(f32)).then_inc(split_out, 16)

            def load_up(e):
                if e < 2:
                    for m in range(2):
                        sp.wait_ge(qk_mm[m], 6 * NG)
                elif e == 2:
                    for m in range(2):
                        sp.wait_ge(v_mm[m], B)
                elif e < 5:
                    sp.wait_ge(score_mm, 2 * B)
                    sp.wait_ge(shear_out, 16 * B)
                elif e == 5:
                    sp.wait_ge(split_out, 176 * NE)
                    sp.wait_ge(probT_mm, 3 * (B - 3))
                elif e == 6:
                    sp.wait_ge(probT_mm, 3 * (B - 1))
                    sp.wait_ge(oT_mm, 2 * (B - 3))
                else:
                    sp.wait_ge(probT_mm, 3 * B)
                    sp.wait_ge(oT_mm, 2 * B)
                sp.dma_start(w_in_all[:, e].bitcast(f32), dram["w_up"][e].rearrange("c p f -> p c f")
                             ).then_inc(w_in_done, 16)

            def group(g):
                n = 4 * g
                if exists(n + 4):
                    for k in range(G):
                        wait_apart(sp, setup_pool, agg_mm, n + k + 1)
                        load_graph(n + 4 + k, k)
                for k in range(G):
                    c = n + k
                    if exists(c - 4):
                        store_h2(c - 4, k)
                    if exists(c - 1):
                        wait_apart(sp, setup_pool, band_in, 16 * c)
                    if exists(c - 2) and k % 2 == 0:
                        store_split(*((g, 0) if k else (g - 1, 1)))
                    if exists(c):
                        shift(c, k)
                    if exists(c) and k % 2 == 0:
                        load_raw(g, k // 2)
                    if isinstance(g, int):
                        for e in range(EARLY_EXPERTS):
                            if LOAD_AT[e] == c:
                                load_up(e)

            group(0)
            group(1)
            with sp.Fori(2, NG - 1) as g:
                group(g)
            group(NG - 1)
            group(NG)
            group(NG + 1)
            sp.wait_ge(split_out, 176 * NE)
            sp.wait_ge(w_in_done, 16 * EARLY_EXPERTS)
            for k in range(2):
                sp.wait_ge(out_free[k], 16 * (B // 2 + 1))

        @block.gpsimd
        def _(pool):
            setup = [0]

            def made(ins):
                setup[0] += 1
                ins.then_inc(setup_pool, 1)
                pool.wait_ge(setup_pool, setup[0])

            made(pool.memset(ids[:, B:B + G], 0))
            pool.wait_ge(ids_in, 32)
            pool.tensor_copy(ids4[:], ids[:, 0:G]).then_inc(staged, 1)
            pool.wait_ge(staged, 1)

            def gather(k):
                pool.indirect_dma_start(tok[k][:], None, dram["tok_emb"],
                                        bass.IndirectOffsetOnAxis(ap=ids4[:, k:k + 1], axis=0)).then_inc(tok_in[k], 16)

            for k in range(G):
                gather(k)
            made(pool.memset(seg_i[:, B:B + G], 0))
            made(pool.tensor_copy(seg_f[:], seg_i[:]))
            pool.tensor_copy(seg4[:], seg_f[:, 0:G]).then_inc(staged, 1)
            made(pool.memset(minus_half[:], -0.5))
            pool.wait_ge(emb_in, 16 * 3)
            made(pool.tensor_tensor(seg0_pos[:], seg0_pos[:], seg0[:], ALU.add))
            made(pool.tensor_tensor(seg_diff[:], seg_diff[:], seg0[:], ALU.subtract))
            assert setup[0] == EARLY
            def embed(a, k):
                wait_apart(pool, setup_pool, agg_mm, a - 1)
                wait_apart(pool, setup_pool, h0_done, 3 * a - 5)
                wait_apart(pool, setup_pool, seg_done, a + 1)
                pool.tensor_tensor(seg_pos[k % 2][:], seg_part[k % 2][:], seg0_pos[:], ALU.add).then_inc(emb_done, 1)
                wait_apart(pool, setup_pool, emb_done, 2 * a + 1)
                wait_apart(pool, setup_pool, tok_in[k], 4 * (a - k) + 16)
                pool.tensor_tensor(emb[k % 2][:], tok[k][:], seg_pos[k % 2][:], ALU.add).then_inc(emb_done, 1)

            def rstd(var_sem, value, mv, ve, out_, eps, done, n):
                wait_apart(pool, setup_pool, var_sem, value)
                pool.tensor_scalar(ve[:], mv[:, 1:2], eps, None, ALU.add).then_inc(done, 1)
                wait_apart(pool, setup_pool, done, 2 * n + 1)
                pool.tensor_tensor(out_[:], ve[:], minus_half[:], ALU.pow).then_inc(done, 1)

            def rstd0(a):
                rstd(h0_done, 3 * a + 3, h_mv, h_ve, h_rstd, 1e-12, h0_rstd, a)

            def affine(a, k):
                wait_apart(pool, setup_pool, hn_done, a + 1)
                pool.tensor_tensor(hg[:], hn[:], gamma[:], ALU.mult).then_inc(h1_done, 1)
                wait_apart(pool, setup_pool, h1_done, 2 * a + 1)
                pool.tensor_tensor(h1[k % 2][:], hg[:], beta[:], ALU.add).then_inc(h1_done, 1)

            def keep(a, k):
                wait_apart(pool, setup_pool, h1_done, 2 * a + 2)
                pool.tensor_tensor(h_res[:, bass.ds(a, 1), :].rearrange("p o d -> p (o d)"), h1[k % 2][:],
                                   attn_bo[:], ALU.add).then_inc(kept, 1)

            def rstd1_(a):
                rstd(h1_stat, 2 * a + 2, mv1, ve1, rstd1, 1e-5, h1_rstd, a)

            def low_part(a, k):
                wait_apart(pool, setup_pool, x_done, 3 * a + 3)
                flat = x_cat[k % 2][:].rearrange("p c s -> p (c s)")
                pool.tensor_tensor(flat[:, D:2 * D], x_full[:], flat[:, 0:D], ALU.subtract).then_inc(x_lo, 1)

            def stage_seg(g):
                wait_apart(pool, setup_pool, seg_done, 4 * g + 4)
                pool.tensor_copy(seg4[:], seg_f[:, bass.ds(4 * g + 4, G)]).then_inc(staged, 1)
                wait_apart(pool, setup_pool, staged, 2 * g + 4)

            def stage_ids(g):
                pool.tensor_copy(ids4[:], ids[:, bass.ds(4 * g + 8, G)]).then_inc(staged, 1)
                wait_apart(pool, setup_pool, staged, 2 * g + 5)

            def subtract_max(n, k):
                wait_apart(pool, setup_pool, max_done, 2 * n + 2)
                band = prob[k][:, :, 0:BAND]
                pool.tensor_tensor(band, band, all_heads(band_max0[k % 2]), ALU.subtract).then_inc(sub_done, 1)

            def low_raw(e, c):
                wait_apart(pool, setup_pool, raw_hi_done, 2 * e + c + 1)
                pool.tensor_tensor(up_raw[0:DC + c].bitcast(f32r), up_raw[0:DC + c], up_hi[0:DC + c].bitcast(f32),
                                   ALU.subtract).then_inc(raw_lo_done, 1)

            def rstd2_(n):
                rstd(h2_done, 3 * n + 3, mv2, ve2, rstd2, 1e-5, h2_rstd, n)

            def scatter(n, k):
                wait_apart(pool, setup_pool, placed, 9 * n + 9)
                pool.tensor_copy(row_a[k % 2][:, D + 1:D + 2], token_no[:, bass.ds(n, 1)]).then_inc(row_done, 1)
                wait_apart(pool, setup_pool, rowb_x, n + 1)
                pool.tensor_copy(row_b[k % 2][:, D + 1:D + 2], token_no[:, bass.ds(n, 1)]).then_inc(row_done, 1)
                wait_apart(pool, setup_pool, row_done, 2 * n + 2)
                for row, free, c in ((row_a, rowa_free, 0), (row_b, rowb_free, 1)):
                    pool.indirect_dma_start(rows, bass.IndirectOffsetOnAxis(ap=pos[k % 2][:, c:c + 1], axis=0),
                                            row[k % 2][:], None).then_inc(free[k % 2], 16)

            pool.wait_ge(staged, 2)
            embed(0, 0)
            embed(1, 1)
            made(pool.memset(ident[:], 0.0))
            made(pool.affine_select(out=ident[:], in_=ident[:], compare_op=ALU.not_equal, fill=1.0, base=0,
                                    pattern=[[-1, P]], channel_multiplier=1))
            for k in range(2):
                made(pool.memset(x_cat[k][:, 3, :], 0.0))
                made(pool.memset(x_cat[k][:, 3, 64:65], 1.0))
                made(pool.memset(x_cat[k][:, 3, 96:97], 1.0))
            made(pool.iota(expert_i[:], pattern=[[1, NE]], base=0, channel_multiplier=0))
            made(pool.tensor_copy(expert_no[:], expert_i[:]))
            made(pool.iota(token_i[:], pattern=[[S, B]], base=0, channel_multiplier=1))
            made(pool.tensor_copy(token_no[:], token_i[:]))
            made(pool.tensor_scalar(route[:], expert_no[:], float(REGION), None, ALU.mult))
            made(pool.memset(ones_bf[:], 1.0))
            made(pool.memset(before[:], 1.0))
            made(pool.affine_select(out=before[:], in_=before[:], compare_op=ALU.is_ge, fill=0.0, base=-1,
                                    pattern=[[1, P]], channel_multiplier=-1))
            made(pool.memset(prob[0][:, :, 0:HALF], 0.0))
            made(pool.memset(zeros, 0.0))
            assert setup[0] == CONSTANTS
            for k in range(G + 2):
                if 2 <= k < G:
                    embed(k, k)
                if 0 < k <= G:
                    rstd0(k - 1)
                if k == 1:
                    pool.wait_ge(const_in, 16 * 5)
                if 1 < k:
                    rstd1_(k - 2)
                if 0 < k <= G:
                    affine(k - 1, k - 1)
                if 1 < k:
                    low_part(k - 2, k - 2)
                if 0 < k <= G:
                    keep(k - 1, k - 1)
            low_part_of("v", v, pool, wv_lo)
            pool.wait_ge(wv_lo, 3)
            for i, free in enumerate(rowa_free + rowb_free):
                pool.dma_start(rows[NOWHERE + i:NOWHERE + i + 1, 0:P], ident[0:1, :]).then_inc(free, 16)
            pool.iota(tile_i[:], pattern=[[1, TILES]], base=0, channel_multiplier=0).then_inc(later, 1)
            pool.iota(step_i[:], pattern=[[P, STEPS]], base=0, channel_multiplier=0).then_inc(later, 1)
            pool.memset(filler[:], 0.0).then_inc(later, 1)
            pool.wait_ge(later, 3)
            pool.tensor_copy(tile_no[:], tile_i[:]).then_inc(later, 1)
            pool.tensor_scalar(base[:], expert_no[:], float(REGION), None, ALU.mult).then_inc(later, 1)
            pool.tensor_copy(step[:], step_i[:]).then_inc(later, 1)
            pool.memset(filler[:, D + 1:D + 2], float(NO_TOKEN)).then_inc(later, 1)
            pool.wait_ge(later, 4)
            pool.tensor_scalar(tile_row[:], tile_no[:], float(P), None, ALU.mult).then_inc(later, 1)

            pool.wait_ge(emb_done, 2 * G)
            pool.tensor_copy(ids4[:], ids[:, G:2 * G]).then_inc(staged, 1)
            pool.wait_ge(staged, 3)
            for k in range(G):
                gather(k)

            def group(g):
                n = 4 * g
                a = n + 4
                more = exists(a)
                if more:
                    stage_seg(g)
                for k in range(G):
                    c = n + k
                    first = (0, 1, 3, 3)[k]
                    if exists(c - 1):
                        subtract_max(c - 1, (k + 3) % G)
                    if more and k == 0:
                        embed(a, 0)
                    if more and k:
                        low_part(a + (0, 0, 1, 3)[k], (0, 0, 1, 3)[k])
                    if more and k == 2:
                        affine(a + 2, 2)
                    if exists(c - 5):
                        scatter(c - 5, (k + 3) % G)
                    if more and k < 2:
                        embed(a + k + 1, k + 1)
                        rstd0(a + k)
                        affine(a + k, k)
                    if more and k == 2:
                        rstd1_(a + 2)
                        rstd0(a + 3)
                    if exists(c - 3):
                        rstd2_(c - 3)
                    if more and k == 0:
                        rstd1_(a)
                        keep(a, 0)
                    if more and k == 1:
                        rstd0(a + 2)
                        rstd1_(a + 1)
                        keep(a + 1, 1)
                        embed(a + 3, 3)
                    if more and k == 2:
                        affine(a + 3, 3)
                        keep(a + 2, 2)
                        low_part(a + 2, 2)
                        rstd1_(a + 3)
                        keep(a + 3, 3)
                    if more and k == 3:
                        stage_ids(g)
                        for j in range(G):
                            gather(j)
                    if exists(n) and k in (1, 3):
                        low_raw(g, k // 2)

            group(0)
            group(1)
            with pool.Fori(2, NG - 1) as g:
                group(g)
            group(NG - 1)
            group(NG)
            group(NG + 1)
            for k in range(G):
                pool.wait_ge(tok_in[k], 16 * (NG + 1))
            for k in range(2):
                pool.wait_ge(rowa_free[k], 16 * (B // 2 + 1))
                pool.wait_ge(rowb_free[k], 16 * (B // 2 + 1))

        @block.scalar
        def _(act):
            def segment(a, k):
                wait_count(act, emb_done, 2 * a - 3)
                act.activation(seg_part[k % 2][:], seg_diff[:], ACT.Copy, scale=seg4[:, k:k + 1]).then_inc(seg_done, 1)

            def agg(a):
                act.wait_ge(agg_mm, a + 1)
                if not isinstance(a, int) or a:
                    act.wait_ge(proj_mm, a)
                act.activation(aggT[0:DC], ps_agg, ACT.Copy).then_inc(agg_ev, 1)

            def x_t(a, k):
                act.wait_ge(xt_mm, a + 1)
                act.activation(xT[:, :, k * S:(k + 1) * S], ps_x[:].rearrange("p (c s) -> p c s", s=S),
                               ACT.Copy).then_inc(xt_ev, 1)

            def high(m, raw):
                act.wait_ge(w_in[m], 16 * 6)
                act.activation(w_split[m][:, 0:3, :].rearrange("p c n -> p (c n)"),
                               raw[:].rearrange("p a b -> p (a b)")[:, 0:3 * A], ACT.Copy).then_inc(w_hi, 1)
                act.wait_ge(setup_dve, 4)
                for p in (64, 96):
                    act.activation(w_split[m][p:p + 1, 4, :], bias_row[m][p:p + 1, :], ACT.Copy).then_inc(w_hi, 1)

            def qk(g, t):
                act.wait_ge(qk_mm[0], 6 * g + t + 1)
                j = 2 * t
                dst = (qT if j < 6 else kT)[:, j % 6, :]
                act.activation(dst, ps_qk[0], ACT.Copy).then_inc(qk_ev[0], 1)

            def v_low(n, k):
                act.wait_ge(v_mm[0], n + 1)
                act.activation(v[:, k, 0:A // 2], ps_v[0][:, 0:A // 2], ACT.Copy).then_inc(v_ev[0], 1)

            def scores(n, k, units=(0, 1)):
                if 0 in units:
                    wait_count(act, shear_out, 16 * n - 16)
                by_bank = score[k % 2][:].rearrange("p (i o) s -> p o i s", o=2)
                for u in units:
                    i0, i1 = HEAD_PAIRS[u]
                    act.wait_ge(score_mm, 2 * n + u + 1)
                    act.activation(by_bank[:, :, i0:i1, :], ps_score[:, :, 0:i1 - i0, :], ACT.Copy).then_inc(score_ev, 1)

            def exps(n, k):
                act.wait_ge(sub_done, n + 1)
                band = prob[k][:, :, 0:BAND]
                act.activation(band, band, ACT.Exp).then_inc(exp_done, 1)
                wait_count(act, norm_done, 5 * n - 5)
                act.activation(e_zero[k % 2][:], band_max0[k % 2][:], ACT.Exp, scale=-1.0).then_inc(exp_done, 1)

            def prob_t(n, k, u):
                act.wait_ge(probT_mm, 3 * n + u + 1)
                act.activation(probT[:, 4 * u:4 * u + 4, :], ps_probT[(3 * k + u) % 2][:].rearrange("p (h s) -> p h s", s=S),
                               ACT.Copy).then_inc(probT2_ev, 1)

            def fill(n, k):
                act.wait_ge(norm_done, 5 * n + 4)
                act.activation(prob[k][:, :, BAND:S], all_heads(p_zero, S - BAND), ACT.Copy).then_inc(fill_done, 1)

            def high_raw(e, c):
                act.wait_ge(raw_in, 48 * e + (16, 48)[c])
                act.activation(up_hi[0:DC + c], up_raw[0:DC + c], ACT.Copy).then_inc(raw_hi_done, 1)

            def copy_row(n, k):
                act.wait_ge(x2_done, n + 1)
                act.wait_ge(rowb_free[k % 2], 8 * (n - k) + 16 * (k // 2) + 16)
                act.activation(row_b[k % 2][:, 0:D], row_a[k % 2][:, 0:D], ACT.Copy).then_inc(rowb_x, 1)

            def o_t(n, half):
                act.wait_ge(oT_mm, 2 * n + half + 1)
                c0, c1 = ((0, 4), (4, 6))[half]
                act.activation(oT[:, c0:c1, :], ps_oT[:, c0:c1, :], ACT.Copy).then_inc(oT_ev, 1)

            def x2_t(n):
                act.wait_ge(x2T_mm, n + 1)
                act.activation(x2T[:], ps_x2T, ACT.Copy).then_inc(x2T_ev, 1)

            def exp_gap(n):
                act.wait_ge(choice, 8 * n + 8)
                act.activation(e_gap[:], gap[:], ACT.Exp).then_inc(e_gap_done, 1)

            act.wait_ge(setup_pool, EARLY)
            act.wait_ge(staged, 2)
            segment(0, 0)
            segment(1, 1)
            agg(0)
            high("q", qT)
            segment(2, 2)
            agg(1)
            high("k", kT)
            segment(3, 3)
            agg(2)
            x_t(0, 0)
            high("v", v)
            agg(3)
            x_t(1, 1)
            x_t(2, 2)
            x_t(3, 3)
            for t in range(6):
                qk(0, t)

            def group(g):
                n = 4 * g
                a = n + 4
                more = exists(a)
                for k in range(G):
                    c = n + k
                    first = (0, 1, 3, 3)[k]
                    k1, k2, k3 = (k + 3) % G, (k + 2) % G, (k + 1) % G
                    if more and k == 0:
                        act.wait_ge(staged, 2 * g + 4)
                        segment(a, 0)
                    if more and k < 3:
                        segment(a + k + 1, k + 1)
                    if exists(c):
                        scores(c, k, (0,))
                    if exists(c - 3):
                        prob_t(c - 3, k3, 1)
                    if exists(c):
                        v_low(c, k)
                    if exists(n) and k in (1, 3):
                        high_raw(g, k // 2)
                    if exists(c - 4):
                        x2_t(c - 4)
                    if exists(c):
                        scores(c, k, (1,))
                    if more and k < 3:
                        agg(a + first)
                    if exists(c - 1):
                        exps(c - 1, k1)
                    if exists(c - 3):
                        prob_t(c - 3, k3, 2)
                        o_t(c - 3, 0)
                    if more and k == 3:
                        x_t(a + 2, 2)
                    if exists(c - 3):
                        o_t(c - 3, 1)
                    if more and k:
                        x_t(a + (0, 0, 1, 3)[k], (0, 0, 1, 3)[k])
                    if more and k == 1:
                        agg(a + 2)
                    if more and k == 3:
                        qk(g + 1, 0)
                    if exists(c - 2):
                        fill(c - 2, k2)
                    if exists(c - 4):
                        copy_row(c - 4, k)
                        exp_gap(c - 4)
                    if more and k == 3:
                        for t in range(1, 6):
                            qk(g + 1, t)

            group(0)
            group(1)
            with act.Fori(2, NG - 1) as g:
                group(g)
            group(NG - 1)
            group(NG)
            group(NG + 1)

        @block.vector
        def _(dve):
            def residual(a, k):
                dve.wait_ge(proj_mm, a + 1)
                wait_count(dve, hn_done, a)
                dve.tensor_tensor(h0[:], ps_proj, emb[k % 2][:], ALU.add).then_inc(h0_done, 1)
                dve.wait_ge(h0_done, 3 * a + 1)
                dve.bn_stats(h_stats[:], h0[:]).then_inc(h0_done, 1)
                wait_apart(dve, setup_pool, h0_done, 3 * a + 2)
                dve.bn_aggr(h_mv[:], h_stats[:]).then_inc(h0_done, 1)

            def norm0(a):
                dve.wait_ge(h0_rstd, 2 * a + 2)
                dve.tensor_scalar(hn[:], h0[:], h_mv[:, 0:1], h_rstd[:, 0:1], ALU.subtract, ALU.mult).then_inc(hn_done, 1)

            def stat1(a, k):
                dve.wait_ge(h1_done, 2 * a + 2)
                dve.bn_stats(stats1[:], h1[k % 2][:]).then_inc(h1_stat, 1)
                wait_apart(dve, setup_pool, h1_stat, 2 * a + 1)
                dve.bn_aggr(mv1[:], stats1[:]).then_inc(h1_stat, 1)

            def x_parts(a, k):
                dve.wait_ge(h1_rstd, 2 * a + 2)
                if k >= 2 or not isinstance(a, int):
                    dve.wait_ge(xt_mm, a - 1)
                cat = x_cat[k % 2][:].rearrange("p c s -> p (c s)")
                dve.tensor_scalar(cat[:, 0:D].bitcast(f32r), h1[k % 2][:], mv1[:, 0:1], rstd1[:, 0:1],
                                  ALU.subtract, ALU.mult).then_inc(x_done, 1)
                dve.tensor_scalar(cat[:, 2 * D:2 * D + 64].bitcast(f32r), h1[k % 2][:, P:D], mv1[:, 0:1], rstd1[:, 0:1],
                                  ALU.subtract, ALU.mult).then_inc(x_done, 1)
                dve.tensor_scalar(x_full[:], h1[k % 2][:], mv1[:, 0:1], rstd1[:, 0:1],
                                  ALU.subtract, ALU.mult).then_inc(x_done, 1)

            def qk(g, t):
                dve.wait_ge(qk_mm[1], 6 * g + t + 1)
                j = 2 * t + 1
                dst = (qT if j < 6 else kT)[:, j % 6, :]
                dve.tensor_copy(dst, ps_qk[1]).then_inc(qk_ev[1], 1)

            def v_high(n, k):
                dve.wait_ge(v_mm[1], n + 1)
                dve.tensor_copy(v[:, k, A // 2:A], ps_v[1][:, 0:A // 2]).then_inc(v_ev[1], 1)

            def maximum(n, k):
                dve.wait_ge(band_in, 16 * n + 16)
                wait_count(dve, exp_done, 2 * n - 2)
                dve.tensor_reduce(band_max[:], prob[k][:, :, 0:BAND], AX.X, ALU.max).then_inc(max_done, 1)
                dve.wait_ge(max_done, 2 * n + 1)
                dve.tensor_scalar(band_max0[k % 2][:], band_max[:], 0.0, None, ALU.max).then_inc(max_done, 1)

            def normalise(n, k):
                dve.wait_ge(exp_done, 2 * n + 2)
                band = prob[k][:, :, 0:BAND]
                dve.tensor_reduce(band_sum[:], band, AX.X, ALU.add).then_inc(norm_done, 1)
                dve.wait_ge(norm_done, 5 * n + 1)
                dve.scalar_tensor_tensor(denom[:], e_zero[k % 2][:], float(S - BAND), band_sum[:],
                                         ALU.mult, ALU.add).then_inc(norm_done, 1)
                dve.wait_ge(norm_done, 5 * n + 2)
                dve.reciprocal(r_denom[:], denom[:]).then_inc(norm_done, 1)
                dve.wait_ge(norm_done, 5 * n + 3)
                wait_count(dve, fill_done, n)
                dve.tensor_tensor(p_zero[:], e_zero[k % 2][:], r_denom[:], ALU.mult).then_inc(norm_done, 1)
                dve.tensor_tensor(band, band, all_heads(r_denom), ALU.mult).then_inc(norm_done, 1)

            def prob_t(n, k):
                dve.wait_ge(probT_mm, 3 * n + 1)
                dve.tensor_copy(probT[:, 0:4, :], ps_probT[(3 * k) % 2][:].rearrange("p (h s) -> p h s", s=S)).then_inc(probT_ev, 1)

            def residual2(n, k):
                dve.wait_ge(attn_mm, n + 1)
                dve.wait_ge(kept, n + 1)
                dve.wait_ge(out_free[k % 2], 8 * (n - k) + 16 * (k // 2) + 16)
                dve.tensor_tensor(h2[k % 2][:], ps_attn, h_res[:, bass.ds(n, 1), :].rearrange("p o d -> p (o d)"),
                                  ALU.add).then_inc(h2_done, 1)
                dve.wait_ge(h2_done, 3 * n + 1)
                dve.bn_stats(stats2[:], h2[k % 2][:]).then_inc(h2_done, 1)
                wait_apart(dve, setup_pool, h2_done, 3 * n + 2)
                dve.bn_aggr(mv2[:], stats2[:]).then_inc(h2_done, 1)

            def norm2(n, k):
                dve.wait_ge(h2_rstd, 2 * n + 2)
                dve.wait_ge(rowa_free[k % 2], 8 * (n - k) + 16 * (k // 2) + 16)
                dve.tensor_scalar(row_a[k % 2][:, 0:D], h2[k % 2][:], mv2[:, 0:1], rstd2[:, 0:1],
                                  ALU.subtract, ALU.mult).then_inc(x2_done, 1)

            def choose(n):
                dve.wait_ge(logit_mm, n + 1)
                dve.tensor_copy(logits[:], ps_logits).then_inc(choice, 1)
                wait_apart(dve, setup_pool, choice, 8 * n + 1)
                dve.max(top[:], logits[:]).then_inc(choice, 1)
                wait_apart(dve, setup_pool, choice, 8 * n + 2)
                dve.max_index(top_i[:], top[:], logits[:]).then_inc(choice, 1)
                dve.wait_ge(choice, 8 * n + 3)
                dve.tensor_copy(top_f[:], top_i[:, 0:2]).then_inc(choice, 1)
                dve.wait_ge(choice, 8 * n + 4)
                dve.tensor_scalar(is_1[:], expert_no[:], top_f[:, 0:1], None, ALU.is_equal).then_inc(choice, 1)
                dve.tensor_scalar(is_2[:], expert_no[:], top_f[:, 1:2], None, ALU.is_equal).then_inc(choice, 1)
                dve.wait_ge(choice, 8 * n + 6)
                dve.tensor_tensor(is_any[:], is_1[:], is_2[:], ALU.add).then_inc(choice, 1)
                dve.tensor_tensor(gap[:], top[:, 1:2], top[:, 0:1], ALU.subtract).then_inc(choice, 1)

            def place(n, k):
                dve.wait_ge(rank_mm, n + 1)
                dve.wait_ge(rank_free, n + 1)
                dve.tensor_tensor(where[:], ps_rank, route[:], ALU.add).then_inc(placed, 1)
                dve.tensor_tensor(route[:], ps_total, route[:], ALU.add).then_inc(rank_free, 1)
                dve.wait_ge(placed, 9 * n + 1)
                dve.tensor_tensor(pick1[:], where[:], is_1[:], ALU.mult).then_inc(placed, 1)
                dve.tensor_tensor(pick2[:], where[:], is_2[:], ALU.mult).then_inc(placed, 1)
                dve.wait_ge(placed, 9 * n + 3)
                dve.tensor_reduce(pos_f[:, 0:1], pick1[:], AX.X, ALU.add).then_inc(placed, 1)
                dve.tensor_reduce(pos_f[:, 1:2], pick2[:], AX.X, ALU.add).then_inc(placed, 1)
                dve.wait_ge(placed, 9 * n + 5)
                dve.wait_ge(rowb_free[k % 2], 8 * (n - k) + 16 * (k // 2) + 16)
                dve.tensor_copy(pos[k % 2][:], pos_f[:]).then_inc(placed, 1)
                dve.wait_ge(e_gap_done, n + 1)
                dve.tensor_scalar(one_e[:], e_gap[:], 1.0, None, ALU.add).then_inc(placed, 1)
                dve.wait_ge(placed, 9 * n + 7)
                dve.reciprocal(row_a[k % 2][:, D:D + 1], one_e[:]).then_inc(placed, 1)
                dve.wait_ge(placed, 9 * n + 8)
                dve.tensor_tensor(row_b[k % 2][:, D:D + 1], row_a[k % 2][:, D:D + 1], e_gap[:], ALU.mult).then_inc(placed, 1)

            dve.sem_inc(rank_free, 1)
            for s_ in out_free:
                dve.sem_inc(s_, 16)
            dve.memset(aggT[DC:DC + 1], 1.0).then_inc(setup_dve, 1)
            for m in "qkv":
                dve.memset(w_split[m][64:P, 4, :].bitcast(f32), 0.0).then_inc(setup_dve, 1)
            for k in range(G + 1):
                if k < G:
                    residual(k, k)
                if k:
                    stat1(k - 1, k - 1)
                if k < G:
                    norm0(k)
                if k == 1:
                    dve.wait_ge(setup_pool, CONSTANTS)
                if k:
                    x_parts(k - 1, k - 1)
                if k in (1, 2):
                    low_part_of("qk"[k - 1], (qT, kT)[k - 1], dve, w_lo)
            for t in range(6):
                qk(0, t)

            def group(g):
                n = 4 * g
                a = n + 4
                more = exists(a)
                for k in range(G):
                    c = n + k
                    first = (0, 1, 3, 3)[k]
                    k1, k2, k3 = (k + 3) % G, (k + 2) % G, (k + 1) % G
                    if exists(c - 3):
                        prob_t(c - 3, k3)
                    if exists(c - 1):
                        maximum(c - 1, k1)
                    if exists(c - 5):
                        place(c - 5, k1)
                    if exists(c - 4):
                        norm2(c - 4, k)
                    if more and k == 2:
                        norm0(a + 2)
                    if exists(c):
                        v_high(c, k)
                    if more and k:
                        x_parts(a + (0, 0, 1, 3)[k], (0, 0, 1, 3)[k])
                    if exists(c - 2):
                        normalise(c - 2, k2)
                    if more and k == 2:
                        stat1(a + 2, 2)
                    if more and k < 3:
                        residual(a + first, first)
                    if exists(c - 4):
                        choose(c - 4)
                    if more and k == 3:
                        qk(g + 1, 0)
                    if more and k < 3:
                        norm0(a + first)
                    if exists(c - 3):
                        residual2(c - 3, k3)
                    if more and k == 3:
                        qk(g + 1, 1)
                    if more and k == 2:
                        x_parts(a + 2, 2)
                    if more and k == 1:
                        residual(a + 2, 2)
                    if more and k < 3:
                        stat1(a + first, first)
                    if more and k == 3:
                        for t in range(2, 6):
                            qk(g + 1, t)

            group(0)
            group(1)
            with dve.Fori(2, NG - 1) as g:
                group(g)
            group(NG - 1)
            group(NG)
            group(NG + 1)

            planned = [0]

            def step_of(ins):
                planned[0] += 1
                ins.then_inc(plan, 1)
                dve.wait_ge(plan, planned[0])

            def per_expert(t_):
                return t_[:].unsqueeze(1).broadcast_to([P, TILES, NE])

            dve.wait_ge(later, 8)
            dve.wait_ge(rank_free, B + 1)
            step_of(dve.tensor_copy(end_of[:], route[:]))
            step_of(dve.tensor_tensor(count[:], route[:], base[:], ALU.subtract))
            step_of(dve.tensor_tensor(over[:], count[:].unsqueeze(2).broadcast_to([P, NE, STEPS]),
                                      step[:].unsqueeze(1).broadcast_to([P, NE, STEPS]), ALU.is_gt))
            step_of(dve.tensor_reduce(tiles[:], over[:], AX.X, ALU.add))
            step_of(dve.tensor_copy(upto[0][:], tiles[:]))
            for i in range(3):
                d = 1 << i
                step_of(dve.tensor_copy(upto[i + 1][:, 0:d], upto[i][:, 0:d]))
                step_of(dve.tensor_tensor(upto[i + 1][:, d:NE], upto[i][:, d:NE], upto[i][:, 0:NE - d], ALU.add))
            step_of(dve.tensor_scalar(jump[:], tiles[:], float(-P), float(REGION), ALU.mult, ALU.add))
            step_of(dve.tensor_tensor(passed, tile_no[:].unsqueeze(2).broadcast_to([P, TILES, NE]),
                                      per_expert(upto[3]), ALU.is_ge))
            step_of(dve.tensor_reduce(owner[:], passed, AX.X, ALU.add))
            step_of(dve.tensor_scalar(expert_of[:], owner[:], float(NE - 1), None, ALU.min))
            step_of(dve.tensor_tensor(jumps, passed, per_expert(jump), ALU.mult))
            step_of(dve.tensor_reduce(offset[:], jumps, AX.X, ALU.add))
            step_of(dve.tensor_tensor(row_f[:], offset[:], tile_row[:], ALU.add))
            step_of(dve.tensor_scalar(row_of[:], row_f[:], float(NOWHERE), None, ALU.min))

        @block.tensor
        def _(pe):
            def mix(a, k, c):
                pe.wait_ge(emb_done, 2 * a + 2)
                pe.wait_ge(graph_in[k], 4 * (a - k) + 16)
                wait_count(pe, h0_done, 3 * a - 2)
                if c is not None:
                    pe.wait_ge(v_ev[0], c + 1)
                    if exists(c - 4):
                        pe.wait_ge(x2T_ev, c - 3)
                for c in range(2):
                    mm = pe.matmul(ps_agg[:, c, :], emb[k % 2][:, c * DC:(c + 1) * DC], graph[k][:], start=True, stop=True)
                mm.then_inc(agg_mm, 1)

            def project(a):
                pe.wait_ge(agg_ev, a + 1)
                for c in range(2):
                    mm = pe.matmul(ps_proj, aggT[0:DC + c, c, :], w_dense[0:DC + c, c, :], start=c == 0, stop=c == 1)
                mm.then_inc(proj_mm, 1)

            def turn_x(a, k, c=None):
                pe.wait_ge(x_lo, a + 1)
                wait_count(pe, xt_ev, a)
                if c is not None:
                    pe.wait_ge(v_ev[1], c + 1)
                    if exists(c - 4):
                        pe.wait_ge(choice, 8 * c - 31)
                for c in range(4):
                    mm = pe.transpose(ps_x[:, c * S:(c + 1) * S], x_cat[k % 2][:, c, :], ident[:])
                mm.then_inc(xt_mm, 1)

            def qk(g, j):
                bank, t = j % 2, j // 2
                if t == 0:
                    pe.wait_ge(xt_ev, 4 * g + 4)
                if t:
                    pe.wait_ge(qk_ev[bank], 6 * g + t)
                elif not isinstance(g, int) or g:
                    pe.wait_ge(score_ev, 8 * g)
                m = "q" if j < 6 else "k"
                for i, (cx, cw) in enumerate(TERMS):
                    mm = pe.matmul(ps_qk[bank], w_split[m][:, cw, (j % 6) * P:(j % 6 + 1) * P], xT[:, cx, :],
                                   start=i == 0, stop=i == KC - 1)
                mm.then_inc(qk_mm[bank], 1)

            def values(n, k, half):
                for i, (cx, cw) in enumerate(TERMS):
                    mm = pe.matmul(ps_v[half][:, 0:A // 2], xT[:, cx, k * S:(k + 1) * S],
                                   w_split["v"][:, cw, half * (A // 2):(half + 1) * (A // 2)],
                                   start=i == 0, stop=i == KC - 1)
                mm.then_inc(v_mm[half], 1)

            def values_low(n, k, mixed):
                pe.wait_ge(h0_done, 3 * mixed - 2)
                if exists(n - 5):
                    pe.wait_ge(x2T_ev, n - 4)
                values(n, k, 0)

            def values_high(n, k, turned):
                pe.wait_ge(xt_ev, turned)
                if exists(n - 5):
                    pe.wait_ge(rank_free, n - 3)
                values(n, k, 1)

            def scores(g, k, u):
                n = 4 * g + k
                if k == 0 and u == 0:
                    pe.wait_ge(qk_ev[0], 6 * g + 6)
                    pe.wait_ge(qk_ev[1], 6 * g + 6)
                else:
                    pe.wait_ge(score_ev, 2 * n + u)
                i0, i1 = HEAD_PAIRS[u]
                for i in range(i0, i1):
                    for o in range(2):
                        mm = pe.matmul(ps_score[:, o, i - i0, :], qT[64 * o:64 * o + 64, i, k * S:(k + 1) * S],
                                       kT[64 * o:64 * o + 64, i, k * S:(k + 1) * S], start=True, stop=True)
                mm.then_inc(score_mm, 1)

            def turn_prob(n, k, u):
                i = 3 * k + u
                if u == 2:
                    pe.wait_ge(probT_ev, n + 1)
                else:
                    wait_count(pe, probT2_ev, 2 * n - 1 + u)
                if u == 0:
                    pe.wait_ge(norm_done, 5 * n + 5)
                    pe.wait_ge(fill_done, n + 1)
                for h in range(4 * u, 4 * u + 4):
                    mm = pe.transpose(ps_probT[i % 2][:, (h % 4) * S:(h % 4 + 1) * S], prob[k][:, h, :], ident[:])
                mm.then_inc(probT_mm, 1)

            def weigh(n, k, u):
                if u == 0:
                    pe.wait_ge(probT_ev, n + 1)
                else:
                    pe.wait_ge(probT2_ev, 2 * n + u)
                if u == 0:
                    pe.wait_ge(v_ev[0], n + 1)
                    pe.wait_ge(v_ev[1], n + 1)
                if u == 2:
                    wait_count(pe, h2_done, 3 * n - 2)
                for h in range(4 * u, 4 * u + 4):
                    r = 64 * (h % 2)
                    mm = pe.matmul(ps_oT[r:r + 64, h // 2, :], v[:, k, h * HD:(h + 1) * HD], probT[:, h, :],
                                   start=True, stop=True)
                if u:
                    mm.then_inc(oT_mm, 1)

            def output(n):
                pe.wait_ge(oT_ev, 2 * n + 2)
                for c in range(A // P):
                    mm = pe.matmul(ps_attn, oT[:, c, :], w_o[:, c, :], start=c == 0, stop=c == A // P - 1)
                mm.then_inc(attn_mm, 1)

            def turn_x2(n, k, mixed):
                pe.wait_ge(x2_done, n + 1)
                pe.wait_ge(h0_done, 3 * mixed - 2)
                if exists(n + 4):
                    pe.wait_ge(v_ev[0], n + 5)
                for c in range(2):
                    mm = pe.transpose(ps_x2T[:, c, :], row_a[k % 2][:, c * DC:(c + 1) * DC], ident[:])
                mm.then_inc(x2T_mm, 1)

            def router(n, turned):
                pe.wait_ge(x2T_ev, n + 1)
                pe.wait_ge(xt_ev, turned)
                if exists(n + 4):
                    pe.wait_ge(v_ev[1], n + 5)
                pe.wait_ge(rank_free, n + 1)
                for c in range(2):
                    mm = pe.matmul(ps_logits, x2T[:, c, :], w_router[:, c, :], start=c == 0, stop=c == 1)
                mm.then_inc(logit_mm, 1)

            def rank(n):
                pe.wait_ge(choice, 8 * n + 7)
                pe.matmul(ps_rank, before[:], is_any[:], start=True, stop=True)
                pe.matmul(ps_total, ones_bf[:], is_any[:], start=True, stop=True).then_inc(rank_mm, 1)

            pe.wait_ge(setup_dve, 1)
            pe.wait_ge(dense_in, 32)
            for k in range(G + 2):
                if k < G:
                    mix(k, k, None)
                    project(k)
                if k == 2:
                    pe.wait_ge(setup_pool, CONSTANTS)
                if 1 < k:
                    turn_x(k - 2, k - 2)
            pe.wait_ge(const_in, 16 * 5)
            pe.wait_ge(w_lo, 6)
            for j in range(12):
                qk(0, j)
            pe.wait_ge(wv_lo, 3)

            def group(g):
                n = 4 * g
                a = n + 4
                more = exists(a)
                for k in range(G):
                    c = n + k
                    first = (0, 1, 3, 3)[k]
                    k3 = (k + 1) % G
                    mixed = [a + j for j in (0, 1, 3, 4)] if more else [B] * 4
                    turned = [a + j for j in (0, 0, 1, 2)] if more else [B] * 4
                    if exists(c - 3):
                        turn_prob(c - 3, k3, 0)
                        turn_prob(c - 3, k3, 1)
                    if exists(c):
                        scores(g, k, 0)
                    if exists(c - 5):
                        rank(c - 5)
                    if exists(c):
                        values_low(c, k, mixed[k])
                    if exists(c - 3):
                        weigh(c - 3, k3, 0)
                    if exists(c):
                        values_high(c, k, turned[k])
                    if exists(c - 4):
                        turn_x2(c - 4, k, mixed[k])
                    if exists(c):
                        scores(g, k, 1)
                    if more and k < 3:
                        mix(a + first, first, c)
                    if exists(c - 3):
                        turn_prob(c - 3, k3, 2)
                    if exists(c - 4):
                        router(c - 4, turned[k])
                    if exists(c - 3):
                        weigh(c - 3, k3, 1)
                    if more and k < 3:
                        project(a + first)
                    if more and k == 3:
                        turn_x(a + 2, 2, c)
                    if exists(c - 3):
                        weigh(c - 3, k3, 2)
                    if more and k:
                        turn_x(a + (0, 0, 1, 3)[k], (0, 0, 1, 3)[k], c)
                    if more and k == 3:
                        qk(g + 1, 0)
                        qk(g + 1, 1)
                    if exists(c - 3):
                        output(c - 3)
                    if more and k == 1:
                        mix(a + 2, 2, c)
                        project(a + 2)
                    if more and k == 3:
                        for j in range(2, 12):
                            qk(g + 1, j)

            group(0)
            group(1)
            with pe.Fori(2, NG - 1) as g:
                group(g)
            group(NG - 1)
            group(NG)
            group(NG + 1)


def expert_block(nc, dram, shared):
    route, ident, tile_row, step, filler, row_of, expert_of, end_of, w_in_all = shared[:9]
    out, rows = dram["out"], dram["rows"]
    ctx = ExitStack()
    with ctx:
        def sb(name, shape, dt=f32):
            return ctx.enter_context(nc.sbuf_tensor("ffn_" + name, shape, dt))

        def sem(name):
            return ctx.enter_context(nc.semaphore("ffn_" + name))

        w_in = w_in_all
        w_out = sb("w_out", [P, NE, FC, D])
        out_b = sb("out_b", [P, NE, D])
        RING = 4
        x = [sb(f"x{k}", [P, ROW]) for k in range(RING)]
        tail = [sb(f"tail{k}", [P, ROW - D]) for k in range(RING)]
        x_cat = [sb(f"x_cat{k}", [P, 4, P]) for k in range(2)]
        xT = [sb(f"xT{k}", [P, 4, P], f32r) for k in range(2)]
        h = [sb(f"h{k}", [P, F]) for k in range(2)]
        hT = sb("hT", [P, FC, P])
        y = [sb(f"y{k}", [P, D]) for k in range(2)]
        yw = [sb(f"yw{k}", [P, D]) for k in range(2)]
        token = [sb(f"token{k}", [P, 1], i32) for k in range(2)]
        ps_xT = ctx.enter_context(nc.psum_tensor("ps_xT", [P, 512], f32))
        ps_h = [ctx.enter_context(nc.psum_tensor(f"ps_h{k}", [P, 1024], f32)) for k in range(2)]
        ps_hT = ctx.enter_context(nc.psum_tensor("ps_hT", [P, 1024], f32))
        ps_y = ctx.enter_context(nc.psum_tensor("ps_y", [P, 512], f32))

        weights_in = [sem(f"weights_in{e}") for e in range(NE)]
        w_ready = sem("w_ready")
        b_ready = sem("b_ready")
        x_hi = sem("x_hi")
        x_lo = sem("x_lo")
        started = sem("started")
        made_d = sem("made_d")
        filled = sem("filled")
        x_in = [sem(f"x_in{k}") for k in range(RING)]
        xT_mm = sem("xT_mm")
        xT_ev = sem("xT_ev")
        h_mm = sem("h_mm")
        gelu_done = sem("gelu_done")
        hT_mm = sem("hT_mm")
        hT_ev = sem("hT_ev")
        y_mm = sem("y_mm")
        y_done = sem("y_done")
        added = sem("added")
        block = ctx.enter_context(nc.Block())

        def load_out(e):
            nc.sync.dma_start(w_out[:, e], dram["wout"][e].rearrange("(c p) n -> p c n", p=P)).then_inc(weights_in[e], 16)

        def load_in(e):
            nc.sync.dma_start(w_in[:, e].bitcast(f32), dram["w_up"][e].rearrange("c p f -> p c f")
                              ).then_inc(weights_in[e], 16)

        def fill_rows(eng, experts):
            for e in experts:
                at = eng.value_load(end_of[0:1, e:e + 1], min_val=0, max_val=NE * REGION - P)
                eng.dma_start(rows[bass.ds(at, P), :], filler[:]).then_inc(filled, 16)

        @block.sync
        def _(sp):
            sp.sem_inc(started, 1)
            fill_rows(sp, range(0, NE, 2))
            load_out(0)
            sp.wait_ge(filled, 16 * (NE + 1))

            def ready(e):
                sp.wait_ge(weights_in[e], 16 if e < EARLY_EXPERTS else 32)
                sp.sem_inc(w_ready, 1)

            def load(t, k):
                at = sp.value_load(row_of[0:1, bass.ds(t, 1)], min_val=0, max_val=NOWHERE)
                sp.dma_start(x[k][:], rows[bass.ds(at, P), :]).then_inc(x_in[k], 16)

            for k in range(RING):
                load(k, k)
            load_out(1)
            sp.dma_start(out_b[:], bass.AP(dram["bo"].tensor, 0, [[0, P], [D, NE], [1, D]])).then_inc(b_ready, 16)
            ready(0)
            for t in range(3):
                sp.wait_ge(x_lo, 2 * t + 2)
                load(t + RING, t)
                load_out(t + 2)
            for e in range(5, NE):
                load_out(e)
            for e in range(EARLY_EXPERTS, NE):
                load_in(e)
            for e in range(1, NE):
                ready(e)
            sp.wait_ge(x_lo, 2 * 3 + 2)
            load(3 + RING, 3)
            with sp.Fori(1, TILES // RING - 1) as r:
                for k in range(RING):
                    t = RING * r + k
                    wait_apart(sp, started, x_lo, 2 * t + 2)
                    load(t + RING, k)
            for t in range(TILES // RING * RING, TILES):
                sp.wait_ge(x_lo, 2 * (t - RING) + 2)
                load(t, t % RING)

        @block.gpsimd
        def _(pool):
            def add(t, k):
                wait_apart(pool, started, y_done, 3 * t + 3)
                pool.indirect_dma_start(out, bass.IndirectOffsetOnAxis(ap=token[k][:], axis=0), yw[k][:], None,
                                        bounds_check=T - 1, oob_is_err=False, compute_op=ALU.add).then_inc(added, 16)
                wait_apart(pool, started, added, 16 * t + 16)

            with pool.Fori(0, TILES // 2) as r:
                for k in range(2):
                    add(2 * r + k, k)
            add(TILES - 1, (TILES - 1) % 2)

        @block.scalar
        def _(act):
            fill_rows(act, range(1, NE, 2))
            act.dma_start(rows[NOWHERE:NOWHERE + P, :], filler[:]).then_inc(filled, 16)

            def split(t, k, kx):
                act.wait_ge(x_in[kx], 16 * (t // RING) + 16 if isinstance(t, int) else 4 * (t - kx) + 16)
                wait_count(act, xT_mm, t - 1)
                cat = x_cat[k][:].rearrange("p c s -> p (c s)")
                act.activation(cat[:, 0:D].bitcast(f32r), x[kx][:, 0:D], ACT.Copy).then_inc(x_hi, 1)
                act.activation(cat[:, 2 * D:2 * D + 64].bitcast(f32r), x[kx][:, P:D], ACT.Copy).then_inc(x_hi, 1)

            def x_t(t, k):
                act.wait_ge(xT_mm, t + 1)
                act.activation(xT[k][:], ps_xT[:].rearrange("p (c s) -> p c s", s=P), ACT.Copy).then_inc(xT_ev, 1)

            def gelu(t, k):
                act.wait_ge(h_mm, t + 1)
                act.activation(h[k][:], ps_h[k][:, 0:F], ACT.Gelu).then_inc(gelu_done, 1)

            act.wait_ge(made_d, 4)
            split(0, 0, 0)
            split(1, 1, 1)
            x_t(0, 0)
            x_t(1, 1)
            split(2, 0, 2)
            gelu(0, 0)

            def turn(t, k, kx):
                gelu(t, k)
                x_t(t + 1, 1 - k)
                split(t + 2, k, kx)

            with act.Fori(0, (TILES - 3) // 4) as r:
                for k in range(4):
                    turn(4 * r + 1 + k, (k + 1) % 2, (k + 3) % 4)
            for t in range((TILES - 3) // 4 * 4 + 1, TILES - 2):
                turn(t, t % 2, (t + 2) % 4)
            gelu(TILES - 2, (TILES - 2) % 2)
            x_t(TILES - 1, (TILES - 1) % 2)
            gelu(TILES - 1, (TILES - 1) % 2)

        @block.vector
        def _(dve):
            for k in range(2):
                dve.memset(x_cat[k][:, 3, 64:P], 0.0).then_inc(made_d, 1)
                dve.wait_ge(made_d, 2 * k + 1)
                dve.memset(x_cat[k][:, 3, 64:P:32], 1.0).then_inc(made_d, 1)

            def low(t, k, kx):
                dve.wait_ge(x_hi, 2 * t + 2)
                cat = x_cat[k][:].rearrange("p c s -> p (c s)")
                dve.tensor_tensor(cat[:, D:2 * D], x[kx][:, 0:D], cat[:, 0:D], ALU.subtract).then_inc(x_lo, 1)
                if not isinstance(t, int) or t >= RING:
                    dve.wait_ge(y_done, 3 * t + 3 - 3 * RING)
                dve.tensor_copy(tail[kx][:], x[kx][:, D:ROW]).then_inc(x_lo, 1)

            def h_t(t):
                for half in range(2):
                    dve.wait_ge(hT_mm, 2 * t + half + 1)
                    c0, c1 = ((0, 4), (4, 6))[half]
                    dve.tensor_copy(hT[:, c0:c1, :], ps_hT[:, c0 * P:c1 * P].rearrange("p (c s) -> p c s", s=P)).then_inc(hT_ev, 1)

            def add_bias(t, k):
                e = dve.value_load(expert_of[0:1, bass.ds(t, 1)], min_val=0, max_val=NE - 1)
                dve.wait_ge(y_mm, t + 1)
                dve.tensor_tensor(y[k][:], ps_y[:, k * 256:k * 256 + D],
                                  out_b[:, bass.ds(e, 1), :].rearrange("p o n -> p (o n)"), ALU.add).then_inc(y_done, 1)

            def weigh(t, k, kx):
                dve.wait_ge(y_done, 3 * t + 1)
                if not isinstance(t, int) or t >= 2:
                    dve.wait_ge(added, 16 * t - 16)
                dve.tensor_scalar(yw[k][:], y[k][:], tail[kx][:, 0:1], None, ALU.mult).then_inc(y_done, 1)
                dve.tensor_copy(token[k][:], tail[kx][:, 1:2]).then_inc(y_done, 1)

            def turn(t, k):
                low(t + 2, k % 2, (k + 2) % 4)
                add_bias(t - 1, (k - 1) % 2)
                h_t(t)
                weigh(t - 1, (k - 1) % 2, (k - 1) % 4)

            low(0, 0, 0)
            low(1, 1, 1)
            dve.wait_ge(b_ready, 16)
            low(2, 0, 2)
            h_t(0)
            for t in range(1, 4):
                turn(t, t % 4)
            with dve.Fori(1, (TILES - 2) // 4) as r:
                for k in range(4):
                    turn(4 * r + k, k)
            for t in range((TILES - 2) // 4 * 4, TILES - 2):
                turn(t, t % 4)
            for t in range(TILES - 2, TILES):
                add_bias(t - 1, (t - 1) % 2)
                h_t(t)
                weigh(t - 1, (t - 1) % 2, (t - 1) % 4)
            add_bias(TILES - 1, (TILES - 1) % 2)
            weigh(TILES - 1, (TILES - 1) % 2, (TILES - 1) % 4)

        @block.tensor
        def _(pe):
            def turn_x(t, k):
                pe.wait_ge(x_lo, 2 * t + 1)
                wait_count(pe, xT_ev, t)
                for c in range(4):
                    mm = pe.transpose(ps_xT[:, c * P:(c + 1) * P], x_cat[k][:, c, :], ident[:])
                mm.then_inc(xT_mm, 1)

            def expert(t):
                return pe.value_load(expert_of[0:1, bass.ds(t, 1)], min_val=0, max_val=NE - 1)

            def up(t, k, e):
                pe.wait_ge(w_ready, e + 1)
                pe.wait_ge(xT_ev, t + 1)
                for c0, c1 in ((0, 512), (512, F)):
                    for i, (cx, cw) in enumerate(TERMS):
                        mm = pe.matmul(ps_h[k][:, c0:c1], xT[k][:, cx, :],
                                       w_in[:, bass.ds(e, 1), cw, c0:c1].rearrange("p o f -> p (o f)"),
                                       start=i == 0, stop=i == KC - 1)
                mm.then_inc(h_mm, 1)

            def turn_h(t, k):
                for half, (c0, c1) in enumerate(((0, 4), (4, 6))):
                    if half == 0:
                        pe.wait_ge(gelu_done, t + 1)
                    for c in range(c0, c1):
                        mm = pe.transpose(ps_hT[:, c * P:(c + 1) * P], h[k][:, c * P:(c + 1) * P], ident[:])
                    mm.then_inc(hT_mm, 1)

            def down(t, k, e):
                for c in range(FC):
                    if c in (0, 4):
                        pe.wait_ge(hT_ev, 2 * t + (1 if c == 0 else 2))
                    mm = pe.matmul(ps_y[:, k * 256:k * 256 + D], hT[:, c, :],
                                   w_out[:, bass.ds(e, 1), c, :].rearrange("p o n -> p (o n)"),
                                   start=c == 0, stop=c == FC - 1)
                mm.then_inc(y_mm, 1)

            turn_x(0, 0)
            turn_x(1, 1)
            up(0, 0, expert(0))

            def turn(t, k):
                turn_h(t - 1, k)
                up(t, (k + 1) % 2, expert(t))
                e = expert(t - 1)
                turn_x(t + 1, k)
                down(t - 1, k, e)

            for t in (1, 2, 3, 4):
                turn(t, (t - 1) % 2)
            with pe.Fori(0, (TILES - 3 - 4) // 4) as r:
                for k in range(4):
                    turn(4 * r + 5 + k, k % 2)
            for t in range(5 + (TILES - 3 - 4) // 4 * 4, TILES - 1):
                turn(t, (t - 1) % 2)
            turn_h(TILES - 2, (TILES - 2) % 2)
            up(TILES - 1, (TILES - 1) % 2, expert(TILES - 1))
            down(TILES - 2, (TILES - 2) % 2, expert(TILES - 2))
            turn_h(TILES - 1, (TILES - 1) % 2)
            down(TILES - 1, (TILES - 1) % 2, expert(TILES - 1))


def tower(nc, dram):
    with ExitStack() as ctx:
        def sb(name, shape, dt=f32):
            return ctx.enter_context(nc.sbuf_tensor(name, shape, dt))

        shared = [sb("route", [P, NE]), sb("ident", [P, P]), sb("tile_row", [P, TILES]), sb("step", [P, STEPS]),
                  sb("filler", [P, ROW]), sb("row_of", [P, TILES], i32), sb("expert_of", [P, TILES], i32),
                  sb("end_of", [P, NE], i32)]
        with ExitStack() as first_user:
            qkv_split = first_user.enter_context(nc.sbuf_tensor("qkv_split", [P, 3, KC, A], f32r))
            room = first_user.enter_context(nc.sbuf_tensor("room", [P, ROOM], f32))
        shared += [sb("w_in_all", [P, NE, KC, F], f32r), qkv_split, room]
        attention_block(nc, dram, shared)
        expert_block(nc, dram, shared)


def kernel(x, mask_BS_i1_0, fside_BSS_graph, L0_tok_tok_emb, L0_tok_seg_emb, L0_tok_pos_emb, L0_tok_dense_w,
           L0_tok_dense_b, L0_tok_ln_gamma, L0_tok_ln_beta, L0_attn_Wq, L0_attn_bq, L0_attn_Wk, L0_attn_bk,
           L0_attn_Wv, L0_attn_bv, L0_attn_Wo, L0_attn_bo, L0_ffn_Wr, L0_ffn_Wi, L0_ffn_bi, L0_ffn_Wo, L0_ffn_bo):
    import numpy as np
    import concourse.bacc as bacc
    from concourse import mybir as mb
    from concourse.bass_utils import run_bass_kernel_spmd

    def turned(a, *axes):
        return np.ascontiguousarray(np.transpose(np.asarray(a), axes))

    def as_is(a):
        return np.ascontiguousarray(np.asarray(a))

    arrays = {
        "ids": turned(x, 1, 0), "mask": turned(mask_BS_i1_0, 1, 0), "graphT": turned(fside_BSS_graph, 0, 2, 1),
        "tok_emb": as_is(L0_tok_tok_emb), "seg_emb": as_is(L0_tok_seg_emb), "pos_emb": as_is(L0_tok_pos_emb),
        "dense_w": as_is(L0_tok_dense_w), "dense_b": as_is(L0_tok_dense_b), "ln_gamma": as_is(L0_tok_ln_gamma),
        "ln_beta": as_is(L0_tok_ln_beta), "wq": as_is(L0_attn_Wq), "bq": as_is(L0_attn_bq), "wk": as_is(L0_attn_Wk),
        "bk": as_is(L0_attn_bk), "wv": as_is(L0_attn_Wv), "bv": as_is(L0_attn_bv), "wo": as_is(L0_attn_Wo),
        "attn_bo": as_is(L0_attn_bo), "router": turned(L0_ffn_Wr, 1, 0), "wi": turned(L0_ffn_Wi, 0, 2, 1),
        "bi": as_is(L0_ffn_bi), "wout": turned(L0_ffn_Wo, 0, 2, 1), "bo": as_is(L0_ffn_bo),
    }
    nc = bacc.Bacc("TRN2", target_bir_lowering=False, num_devices=1)
    dram = {n: nc.dram_tensor(f"in_{n}", a.shape, mb.dt.from_np(a.dtype), kind="ExternalInput").ap()
            for n, a in arrays.items()}
    dram["out"] = nc.dram_tensor("out_rows", (T, D), f32, kind="ExternalOutput").ap()
    dram["shear"] = nc.dram_tensor("shear", (P * PITCH + HALF,), f32, kind="Internal").ap()
    dram["w_up"] = nc.dram_tensor("w_up", (NE, KC, P, F), f32, kind="Internal").ap()
    dram["rows"] = nc.dram_tensor("rows", (NOWHERE + P, ROW), f32, kind="Internal").ap()
    tower(nc, dram)
    r = run_bass_kernel_spmd(nc, [{f"in_{n}": a for n, a in arrays.items()}], core_ids=[0])
    return r.results[0]["out_rows"].reshape(B, S, D)
```
